# Optimizing a Trainium2 kernel written in Bass

```python
import numpy as np
import jax
import jax.numpy as jnp

def _softmax(x, axis=-1):
    return jax.nn.softmax(x, axis=axis)

def _gelu(x):
    return jax.nn.gelu(x, approximate=True)

def _silu(x):
    return jax.nn.silu(x)

def _sigmoid(x):
    return jax.nn.sigmoid(x)

def _layernorm(x, axis=-1, eps=1e-05):
    m = jnp.mean(x, axis=axis, keepdims=True)
    v = jnp.var(x, axis=axis, keepdims=True)
    return (x - m) / jnp.sqrt(v + eps)

def _scatter_add(tgt, idx, src, axis=0):
    return tgt.at[idx].add(src)

def _segment_sum(src, seg, n):
    return jax.ops.segment_sum(src, seg, n)
kernel_name = 'mk_seq_postln_d1_jaxref_r8_54e6e2'

def setup_inputs(seed: int=0):
    np.random.seed(seed)
    _w = jnp.asarray

    def _L0_attn_setup():
        import jax, jax.numpy as jnp
        import numpy as np
        DT_MIN, DT_MAX = (0.001, 0.1)
        CHUNK = 64
        key = jax.random.key(seed)
        ks = jax.random.split(key, 8)
        b, L, D = (2, 512, 128)
        d_inner, d_state, nheads, K = (256, 128, 32, 4)
        conv_dim = d_inner + 2 * d_state
        d_in_proj = 2 * d_inner + 2 * d_state + nheads
        f32 = jnp.float32
        return {'x': jax.random.normal(ks[0], (b, L, D), f32), 'in_proj_w': jax.random.normal(ks[1], (d_in_proj, D), f32) * D ** (-0.5), 'conv_w': jax.random.normal(ks[2], (conv_dim, K), f32) * 0.3, 'conv_b': jnp.zeros((conv_dim,), f32), 'dt_bias': jax.random.normal(ks[3], (nheads,), f32) * 0.5, 'A_log': jnp.log(jax.random.uniform(ks[4], (nheads,), f32, 1.0, 16.0)), 'D_skip': jnp.ones((nheads,), f32), 'norm_w': jnp.ones((d_inner,), f32), 'out_proj_w': jax.random.normal(ks[5], (D, d_inner), f32) * d_inner ** (-0.5), 'ln_w': jnp.ones((D,), f32), 'ln_b': jnp.zeros((D,), f32)}
    _L0_attn_in = _L0_attn_setup()

    def _L0_ffn_setup():
        import jax, jax.numpy as jnp
        import numpy as np
        B, S, H, I, E, K = (4, 256, 128, 344, 4, 2)
        key = jax.random.key(seed)
        ks = jax.random.split(key, 8)
        inv_h = 1.0 / np.sqrt(H)
        inv_i = 1.0 / np.sqrt(I)
        return {'x': jax.random.normal(ks[0], (B, S, H), jnp.float32), 'gate_w': jax.random.normal(ks[1], (E, H), jnp.float32) * inv_h, 'eg': jax.random.normal(ks[2], (E, I, H), jnp.float32) * inv_h, 'eu': jax.random.normal(ks[3], (E, I, H), jnp.float32) * inv_h, 'ed': jax.random.normal(ks[4], (E, H, I), jnp.float32) * inv_i, 'sg': jax.random.normal(ks[5], (I, H), jnp.float32) * inv_h, 'su': jax.random.normal(ks[6], (I, H), jnp.float32) * inv_h, 'sd': jax.random.normal(ks[7], (H, I), jnp.float32) * inv_i}
    _L0_ffn_in = _L0_ffn_setup()
    _d = {'L0_attn_x': _L0_attn_in['x'], 'L0_attn_in_proj_w': _L0_attn_in['in_proj_w'], 'L0_attn_conv_w': _L0_attn_in['conv_w'], 'L0_attn_conv_b': _L0_attn_in['conv_b'], 'L0_attn_dt_bias': _L0_attn_in['dt_bias'], 'L0_attn_A_log': _L0_attn_in['A_log'], 'L0_attn_D_skip': _L0_attn_in['D_skip'], 'L0_attn_norm_w': _L0_attn_in['norm_w'], 'L0_attn_out_proj_w': _L0_attn_in['out_proj_w'], 'L0_attn_ln_w': _L0_attn_in['ln_w'], 'L0_attn_ln_b': _L0_attn_in['ln_b'], 'L0_ffn_gate_w': _L0_ffn_in['gate_w'], 'L0_ffn_eg': _L0_ffn_in['eg'], 'L0_ffn_eu': _L0_ffn_in['eu'], 'L0_ffn_ed': _L0_ffn_in['ed'], 'L0_ffn_sg': _L0_ffn_in['sg'], 'L0_ffn_su': _L0_ffn_in['su'], 'L0_ffn_sd': _L0_ffn_in['sd']}
    _x0 = _d['L0_attn_x']
    _d['L0_attn_x'] = jax.random.normal(jax.random.fold_in(jax.random.key(seed), 1), (8, 256, 128), dtype=_x0.dtype)
    del _x0
    return _d

def reference(L0_attn_x, L0_attn_in_proj_w, L0_attn_conv_w, L0_attn_conv_b, L0_attn_dt_bias, L0_attn_A_log, L0_attn_D_skip, L0_attn_norm_w, L0_attn_out_proj_w, L0_attn_ln_w, L0_attn_ln_b, L0_ffn_gate_w, L0_ffn_eg, L0_ffn_eu, L0_ffn_ed, L0_ffn_sg, L0_ffn_su, L0_ffn_sd):

    def _L0_attn_ref(x, in_proj_w, conv_w, conv_b, dt_bias, A_log, D_skip, norm_w, out_proj_w, ln_w, ln_b):
        import jax, jax.numpy as jnp
        import numpy as np
        DT_MIN, DT_MAX = (0.001, 0.1)
        CHUNK = 64
        b, L, d_model = x.shape
        d_inner = norm_w.shape[0]
        nheads = A_log.shape[0]
        hd = d_inner // nheads
        conv_dim = conv_w.shape[0]
        d_state = (conv_dim - d_inner) // 2
        Q = CHUNK
        c = L // Q
        zxbcdt = jnp.einsum('bld,kd->blk', x, in_proj_w)
        z = zxbcdt[..., :d_inner]
        xBC = zxbcdt[..., d_inner:d_inner + conv_dim]
        dt_raw = zxbcdt[..., d_inner + conv_dim:]
        K = conv_w.shape[1]
        xp = jnp.pad(xBC, ((0, 0), (K - 1, 0), (0, 0)))
        conv = sum((xp[:, k:k + L, :] * conv_w[:, k] for k in range(K))) + conv_b
        xBC = jax.nn.silu(conv)
        x_ssm = xBC[..., :d_inner]
        Bm = xBC[..., d_inner:d_inner + d_state]
        Cm = xBC[..., d_inner + d_state:]
        dt = DT_MIN + (DT_MAX - DT_MIN) * jax.nn.sigmoid(dt_raw + dt_bias)
        A = -jnp.exp(A_log)
        xh = x_ssm.reshape(b, c, Q, nheads, hd)
        dtc = dt.reshape(b, c, Q, nheads)
        x_dt = xh * dtc[..., None]
        dA = jnp.einsum('bcqh,h->bhcq', dtc, A)
        Acum = jnp.cumsum(dA, axis=-1)
        Bc = Bm.reshape(b, c, Q, d_state)
        Cc = Cm.reshape(b, c, Q, d_state)
        seg = Acum[..., :, None] - Acum[..., None, :]
        mask = jnp.tril(jnp.ones((Q, Q), bool))
        Lmat = jnp.exp(jnp.where(mask, seg, -jnp.inf))
        Yd = jnp.einsum('bcqn,bcsn,bhcqs,bcshp->bcqhp', Cc, Bc, Lmat, x_dt)
        decay_states = jnp.exp(Acum[..., -1:] - Acum)
        states = jnp.einsum('bcqn,bhcq,bcqhp->bchpn', Bc, decay_states, x_dt)
        chunk_decay = jnp.exp(Acum[..., -1])

        def step(carry, inp):
            st, dec = inp
            return (dec[..., None, None] * carry + st, carry)
        _, prevs = jax.lax.scan(step, jnp.zeros((b, nheads, hd, d_state), x.dtype), (jnp.moveaxis(states, 1, 0), jnp.moveaxis(chunk_decay, 2, 0)))
        prevs = jnp.moveaxis(prevs, 0, 1)
        Yo = jnp.einsum('bcqn,bchpn,bhcq->bcqhp', Cc, prevs, jnp.exp(Acum))
        Y = (Yd + Yo).reshape(b, L, nheads, hd) + D_skip[None, None, :, None] * xh.reshape(b, L, nheads, hd)
        y = Y.reshape(b, L, d_inner)
        y = y * jax.nn.silu(z)
        y = y * jax.lax.rsqrt(jnp.mean(y * y, axis=-1, keepdims=True) + 1e-05) * norm_w
        out = jnp.einsum('bli,di->bld', y, out_proj_w)
        mu = jnp.mean(out, axis=-1, keepdims=True)
        var = jnp.mean((out - mu) ** 2, axis=-1, keepdims=True)
        ln = (out - mu) * jax.lax.rsqrt(var + 1e-05) * ln_w + ln_b
        return x + ln

    def _L0_ffn_ref(x, gate_w, eg, eu, ed, sg, su, sd):
        import jax, jax.numpy as jnp
        import numpy as np
        B, S, H, I, E, K = (4, 256, 128, 344, 4, 2)
        xf = x.reshape(-1, x.shape[-1])
        scores = jax.nn.softmax(xf @ gate_w.T, axis=-1)
        topk_w, topk_idx = jax.lax.top_k(scores, K)
        topk_w = topk_w / (topk_w.sum(axis=-1, keepdims=True) + 1e-20)
        comb = jnp.sum(jax.nn.one_hot(topk_idx, E, dtype=x.dtype) * topk_w[..., None], axis=1)
        g = jax.nn.silu(jnp.einsum('nh,eih->eni', xf, eg))
        u = jnp.einsum('nh,eih->eni', xf, eu)
        y_exp = jnp.einsum('eni,ehi->enh', g * u, ed)
        y = jnp.einsum('enh,ne->nh', y_exp, comb)
        y = y + jax.nn.silu(xf @ sg.T) * (xf @ su.T) @ sd.T
        return y.reshape(x.shape)
    x = L0_attn_x
    x = _layernorm(x + _L0_attn_ref(x, L0_attn_in_proj_w, L0_attn_conv_w, L0_attn_conv_b, L0_attn_dt_bias, L0_attn_A_log, L0_attn_D_skip, L0_attn_norm_w, L0_attn_out_proj_w, L0_attn_ln_w, L0_attn_ln_b), axis=-1)
    x = _layernorm(x + _L0_ffn_ref(x, L0_ffn_gate_w, L0_ffn_eg, L0_ffn_eu, L0_ffn_ed, L0_ffn_sg, L0_ffn_su, L0_ffn_sd), axis=-1)
    return x

_drawn_inputs = setup_inputs


def setup_inputs(seed=0):
    import zlib

    import numpy as np

    out = dict(_drawn_inputs(seed))
    spreads = {'L0_attn_conv_b': (0.0, 0.1),
     'L0_attn_D_skip': (1.0, 0.2),
     'L0_attn_norm_w': (1.0, 0.2),
     'L0_attn_ln_w': (1.0, 0.2),
     'L0_attn_ln_b': (0.0, 0.1)}
    factors = {}
    for name, (base, spread) in spreads.items():
        noise = np.random.default_rng([zlib.crc32(name.encode()), seed]).standard_normal(out[name].shape)
        drawn = base * np.exp(spread * noise) if base else spread * noise
        out[name] = jnp.asarray(drawn.astype(out[name].dtype))
    for name, factor in factors.items():
        out[name] = (out[name] * factor).astype(out[name].dtype)
    return out
```

```python
from contextlib import ExitStack

import numpy as np

import concourse.bass as bass
from concourse import mybir

F32 = mybir.dt.float32
F32R = mybir.dt.float32r
ALU = mybir.AluOpType
ACT = mybir.ActivationFunctionType

P = 128
NB, L, D = 8, 256, 128
NT = L // P
Q = 64
NC = L // Q
NH, HD = 32, 8
DI = NH * HD
NP = NH // 2
K = 4
DT_MIN, DT_MAX = 0.001, 0.1
EPS = 1e-5
E, I = 4, 344
NE = E + 1
HC = [(0, 128), (128, 128), (256, 88)]
BT = 512
NBLK = NB * L // BT
NR = 64 + 4 * NC
PADW = 96 * NH // 4


class Batch:

    def __init__(self, k, par, half):
        self.k, self.par, self.half = k, par, half
        self.first = isinstance(k, int) and k == 0
        self.early = isinstance(k, int) and k < 2


def mamba_moe(nc, a, out):
    with ExitStack() as ctx:
        def sb(name, shape, dt=F32):
            return ctx.enter_context(nc.sbuf_tensor(name, shape, dt))

        def sem(name):
            return ctx.enter_context(nc.semaphore(name))

        def view(t, part, nparts, off, dims):
            row = 1
            for n in t.shape[1:]:
                row *= n
            return bass.AP(t, part * row + off, [[row, nparts], *dims])

        sums_d = [nc.dram_tensor(f"sums_d{p}", [64, NC, Q], F32, kind="Internal").ap() for p in range(2)]

        bank = [ctx.enter_context(nc.psum_tensor(f"bank{i}", [P, 512], F32)) for i in range(8)]
        ps_seg = bank[0:2]
        ps_y = bank[2]
        ps_yo = bank[3]
        ps_gl = bank[4]
        ps_so = bank[5]
        ps_a, ps_b = bank[6], bank[7]

        ident = sb("ident", [P, P])
        tril = sb("tril", [P, Q])
        negpar = sb("negpar", [64, 2])
        reset = sb("reset", [64, L])
        selE = sb("selE", [64, DI], F32R)
        ones4_f = sb("ones4_f", [NR, NC, P])
        hilo = sb("hilo", [2, 2])
        ones = sb("ones", [P, 2])
        ones32 = sb("ones32", [32, P])
        cw_b = sb("cw_b", [P, K, 512])
        w_cv = sb("w_cv", [P, 320])
        w_hi = sb("w_hi", [P, 320], F32R)
        w_lo = sb("w_lo", [P, 320], F32R)
        cv_hi = sb("cv_hi", [P, K, 512], F32R)
        cv_lo = sb("cv_lo", [P, K, 512], F32R)
        cb_r = sb("cb_r", [2, 512], F32R)
        ones_r = sb("ones_r", [2, L], F32R)
        dtb = sb("dtb", [64, 1])
        dtb_h = sb("dtb_h", [64, 1])
        alog = sb("alog", [64, 1])
        aexp = sb("aexp", [64, 1])
        aneg = sb("aneg", [64, 1])
        dskip = sb("dskip", [P, 2])
        nw = sb("nw", [P, 2])
        wo = sb("wo", [P, 2, D])
        lnw = sb("lnw", [P, D])
        lnb = sb("lnb", [P, D])
        gw = sb("gw", [D, E])
        g_hi = sb("g_hi", [D, NE * I], F32R)
        g_lo = sb("g_lo", [D, NE * I], F32R)
        u_hi = sb("u_hi", [D, NE * I], F32R)
        u_lo = sb("u_lo", [D, NE * I], F32R)
        wd = sb("wd", [P, NE, len(HC), D])

        xTf = sb("xTf", [D, 2, L])
        xtok = sb("xtok", [P, 2, NT, D])
        xTh = [sb(f"xTh{p}", [D, K - 1 + L], F32R) for p in range(2)]
        xTl = [sb(f"xTl{p}", [D, K - 1 + L], F32R) for p in range(2)]
        th = sb("th", [P, 3, 512])
        tdt = sb("tdt", [64, L])
        dd = sb("dd", [64, L])
        dA = sb("dA", [64, L])
        acum = sb("acum", [64, L])
        a_hl = sb("a_hl", [64, L], F32R)
        adif = sb("adif", [64, L])
        eT = sb("eT", [64, L])
        e_hl = sb("e_hl", [64, L], F32R)
        ddiag = sb("ddiag", [32, 2, NH])
        neg = [sb(f"neg{p}", [NR, NC, 2, Q], F32R) for p in range(2)]
        mov = [sb(f"mov{p}", [NR, NP * Q], F32R) for p in range(2)]
        xs = [sb(f"xs{p}", [P, 2, L]) for p in range(2)]
        bc = [sb(f"bc{p}", [P, 2, L]) for p in range(2)]
        sz = [sb(f"sz{p}", [P, 2, L]) for p in range(2)]
        dd2 = sb("dd2", [64, NC, 2, Q])
        b2 = sb("b2", [P, NC, 2, Q])
        xs2 = sb("xs2", [P, 2, NC, 2, Q])
        ddt = sb("ddt", [P, NC * 64 + 64])
        btok = sb("btok", [Q, 3, P])
        eb = [sb(f"eb{p}", [P, 2, L]) for p in range(2)]
        xpad = sb("xpad", [P, NC, PADW])
        xdd = sb("xdd", [Q, 3, DI])
        gm = sb("gm", [P, NC, Q])
        ee = sb("ee", [P, 2, 512])
        mm = sb("mm", [P, 2, 512])
        sel_f, selE_f = ee[0:64, :, :].rearrange("p a n -> p (a n)"), mm[0:64, 0, 0:DI]
        st = sb("st", [P, 3, DI])
        stm = sb("stm", [P, DI])
        yo = sb("yo", [P, 2, L])
        yv = sb("yv", [P, 2, L])
        yf = sb("yf", [P, 2, L])
        ysq = sb("ysq", [P, 2, L])
        cb_f, cb_h, cb_s = (t[0:2, :, :].rearrange("r m l -> r (m l)") for t in (yo, yv, ysq))
        xx = sb("xx", [P, 2, NT, D])
        bn = sb("bn", [P, NT, 6])
        mv = sb("mv", [P, NT, 2])
        m1 = sb("m1", [P, NT])
        w1 = sb("w1", [P, NT])
        s1 = sb("s1", [P, NT])
        an = sb("an", [P, NT, D])
        rr = sb("rr", [P, NT, D])
        bn2 = sb("bn2", [P, NT, 6])
        mv2 = sb("mv2", [P, NT, 2])
        s2 = sb("s2", [P, NT])
        pause = sb("pause", [P, 1])
        w2 = sb("w2", [P, NT])
        mhalf = sb("mhalf", [P, 4])
        x1c = sb("x1c", [P, 2, NT, D])
        x1Tf = sb("x1Tf", [D, L])
        x1 = sb("x1", [P, NB * NT, D])
        x1_flat = x1[:, :, :].rearrange("p t d -> p (t d)")
        w_raw, gu_f = x1_flat[:, 0:832], x1_flat[:, 0:NE * I]
        wo_f = x1_flat[:, NE * I:NE * I + 2 * D].rearrange("p (g d) -> p g d", g=2)
        x1h = sb("x1h", [D, NB * L], F32R)
        x1l = sb("x1l", [D, NB * L], F32R)
        lg = sb("lg", [P, NB * NT, E])

        s_w = sem("weights_loaded")
        s_w2 = sem("ffn_weights_loaded")
        s_gu = sem("gate_loaded")
        s_up = sem("up_loaded")
        s_xin = [sem(f"x_loaded{p}") for p in range(2)]
        s_su = sem("setup_vector")
        s_sua = sem("setup_scalar")
        s_sup = sem("setup_pool")
        s_ps = sem("pool_setup_step")
        s_xh = sem("x_high")
        s_xl = sem("x_low")
        s_dtp = sem("dt_in_psum")
        s_xp = sem("xbc_z_in_psum")
        s_td = sem("dt_tanh")
        s_th = sem("silu_tanh")
        s_dt = sem("dt_chain")
        s_sl = sem("silu_done")
        s_ah = sem("sums_high")
        s_al = sem("sums_low")
        s_ng = sem("neg_sums")
        s_df = sem("decay_exponent")
        s_et = sem("exp_sums")
        s_dc = sem("exp_decay")
        s_eh = sem("exp_high")
        s_el = sem("exp_low")
        s_dd = sem("dt_decayed")
        s_dg = sem("decay_diagonal")
        s_fl = [sem(f"sums_flat{p}") for p in range(2)]
        s_d2 = sem("dt_doubled")
        s_b2 = sem("b_doubled")
        s_x2 = sem("x_doubled")
        s_fw = sem("sums_in_dram")
        s_ddp = sem("dt_tokens_psum")
        s_btp = sem("b_tokens_psum")
        s_ebp = sem("exp_rows_psum")
        s_xtp = sem("x_tokens_psum")
        s_ddt = sem("dt_tokens")
        s_bt = sem("b_tokens")
        s_eb = sem("exp_rows")
        s_pad = sem("x_padded")
        s_xd = sem("x_decayed")
        s_g = sem("g_in_psum")
        s_gm = sem("g_masked")
        s_sg = sem("seg_in_psum")
        s_e = sem("decays")
        s_m = sem("m_ready")
        s_yd = sem("yd_done")
        s_st = sem("state_in_psum")
        s_s = sem("state_ready")
        s_sm = sem("state_decayed")
        s_yo = sem("yo_in_psum")
        s_y = sem("y_steps")
        s_sq = sem("y_squared")
        s_op = sem("proj_in_psum")
        s_x2x = sem("x_doubled_sum")
        s_xx = sem("residual_ready")
        s_ln = sem("norm_steps")
        s_pw = sem("rsqrt_done")
        s_x1 = sem("x1_ready")
        s_kp = sem("x1_kept")
        s_x1p = sem("x1t_in_psum")
        s_x1f = sem("x1t_copied")
        s_x1l = sem("x1t_low")
        s_lp = sem("logits_in_psum")
        s_lg = sem("logits_kept")
        s_gp = sem("gate_in_psum")
        s_uo = sem("up_in_psum")
        s_si = sem("gate_silu")
        s_h = sem("hidden_ready")
        s_dn = sem("hidden_used")
        s_ye = sem("expert_in_psum")
        s_cb = sem("comb_steps")
        s_ac = sem("acc_steps")
        s_f2 = sem("final_stats")
        s_fp = sem("final_rsqrt")
        s_fo = sem("final_ready")
        s_out = sem("stored")
        sg, hh = cw_b, th
        fbn = sb("fbn", [P, 4, 6])
        fmv = sb("fmv", [P, 4, 2])
        fs = sb("fs", [P, 4])
        fw = sb("fw", [P, 4])
        acc, fo = yv[:, :, :].rearrange("p a (t d) -> p (a t) d", d=D), yf[:, :, :].rearrange("p a (t d) -> p (a t) d", d=D)
        NTT = NB * NT
        cmx = sb("cmx", [P, NTT])
        cex = sb("cex", [P, NTT, E])
        csm = sb("csm", [P, NTT])
        crc = sb("crc", [P, NTT])
        cpr = sb("cpr", [P, NTT, E])
        cge = sb("cge", [P, 6, NTT])
        crk = sb("crk", [P, NTT, E])
        csl = sb("csl", [P, NTT, E])
        cts = sb("cts", [P, NTT])
        comb = sb("comb", [P, NTT, E])

        block = ctx.enter_context(nc.Block())

        N_W = 19
        N_PS = 13

        @block.sync
        def _(sp):
            def load_x(b):
                at, once = (x if isinstance(x, int) else sp.snap(x) for x in (b.k * (D * L), b.k - 1))
                if not b.early:
                    sp.wait_ge(s_xh, once)
                    sp.wait_ge(s_xl, once)
                    sp.wait_ge(s_x2x, once)
                sp.dma_start(xTf[:, b.par, :], bass.AP(a["xT"].tensor, at, [[L, D], [1, L]])).then_inc(s_xin[b.par], 16)
                sp.dma_start(xtok[:, b.par, :, :], bass.AP(a["x"].tensor, at, [[D, P], [P * D, NT], [1, D]])).then_inc(s_xin[b.par], 16)

            def flatten(b):
                made, sent = (x if isinstance(x, int) else sp.snap(x) for x in (b.k + 1, 16 * (b.k + 1)))
                sp.wait_ge(s_ah, made)
                sp.wait_ge(s_al, made)
                if not b.early:
                    sp.wait_ge(s_g, b.k)
                if b.early and not b.first:
                    sp.wait_ge(s_ps, N_PS)
                if b.first:
                    sp.wait_ge(s_ps, N_PS)
                sp.dma_start(sums_d[b.par].rearrange("h c q -> h (c q)"), a_hl[:, :].bitcast(F32)).then_inc(s_fw, 16)
                sp.wait_ge(s_fw, sent)
                for part in range(2):
                    for h2 in range(2):
                        row = 64 + NC * (2 * part + h2)
                        dst = mov[b.par][row:row + NC, :].bitcast(F32).rearrange("c (h q) -> c h q", q=Q)
                        src = sums_d[b.par][32 * part:32 * part + 32].rearrange("(h g) c q -> g c h q", g=2)[h2]
                        sp.dma_start(dst, src).then_inc(s_fl[b.par], 16)

            sp.dma_start(w_raw[:, 0:800], a["in_wT"]).then_inc(s_w, 16)
            sp.dma_start(w_raw[:, 800:832], a["in_wT"][:, 768:800]).then_inc(s_w, 16)
            load_x(Batch(0, 0, 0))
            sp.dma_start(cw_b[:, :, :], a["cwT"].rearrange("(o k) c -> o k c", o=1).broadcast_to([P, K, 512])).then_inc(s_w, 16)
            for r in range(2):
                sp.dma_start(yo[r:r + 1, :, :].rearrange("r m l -> r (m l)"), a["cb"]).then_inc(s_w, 16)
                sp.dma_start(dtb[32 * r:32 * r + 32, :], a["dtb"]).then_inc(s_w, 16)
                sp.dma_start(alog[32 * r:32 * r + 32, :], a["alog"]).then_inc(s_w, 16)
            for dst, name in ((ident, "c_ident"), (tril, "c_tril"), (negpar, "c_negpar"), (reset, "c_reset"),
                              (selE_f, "c_selE"), (sel_f, "c_sel"), (hilo, "c_hilo"), (nw, "nw"), (dskip, "dskip")):
                sp.dma_start(dst[:, :], a[name]).then_inc(s_w, 16)
            sp.dma_start(ones4_f[64:NR, :, :], a["c_ones4"]).then_inc(s_w, 16)
            load_x(Batch(1, 1, 0))
            sp.dma_start(wo_f[:, :, :], a["woT"].rearrange("(g p) d -> p g d", p=P)).then_inc(s_w2, 16)
            sp.dma_start(lnw[:, :], a["lnw"].broadcast_to([P, D])).then_inc(s_w2, 16)
            sp.dma_start(lnb[:, :], a["lnb"].broadcast_to([P, D])).then_inc(s_w2, 16)
            sp.dma_start(gw[:, :], a["gwT"]).then_inc(s_w2, 16)
            flatten(Batch(0, 0, 0))
            sp.wait_ge(s_su, 4)
            sp.dma_start(gu_f[:, 0:E * I], a["egT"]).then_inc(s_gu, 16)
            sp.dma_start(gu_f[:, E * I:], a["sgT"]).then_inc(s_gu, 16)
            for c, (h0, hn) in enumerate(HC):
                sp.dma_start(wd[0:hn, 0:E, c, :], a["edT"][:, h0:h0 + hn, :].rearrange("e i d -> i e d")).then_inc(s_w2, 16)
                sp.dma_start(wd[0:hn, E, c, :], a["sdT"][h0:h0 + hn, :]).then_inc(s_out if c == len(HC) - 1 else s_w2, 16)
            sp.wait_ge(s_sua, 4)
            sp.wait_ge(s_sup, 1)
            sp.dma_start(gu_f[:, 0:E * I], a["euT"]).then_inc(s_up, 16)
            sp.dma_start(gu_f[:, E * I:], a["suT"]).then_inc(s_up, 16)
            flatten(Batch(1, 1, 0))

            def body(b, nxt, nxt2, prv):
                if nxt2:
                    load_x(nxt2)
                if nxt and not nxt.early:
                    flatten(nxt)

            body(Batch(0, 0, 0), Batch(1, 1, 0), Batch(2, 0, 1), None)
            with sp.Fori(0, 2) as i:
                body(Batch(2 * i + 1, 1, i), Batch(2 * i + 2, 0, i + 1), Batch(2 * i + 3, 1, i + 1), Batch(2 * i, 0, i))
                body(Batch(2 * i + 2, 0, i + 1), Batch(2 * i + 3, 1, i + 1), Batch(2 * i + 4, 0, i + 2), Batch(2 * i + 1, 1, i))
            body(Batch(5, 1, 2), Batch(6, 0, 3), Batch(7, 1, 3), Batch(4, 0, 2))
            body(Batch(6, 0, 3), Batch(7, 1, 3), None, Batch(5, 1, 2))
            with sp.Fori(0, NBLK) as n:
                sp.wait_ge(s_fo, 4 * n + 4)
                sp.dma_start(out[bass.ds(n * BT, BT), :].rearrange("(t p) d -> p t d", p=P), fo[:, :, :]).then_inc(s_out, 16)
            sp.wait_ge(s_out, 16 * (NBLK + 1))

        def schedule(pieces, eng):
            def body(b, nxt, prv):
                pieces(b, nxt, prv)

            b = [Batch(k, k % 2, k // 2) for k in range(NB)]
            body(None, b[0], None)
            body(b[0], b[1], None)
            with eng.Fori(0, NB // 2 - 1) as i:
                k0, k1, k2, k3 = (Batch(2 * i + n, n % 2, i + n // 2) for n in range(4))
                body(k1, k2, k0)
                body(k2, k3, k1)
            body(b[7], None, b[6])
            body(None, None, b[7])

        @block.tensor
        def _(pe):
            def mm3(dst, hi, lo, rhi, rlo, first, last):
                pe.matmul(dst, hi, rhi, start=first, stop=False)
                pe.matmul(dst, hi, rlo, start=False, stop=False)
                return pe.matmul(dst, lo, rhi, start=False, stop=last)

            def dt_proj(b):
                pe.wait_ge(s_xh, b.k + 1)
                pe.wait_ge(s_xl, b.k + 1)
                if b.first:
                    pe.wait_ge(s_su, 2)
                    pe.wait_ge(s_sua, 2)
                else:
                    pe.wait_ge(s_pad, 4 * b.k)
                    pe.wait_ge(s_xd, 2 * b.k)
                h, l = xTh[b.par][:, K - 1:], xTl[b.par][:, K - 1:]
                mm3(ps_a[0:64, 0:L], w_hi[:, 256:320], w_lo[:, 256:320], h, l, True, True).then_inc(s_dtp, 1)

            def conv(b, dst, chunks):
                for m, ch in enumerate(chunks):
                    o = dst[:, m * L:(m + 1) * L]
                    for t in range(K):
                        c = slice(ch * P, ch * P + P)
                        mm3(o, cv_hi[:, t, c], cv_lo[:, t, c], xTh[b.par][:, t:t + L], xTl[b.par][:, t:t + L], t == 0, False)
                    ins = pe.matmul(o, cb_r[:, ch * P:ch * P + P], ones_r[:, :], start=False, stop=True)
                ins.then_inc(s_xp, 1)

            def x_proj(b):
                if b.first:
                    pe.wait_ge(s_su, 5)
                    pe.wait_ge(s_sua, 3)
                    pe.wait_ge(s_ps, N_PS)
                else:
                    pe.wait_ge(s_pad, 4 * b.k - 2)
                    pe.wait_ge(s_xd, 2 * b.k - 1)
                conv(b, ps_b, (0, 1))

            def bc_proj(b):
                pe.wait_ge(s_td, b.k + 1)
                conv(b, ps_a, (2, 3))

            def z_proj(b):
                pe.wait_ge(s_sl, 3 * b.k + 1)
                h, l = xTh[b.par][:, K - 1:], xTl[b.par][:, K - 1:]
                for m in range(2):
                    c = slice(m * P, m * P + P)
                    ins = mm3(ps_b[:, m * L:(m + 1) * L], w_hi[:, c], w_lo[:, c], h, l, True, True)
                ins.then_inc(s_xp, 1)

            def turn_dt(b):
                pe.wait_ge(s_sl, 3 * b.k + 2)
                pe.wait_ge(s_d2, b.k + 1)
                pe.wait_ge(s_dg, b.k + 1)
                pe.matmul(ps_a[:, 0:64], dd2[:, 0, :, :].rearrange("h a q -> h (a q)"), ident[0:64, 0:64], start=True, stop=True)
                for c in range(1, NC):
                    pe.transpose(ps_a[:, c * 64:c * 64 + 64], dd2[:, c, :, :].rearrange("h a q -> h (a q)"), ident[0:64, 0:64])
                pe.matmul(ps_a[:, 256:320], ones32[:, :], ddiag[:, :, :], start=True, stop=True).then_inc(s_ddp, 1)

            def turn_b(b):
                pe.wait_ge(s_sl, 3 * b.k + 3)
                pe.matmul(ps_b[0:Q, 0:P], bc[b.par][:, 0, 0:Q], ident[:, :], start=True, stop=True)
                for c in range(1, 3):
                    ins = pe.transpose(ps_b[0:Q, c * P:c * P + P], bc[b.par][:, 0, c * Q:c * Q + Q], ident[:, :])
                ins.then_inc(s_btp, 1)

            def spread_exp(b):
                pe.wait_ge(s_ddt, b.k + 1)
                pe.wait_ge(s_eh, b.k + 1)
                pe.wait_ge(s_el, b.k + 1)
                if b.first:
                    pe.wait_ge(s_ps, N_PS)
                for m in range(2):
                    ins = pe.matmul(ps_a[:, m * L:(m + 1) * L], selE[:, m * P:(m + 1) * P], e_hl[:, :], start=True, stop=True)
                ins.then_inc(s_ebp, 1)

            def turn_x(b):
                pe.wait_ge(s_bt, b.k + 1)
                pe.wait_ge(s_x2, 2 * (b.k + 1))
                for c in range(NC):
                    dst = ps_b if c < 2 else ps_a
                    if c == 2:
                        pe.wait_ge(s_eb, b.k + 1)
                    for m in range(2):
                        ins = pe.transpose(dst[:, (c % 2) * DI + m * P:(c % 2) * DI + (m + 1) * P],
                                           xs2[:, m, c, :, :].rearrange("h a q -> h (a q)"), ident[:, :])
                    if c % 2:
                        ins.then_inc(s_xtp, 1)

            def g_of(b):
                pe.wait_ge(s_b2, b.k + 1)
                for c in range(NC):
                    ins = pe.matmul(ps_gl[:, c * Q:c * Q + Q], b2[:, c, :, :].rearrange("h a q -> h (a q)"),
                                    bc[b.par][:, 1, c * Q:c * Q + Q], start=True, stop=True)
                ins.then_inc(s_g, 1)

            def seg(b, n):
                if n == 0:
                    pe.wait_ge(s_fl[b.par], 64 * (b.half + 1))
                    pe.wait_ge(s_ng, b.k + 1)
                if not (b.first and n < 2):
                    pe.wait_ge(s_e, 8 * b.k + n - 1)
                c, hf = n // 2, n % 2
                pe.matmul(ps_seg[hf][:, :], neg[b.par][:, c, :, :], mov[b.par][:, hf * 512:hf * 512 + 512],
                          start=True, stop=True).then_inc(s_sg, 1)

            def y_in(b, n):
                if n == 0:
                    pe.wait_ge(s_pad, 4 * (b.k + 1))
                    if not b.first:
                        pe.wait_ge(s_y, 5 * b.k)
                pe.wait_ge(s_m, 8 * b.k + n + 1)
                c, hf = n // 2, n % 2
                for i in range(2):
                    for j in range(4):
                        ins = pe.matmul(ps_y[32 * j:32 * j + 32, hf * L + c * Q:hf * L + c * Q + Q],
                                        xpad[:, c, (hf * 4 + j) * 96 + i * 32:(hf * 4 + j) * 96 + i * 32 + 32],
                                        mm[:, n % 2, (2 * j + i) * Q:(2 * j + i) * Q + Q], start=(i == 0), stop=(i == 1))
                ins.then_inc(s_yd, 1)

            def state(b, c):
                if c == 0:
                    pe.wait_ge(s_xd, 2 * (b.k + 1))
                    pe.wait_ge(s_bt, b.k + 1)
                    if not b.first:
                        pe.wait_ge(s_ln, 11 * b.k - 3)
                else:
                    pe.wait_ge(s_s, 3 * b.k + c)
                pe.matmul(ps_so[:, 0:DI], btok[:, c, :], xdd[:, c, :], start=True, stop=True).then_inc(s_st, 1)

            def y_out(b):
                for c in range(1, NC):
                    pe.wait_ge(s_s, 3 * b.k + c)
                    for m in range(2):
                        ins = pe.matmul(ps_yo[:, m * L + c * Q:m * L + c * Q + Q], st[:, c - 1, m * P:(m + 1) * P],
                                        bc[b.par][:, 1, c * Q:c * Q + Q], start=True, stop=True)
                ins.then_inc(s_yo, 1)

            def project(b):
                pe.wait_ge(s_sq, b.k + 1)
                pe.wait_ge(s_y, 5 * (b.k + 1))
                pe.wait_ge(s_s, 3 * (b.k + 1))
                for t in range(NT):
                    for m in range(2):
                        pe.matmul(ps_so[:, t * D:(t + 1) * D], yf[:, m, t * P:(t + 1) * P], wo[:, m, :], start=(m == 0), stop=(m == 1))
                for t in range(NT):
                    for m in range(2):
                        ins = pe.matmul(ps_so[:, 256 + t:257 + t], ysq[:, m, t * P:(t + 1) * P], ones[:, 0:1], start=(m == 0), stop=(m == 1))
                ins.then_inc(s_op, 1)

            def turn_x1(b):
                pe.wait_ge(s_x1, 2 * (b.k + 1))
                if b.k is not None and not (isinstance(b.k, int) and b.k == 7):
                    pe.wait_ge(s_gm, b.k + 2)
                for t in range(NT):
                    ins = pe.transpose(ps_gl[:, t * P:(t + 1) * P], x1c[:, b.par, t, :], ident[:, :])
                ins.then_inc(s_x1p, 1)

            def logits(b):
                pe.wait_ge(s_x1f, 2 * (b.k + 1))
                for t in range(NT):
                    ins = pe.matmul(ps_gl[:, 256 + t * E:256 + (t + 1) * E], x1Tf[:, t * P:(t + 1) * P], gw[:, :], start=True, stop=True)
                ins.then_inc(s_lp, 1)

            def pieces(b, nxt, prv):
                if b:
                    g_of(b)
                    seg(b, 0)
                    seg(b, 1)
                if prv:
                    project(prv)
                if nxt:
                    dt_proj(nxt)
                    x_proj(nxt)
                if b:
                    y_in(b, 0)
                    seg(b, 2)
                    y_in(b, 1)
                    seg(b, 3)
                if nxt:
                    bc_proj(nxt)
                if b:
                    y_in(b, 2)
                    seg(b, 4)
                    state(b, 0)
                    y_in(b, 3)
                    seg(b, 5)
                if nxt:
                    z_proj(nxt)
                if prv:
                    turn_x1(prv)
                if b:
                    state(b, 1)
                    y_in(b, 4)
                    seg(b, 6)
                    y_in(b, 5)
                    seg(b, 7)
                    state(b, 2)
                if prv:
                    logits(prv)
                if nxt:
                    turn_dt(nxt)
                    turn_b(nxt)
                if b:
                    y_in(b, 6)
                    y_in(b, 7)
                    y_out(b)
                if nxt:
                    spread_exp(nxt)
                    turn_x(nxt)

            pe.wait_ge(s_su, 1)
            schedule(pieces, pe)

            pe.wait_ge(s_sua, 6)
            pe.wait_ge(s_sup, 2)
            pe.wait_ge(s_x1l, NB)
            steps = [(e, c) for e in ([E] + list(range(E))) for c in range(len(HC))]
            NS = len(steps)

            def up(n, s):
                e, c = steps[s]
                h0, hn = HC[c]
                w = slice(e * I + h0, e * I + h0 + hn)
                xh, xl = x1h[:, bass.ds(n * BT, BT)], x1l[:, bass.ds(n * BT, BT)]
                g, u = bank[s % 3], bank[3 + s % 3]
                if s >= 3:
                    pe.wait_ge(s_h, n * NS + s - 2)
                mm3(g[0:hn, :], g_hi[:, w], g_lo[:, w], xh, xl, True, True).then_inc(s_gp, 1)
                mm3(u[0:hn, :], u_hi[:, w], u_lo[:, w], xh, xl, True, True).then_inc(s_uo, 1)

            def down(n, s):
                e, c = steps[s]
                hn = HC[c][1]
                o = s // len(HC)
                pe.wait_ge(s_h, n * NS + s + 1)
                if c == 0:
                    pe.wait_ge(s_ac, n * 17 + 1 + (1 + 4 * (o - 2) if o >= 2 else 0))
                for t in range(4):
                    ins = pe.matmul(bank[6 + o % 2][:, t * D:(t + 1) * D], hh[0:hn, s % 3, t * P:(t + 1) * P], wd[0:hn, e, c, :],
                                    start=(c == 0 and t == 0), stop=(c == len(HC) - 1), skip_group_check=True)
                ins.then_inc(s_dn, 1)

            with pe.Fori(0, NBLK) as n:
                for s in range(NS + 2):
                    if s < NS:
                        up(n, s)
                    if s >= 2:
                        down(n, s - 2)

        @block.scalar
        def _(act):
            act.wait_ge(s_w, 16 * N_W)
            act.activation(aexp[:, :], alog[:, :], ACT.Exp).then_inc(s_sua, 1)
            act.wait_ge(s_su, 1)
            act.activation(w_hi[:, :], w_cv[:, :], ACT.Copy).then_inc(s_sua, 1)
            act.wait_ge(s_su, 4)
            act.activation(cv_hi[:, :, :], cw_b[:, :, :], ACT.Copy).then_inc(s_sua, 1)

            def x_high(b):
                act.wait_ge(s_xin[b.par], 32 * (b.half + 1))
                if not b.early:
                    act.wait_ge(s_xp, 3 * (b.k - 1))
                if b.first:
                    act.wait_ge(s_ps, N_PS)
                act.activation(xTh[b.par][:, K - 1:], xTf[:, b.par, :], ACT.Copy).then_inc(s_xh, 1)

            def dt_tanh(b):
                act.wait_ge(s_dtp, b.k + 1)
                if b.first:
                    act.wait_ge(s_su, 3)
                else:
                    act.wait_ge(s_dt, 3 * b.k - 2)
                act.activation(tdt[:, :], ps_a[0:64, 0:L], ACT.Tanh, bias=dtb_h[:, 0:1], scale=0.5).then_inc(s_td, 1)

            def silu_tanh(b, n, src):
                act.wait_ge(s_xp, 3 * b.k + n + 1)
                if not b.first:
                    act.wait_ge(s_sl, 3 * (b.k - 1) + n + 1)
                act.activation(th[:, n, :], src[:, :], ACT.Tanh).then_inc(s_th, 1)

            def exps(b):
                act.wait_ge(s_dt, 3 * (b.k + 1))
                if not b.first:
                    act.wait_ge(s_el, b.k)
                    act.wait_ge(s_dg, b.k)
                act.activation(eT[:, :], acum[:, :], ACT.Exp).then_inc(s_et, 1)
                act.wait_ge(s_df, b.k + 1)
                if not b.first:
                    act.wait_ge(s_dd, b.k)
                act.activation(adif[:, :], adif[:, :], ACT.Exp).then_inc(s_dc, 1)

            def double(b, part):
                if part == "x":
                    act.wait_ge(s_sl, 3 * b.k + 1)
                    if not b.first:
                        act.wait_ge(s_xtp, 2 * b.k)
                    for m in range(2):
                        act.activation(xs2[:, m, :, :, :], view(xs[b.par], 0, P, m * L, [[Q, NC], [0, 2], [1, Q]]), ACT.Copy).then_inc(s_x2, 1)
                elif part == "b":
                    act.wait_ge(s_sl, 3 * b.k + 2)
                    if not b.first:
                        act.wait_ge(s_g, b.k)
                    act.activation(b2[:, :, :, :], view(bc[b.par], 0, P, 0, [[Q, NC], [0, 2], [1, Q]]), ACT.Copy).then_inc(s_b2, 1)
                else:
                    act.wait_ge(s_dd, b.k + 1)
                    if not b.first:
                        act.wait_ge(s_ddp, b.k)
                    act.activation(dd2[:, :, :, :], view(dd, 0, 64, 0, [[Q, NC], [0, 2], [1, Q]]), ACT.Copy).then_inc(s_d2, 1)

            def copies(b):
                act.wait_ge(s_ddp, b.k + 1)
                if not b.first:
                    act.wait_ge(s_s, 3 * b.k)
                act.activation(ddt[:, :], ps_a[:, 0:320], ACT.Copy).then_inc(s_ddt, 1)
                act.wait_ge(s_btp, b.k + 1)
                if not b.first:
                    act.wait_ge(s_st, 3 * b.k)
                act.activation(btok[:, :, :], ps_b[0:Q, 0:384], ACT.Copy).then_inc(s_bt, 1)
                act.wait_ge(s_ebp, b.k + 1)
                if not b.early:
                    act.wait_ge(s_y, 5 * (b.k - 1))
                act.activation(eb[b.par][:, :, :], ps_a[:, :], ACT.Copy).then_inc(s_eb, 1)

            def decays(b, n):
                act.wait_ge(s_sg, 8 * b.k + n + 1)
                if not (b.first and n < 2):
                    act.wait_ge(s_m, 8 * b.k + n - 1)
                act.activation(ee[:, n % 2, :], ps_seg[n % 2][:, :], ACT.Exp).then_inc(s_e, 1)

            def y_square(b):
                act.wait_ge(s_y, 5 * (b.k + 1))
                if not b.first:
                    act.wait_ge(s_op, b.k)
                act.activation(ysq[:, :, :], yf[:, :, :], ACT.Square).then_inc(s_sq, 1)

            def x1_turned(b):
                act.wait_ge(s_x1p, b.k + 1)
                act.activation(x1Tf[:, :], ps_gl[:, 0:L], ACT.Copy).then_inc(s_x1f, 1)
                act.activation(x1h[:, bass.ds(b.k * L, L)], ps_gl[:, 0:L], ACT.Copy).then_inc(s_x1f, 1)

            def keep_logits(b):
                act.wait_ge(s_lp, b.k + 1)
                act.activation(lg[:, bass.ds(b.k * NT, NT), :], ps_gl[:, 256:256 + NT * E], ACT.Copy).then_inc(s_lg, 1)

            def pieces(b, nxt, prv):
                if nxt:
                    x_high(nxt)
                if b:
                    decays(b, 0)
                    decays(b, 1)
                if nxt:
                    dt_tanh(nxt)
                if b:
                    decays(b, 2)
                if nxt:
                    silu_tanh(nxt, 0, ps_b)
                if b:
                    decays(b, 3)
                if nxt:
                    exps(nxt)
                    silu_tanh(nxt, 1, ps_a)
                    double(nxt, "x")
                if b:
                    decays(b, 4)
                    decays(b, 5)
                if nxt:
                    silu_tanh(nxt, 2, ps_b)
                    double(nxt, "b")
                    double(nxt, "dt")
                if prv:
                    x1_turned(prv)
                if b:
                    decays(b, 6)
                    decays(b, 7)
                if prv:
                    keep_logits(prv)
                if nxt:
                    copies(nxt)
                if b:
                    y_square(b)

            def once():
                act.wait_ge(s_gu, 32)
                act.activation(g_hi[:, :], gu_f[:, :], ACT.Copy).then_inc(s_sua, 1)

            b = [Batch(k, k % 2, k // 2) for k in range(NB)]
            pieces(None, b[0], None)
            once()
            pieces(b[0], b[1], None)
            act.wait_ge(s_up, 32)
            act.activation(u_hi[:, :], gu_f[:, :], ACT.Copy).then_inc(s_sua, 1)
            with act.Fori(0, NB // 2 - 1) as i:
                k0, k1, k2, k3 = (Batch(2 * i + n, n % 2, i + n // 2) for n in range(4))
                pieces(k1, k2, k0)
                pieces(k2, k3, k1)
            pieces(b[7], None, b[6])
            pieces(None, None, b[7])
            act.wait_ge(s_cb, 2)
            act.activation(cex[:, :, :], cpr[:, :, :], ACT.Exp).then_inc(s_sua, 1)

            NS = NE * len(HC)
            with act.Fori(0, NBLK) as n:
                for s in range(NS):
                    hn = HC[s % 3][1]
                    act.wait_ge(s_gp, n * NS + s + 1)
                    if s >= 3:
                        act.wait_ge(s_h, n * NS + s - 2)
                    act.activation(sg[0:hn, s % 3, :], bank[s % 3][0:hn, :], ACT.Silu).then_inc(s_si, 1)

        @block.vector
        def _(dve):
            dve.wait_ge(s_w, 16 * N_W)
            dve.tensor_scalar(w_cv[:, 0:256], w_raw[:, 0:256], 0.5, None, ALU.mult)
            dve.tensor_scalar(w_cv[:, 256:320], w_raw[:, 768:832], 1.0, None, ALU.mult).then_inc(s_su, 1)
            dve.wait_ge(s_sua, 2)
            dve.tensor_tensor(w_lo[:, :], w_cv[:, :], w_hi[:, :].bitcast(F32), ALU.subtract).then_inc(s_su, 1)
            dve.tensor_scalar(dtb_h[:, :], dtb[:, :], 0.5, None, ALU.mult)
            dve.tensor_scalar(aneg[:, :], aexp[:, :], -1.0, None, ALU.mult).then_inc(s_su, 1)
            dve.scalar_tensor_tensor(out=cw_b[:, :, :], in0=cw_b[:, :, :], scalar=0.5,
                                     in1=view(x1, 0, P, 256, [[0, K], [1, 512]]), op0=ALU.mult, op1=ALU.mult).then_inc(s_su, 1)
            dve.wait_ge(s_sua, 3)
            dve.tensor_tensor(cv_lo[:, :, :], cw_b[:, :, :], cv_hi[:, :, :].bitcast(F32), ALU.subtract).then_inc(s_su, 1)

            def dt_chain(b):
                dve.wait_ge(s_td, b.k + 1)
                if not b.first:
                    dve.wait_ge(s_ddp, b.k)
                dve.tensor_scalar(dd[:, :], tdt[:, :], (DT_MAX - DT_MIN) / 2, (DT_MAX + DT_MIN) / 2, ALU.mult, ALU.add).then_inc(s_dt, 1)
                dve.wait_ge(s_dt, 3 * b.k + 1)
                dve.tensor_scalar(dA[:, :], dd[:, :], aneg[:, 0:1], None, ALU.mult).then_inc(s_dt, 1)
                dve.wait_ge(s_dt, 3 * b.k + 2)
                if not b.first:
                    dve.wait_ge(s_al, b.k)
                    dve.wait_ge(s_df, b.k)
                    dve.wait_ge(s_et, b.k)
                dve.tensor_tensor_scan(acum[:, :], reset[:, :], dA[:, :], 0.0, ALU.mult, ALU.add).then_inc(s_dt, 1)

            def silu(b, n, src, dst):
                dve.wait_ge(s_th, 3 * b.k + n + 1)
                if not b.early:
                    if n == 0:
                        dve.wait_ge(s_xtp, 2 * (b.k - 1))
                    if n == 1:
                        dve.wait_ge(s_yo, b.k - 1)
                        dve.wait_ge(s_btp, b.k - 1)
                    dve.wait_ge(s_y, 5 * (b.k - 1))
                dve.scalar_tensor_tensor(out=dst[b.par][:, :, :].rearrange("p a l -> p (a l)"), in0=th[:, n, :], scalar=1.0,
                                         in1=src[:, :], op0=ALU.add, op1=ALU.mult).then_inc(s_sl, 1)

            def pad_x(b, g):
                src = ps_b if g == 0 else ps_a
                dve.wait_ge(s_xtp, 2 * b.k + g + 1)
                if g == 0:
                    dve.wait_ge(s_ddt, b.k + 1)
                    if b.first:
                        dve.wait_ge(s_ps, N_PS)
                    else:
                        dve.wait_ge(s_yd, 8 * b.k)
                        dve.wait_ge(s_st, 3 * b.k)
                for h2 in range(2):
                    dve.tensor_tensor(view(xpad, 64 * h2, 64, 2 * g * PADW + 8 * h2, [[PADW, 2], [48, NP], [1, HD]]),
                                      view(src, 64 * h2, 64, 8 * h2, [[DI, 2], [16, NP], [1, HD]]),
                                      view(ddt, 64 * h2, 64, 2 * g * 64 + h2, [[64, 2], [2, NP], [0, HD]]),
                                      ALU.mult).then_inc(s_pad, 1)
                n = 2 if g == 0 else 1
                dve.tensor_tensor(view(xdd, 0, 64, 2 * g * DI, [[DI, n], [HD, NH], [1, HD]]),
                                  view(src, 0, 64, 0, [[DI, n], [HD, NH], [1, HD]]),
                                  view(ddt, 0, 64, 2 * g * 64 + 32, [[64, n], [1, NH], [0, HD]]),
                                  ALU.mult).then_inc(s_xd, 1)

            def g_mask(b):
                dve.wait_ge(s_g, b.k + 1)
                if not b.first:
                    dve.wait_ge(s_m, 8 * b.k)
                dve.tensor_tensor(gm[:, :, :], view(ps_gl, 0, P, 0, [[Q, NC], [1, Q]]), view(tril, 0, P, 0, [[0, NC], [1, Q]]),
                                  ALU.mult).then_inc(s_gm, 1)

            def m_of(b, n):
                if n == 0:
                    dve.wait_ge(s_gm, b.k + 1)
                dve.wait_ge(s_e, 8 * b.k + n + 1)
                if not (b.first and n < 2):
                    dve.wait_ge(s_yd, 8 * b.k + n - 1)
                c = n // 2
                dve.scalar_tensor_tensor(out=view(mm, 0, P, (n % 2) * 512, [[Q, 8], [1, Q]]), in0=view(ee, 0, P, (n % 2) * 512, [[Q, 8], [1, Q]]),
                                         scalar=1.0, in1=view(gm, 0, P, c * Q, [[0, 8], [1, Q]]), op0=ALU.min, op1=ALU.mult).then_inc(s_m, 1)

            def state(b, c):
                dve.wait_ge(s_st, 3 * b.k + c + 1)
                if c == 0:
                    if not b.first:
                        dve.wait_ge(s_yo, b.k)
                    dve.tensor_copy(st[:, 0, :], ps_so[:, 0:DI]).then_inc(s_s, 1)
                    return
                dve.wait_ge(s_s, 3 * b.k + c)
                dve.tensor_tensor(view(stm, 0, P, 0, [[HD, NH], [1, HD]]), view(st, 0, P, (c - 1) * DI, [[HD, NH], [1, HD]]),
                                  view(ddt, 0, P, 256 + (c - 1) * 32, [[1, NH], [0, HD]]), ALU.mult).then_inc(s_sm, 1)
                dve.wait_ge(s_sm, 2 * b.k + c)
                dve.tensor_tensor(st[:, c, :], stm[:, :], ps_so[:, 0:DI], ALU.add).then_inc(s_s, 1)

            def y_of(b):
                dve.wait_ge(s_yd, 8 * (b.k + 1))
                for m in range(2):
                    dve.scalar_tensor_tensor(out=yv[:, m, :], in0=xs[b.par][:, m, :], scalar=dskip[:, m:m + 1], in1=ps_y[:, m * L:(m + 1) * L],
                                             op0=ALU.mult, op1=ALU.add).then_inc(s_y, 1)
                dve.wait_ge(s_yo, b.k + 1)
                dve.wait_ge(s_eb, b.k + 1)
                dve.tensor_tensor(yo[:, :, Q:], view(ps_yo, 0, P, Q, [[L, 2], [1, L - Q]]), eb[b.par][:, :, Q:], ALU.mult).then_inc(s_y, 1)
                dve.wait_ge(s_y, 5 * b.k + 3)
                dve.tensor_tensor(yv[:, :, Q:], yv[:, :, Q:], yo[:, :, Q:], ALU.add).then_inc(s_y, 1)
                dve.wait_ge(s_y, 5 * b.k + 4)
                if not b.first:
                    dve.wait_ge(s_op, b.k)
                    dve.wait_ge(s_sq, b.k)
                dve.tensor_tensor(yf[:, :, :], yv[:, :, :], sz[b.par][:, :, :], ALU.mult).then_inc(s_y, 1)

            def norm_a(b):
                dve.wait_ge(s_op, b.k + 1)
                for t in range(NT):
                    dve.bn_stats(bn[:, t, :], ps_so[:, t * D:(t + 1) * D]).then_inc(s_ln, 1)
                dve.wait_ge(s_ln, 11 * b.k + 2)
                dve.tensor_scalar(m1[:, :], ps_so[:, 256:256 + NT], EPS / DI, EPS * EPS, ALU.mult, ALU.add).then_inc(s_ln, 1)
                for t in range(NT):
                    dve.bn_aggr(mv[:, t, :], bn[:, t, :]).then_inc(s_ln, 1)
                dve.wait_ge(s_ln, 11 * b.k + 5)
                dve.tensor_tensor(w1[:, :], mv[:, :, 1], m1[:, :], ALU.add).then_inc(s_ln, 1)

            def norm_b(b):
                dve.wait_ge(s_pw, 2 * b.k + 1)
                for t in range(NT):
                    dve.tensor_scalar(an[:, t, :], ps_so[:, t * D:(t + 1) * D], mv[:, t, 0:1], s1[:, t:t + 1], ALU.subtract, ALU.mult).then_inc(s_ln, 1)
                dve.wait_ge(s_ln, 11 * b.k + 8)
                dve.tensor_tensor(an[:, :, :], an[:, :, :], view(lnw, 0, P, 0, [[0, NT], [1, D]]), ALU.mult).then_inc(s_ln, 1)
                dve.wait_ge(s_ln, 11 * b.k + 9)
                dve.wait_ge(s_xx, b.k + 1)
                dve.tensor_tensor(rr[:, :, :], an[:, :, :], xx[:, b.par, :, :], ALU.add).then_inc(s_ln, 1)

            def norm_c(b):
                dve.wait_ge(s_ln, 11 * b.k + 10)
                for t in range(NT):
                    dve.bn_stats(bn2[:, t, :], rr[:, t, :]).then_inc(s_f2, 1)
                dve.wait_ge(s_f2, 5 * b.k + 2)
                dve.memset(pause[:, :], 0.0)
                for t in range(NT):
                    dve.bn_aggr(mv2[:, t, :], bn2[:, t, :]).then_inc(s_f2, 1)
                dve.wait_ge(s_f2, 5 * b.k + 4)
                dve.tensor_scalar(w2[:, :], mv2[:, :, 1], EPS, None, ALU.add).then_inc(s_f2, 1)

            def norm_d(b):
                dve.wait_ge(s_pw, 2 * b.k + 2)
                for t in range(NT):
                    dve.tensor_scalar(x1c[:, b.par, t, :], rr[:, t, :], mv2[:, t, 0:1], s2[:, t:t + 1], ALU.subtract, ALU.mult).then_inc(s_x1, 1)
                dve.memset(m1[:, 0:1], 0.0).then_inc(s_ln, 1)

            def pieces(b, nxt, prv):
                if b:
                    g_mask(b)
                    m_of(b, 0)
                if prv:
                    norm_a(prv)
                if b:
                    m_of(b, 1)
                if nxt:
                    dt_chain(nxt)
                if prv:
                    norm_b(prv)
                if b:
                    m_of(b, 2)
                if nxt:
                    silu(nxt, 0, ps_b, xs)
                if prv:
                    norm_c(prv)
                if b:
                    m_of(b, 3)
                    state(b, 0)
                if prv:
                    norm_d(prv)
                if nxt:
                    silu(nxt, 1, ps_a, bc)
                if b:
                    m_of(b, 4)
                    state(b, 1)
                    m_of(b, 5)
                if nxt:
                    silu(nxt, 2, ps_b, sz)
                if b:
                    m_of(b, 6)
                    state(b, 2)
                    m_of(b, 7)
                    y_of(b)
                if nxt:
                    pad_x(nxt, 0)
                    pad_x(nxt, 1)

            schedule(pieces, dve)

            dve.wait_ge(s_lg, NB)
            steps = 0

            def did(ins):
                nonlocal steps
                steps += 1
                ins.then_inc(s_cb, 1)
                dve.wait_ge(s_cb, steps)

            def over_e(t):
                return view(t, 0, P, 0, [[1, NTT], [0, E]])

            did(dve.tensor_reduce(cmx[:, :], lg[:, :, :], mybir.AxisListType.X, ALU.max))
            did(dve.tensor_tensor(cpr[:, :, :], lg[:, :, :], over_e(cmx), ALU.subtract))
            dve.wait_ge(s_sua, 6)
            did(dve.tensor_reduce(csm[:, :], cex[:, :, :], mybir.AxisListType.X, ALU.add))
            did(dve.reciprocal(crc[:, :], csm[:, :]))
            did(dve.tensor_tensor(cpr[:, :, :], cex[:, :, :], over_e(crc), ALU.mult))
            pairs = [(f, g) for f in range(E) for g in range(f + 1, E)]
            for n, (f, g) in enumerate(pairs):
                did(dve.tensor_tensor(cge[:, n, :], cpr[:, :, f], cpr[:, :, g], ALU.is_ge))
            for e in range(E):
                did(dve.memset(crk[:, :, e], float(E - 1 - e)))
                for n, (f, g) in enumerate(pairs):
                    if e in (f, g):
                        did(dve.tensor_tensor(crk[:, :, e], crk[:, :, e], cge[:, n, :], ALU.add if e == g else ALU.subtract))
            did(dve.scalar_tensor_tensor(out=csl[:, :, :], in0=crk[:, :, :], scalar=1.5, in1=cpr[:, :, :], op0=ALU.is_lt, op1=ALU.mult))
            did(dve.tensor_reduce(cts[:, :], csl[:, :, :], mybir.AxisListType.X, ALU.add))
            did(dve.tensor_scalar(csm[:, :], cts[:, :], 1e-20, None, ALU.add))
            did(dve.reciprocal(crc[:, :], csm[:, :]))
            dve.tensor_tensor(comb[:, :, :], csl[:, :, :], over_e(crc), ALU.mult).then_inc(s_ac, 1)

            NS = NE * len(HC)
            dve.wait_ge(s_kp, NB)

            def hidden(n, s):
                hn = HC[s % 3][1]
                dve.wait_ge(s_si, n * NS + s + 1)
                dve.wait_ge(s_uo, n * NS + s + 1)
                if s >= 3:
                    dve.wait_ge(s_dn, n * NS + s - 2)
                dve.tensor_tensor(hh[0:hn, s % 3, :], sg[0:hn, s % 3, :], bank[3 + s % 3][0:hn, :], ALU.mult).then_inc(s_h, 1)

            def add_expert(n, o):
                dve.wait_ge(s_dn, n * NS + 3 * o + 3)
                ps = bank[6 + o % 2]
                if o == 0:
                    dve.tensor_tensor(yv[:, :, :].rearrange("p a l -> p (a l)"), ps[:, :],
                                      x1[:, bass.ds(n * 4, 4), :].rearrange("p t d -> p (t d)"), ALU.add).then_inc(s_ac, 1)
                    return
                dve.wait_ge(s_ac, 17 * n + 2 + 4 * (o - 1))
                for t in range(4):
                    dve.scalar_tensor_tensor(out=acc[:, t, :], in0=ps[:, t * D:(t + 1) * D], scalar=comb[:, bass.ds(n * 4 + t, 1), o - 1],
                                             in1=acc[:, t, :], op0=ALU.mult, op1=ALU.add).then_inc(s_ac, 1)

            with dve.Fori(0, NBLK) as n:
                for s in range(NS):
                    hidden(n, s)
                    if s >= 5 and s % 3 == 2:
                        add_expert(n, s // 3 - 1)
                add_expert(n, NE - 1)
                dve.wait_ge(s_ac, 17 * n + 18)
                for t in range(4):
                    dve.bn_stats(fbn[:, t, :], acc[:, t, :]).then_inc(s_f2, 1)
                dve.wait_ge(s_f2, 5 * NB + 9 * n + 4)
                dve.memset(pause[:, :], 0.0)
                for t in range(4):
                    dve.bn_aggr(fmv[:, t, :], fbn[:, t, :]).then_inc(s_f2, 1)
                dve.wait_ge(s_f2, 5 * NB + 9 * n + 8)
                dve.tensor_scalar(fw[:, :], fmv[:, :, 1], EPS, None, ALU.add).then_inc(s_f2, 1)
                dve.wait_ge(s_fp, n + 1)
                dve.wait_ge(s_out, 16 * (n + 1))
                for t in range(4):
                    dve.tensor_scalar(fo[:, t, :], acc[:, t, :], fmv[:, t, 0:1], fs[:, t:t + 1], ALU.subtract, ALU.mult).then_inc(s_fo, 1)

        @block.gpsimd
        def _(pool):
            steps = 0

            def step(ins):
                nonlocal steps
                steps += 1
                ins.then_inc(s_ps, 1)
                pool.wait_ge(s_ps, steps)

            for p in range(2):
                pool.memset(xTh[p][:, 0:K - 1].bitcast(F32), 0.0)
                pool.memset(xTl[p][:, 0:K - 1].bitcast(F32), 0.0)
            pool.memset(xpad[:, :, :], 0.0)
            pool.memset(ones[:, :], 1.0)
            pool.memset(mhalf[:, :], -0.5)
            step(pool.memset(pause[:, :], 0.0))
            step(pool.memset(ones32[:, :], 1.0))
            step(pool.memset(ones_r[:, :].bitcast(F32), 1.0))
            pool.wait_ge(s_w, 16 * N_W)
            for p in range(2):
                step(pool.tensor_copy(neg[p][64:NR, :, :, :].rearrange("r c h q -> r (c h q)"), ones4_f[64:NR, :, :].rearrange("r c n -> r (c n)")))
                step(pool.tensor_copy(mov[p][0:64, :], sel_f))
            step(pool.tensor_copy(selE[:, :], selE_f))
            step(pool.tensor_scalar(cb_s, cb_f, 0.5, None, ALU.mult))
            step(pool.tensor_copy(cb_r[:, :], cb_s))
            step(pool.tensor_scalar(cb_h, cb_r[:, :].bitcast(F32), hilo[:, 0:1], None, ALU.mult))
            step(pool.tensor_scalar(cb_s, cb_s, hilo[:, 1:2], None, ALU.mult))
            step(pool.tensor_tensor(cb_r[:, :], cb_s, cb_h, ALU.add))

            def x_low(b):
                pool.wait_ge(s_xh, b.k + 1)
                if not b.early:
                    pool.wait_ge(s_xp, 3 * (b.k - 1))
                pool.tensor_tensor(xTl[b.par][:, K - 1:], xTf[:, b.par, :], xTh[b.par][:, K - 1:].bitcast(F32), ALU.subtract).then_inc(s_xl, 1)

            def sums(b):
                pool.wait_ge(s_dt, 3 * (b.k + 1))
                if not b.first:
                    pool.wait_ge(s_fw, 16 * b.k)
                pool.tensor_tensor(view(adif, 0, 64, 0, [[Q, NC], [1, Q]]), view(acum, 0, 64, Q - 1, [[Q, NC], [0, Q]]),
                                   view(acum, 0, 64, 0, [[Q, NC], [1, Q]]), ALU.subtract).then_inc(s_df, 1)
                pool.tensor_copy(a_hl[:, :], acum[:, :]).then_inc(s_ah, 1)
                pool.wait_ge(s_ah, b.k + 1)
                pool.wait_ge(s_df, b.k + 1)
                pool.tensor_tensor(a_hl[32:64, :], acum[32:64, :], a_hl[32:64, :].bitcast(F32), ALU.subtract).then_inc(s_al, 1)
                pool.wait_ge(s_al, b.k + 1)
                if not b.early:
                    pool.wait_ge(s_sg, 8 * (b.k - 1))
                pool.tensor_tensor(neg[b.par][0:64, :, :, :], view(a_hl, 0, 64, 0, [[Q, NC], [0, 2], [1, Q]]).bitcast(F32),
                                   view(negpar, 0, 64, 0, [[0, NC], [1, 2], [0, Q]]), ALU.mult).then_inc(s_ng, 1)

            def exp_parts(b):
                pool.wait_ge(s_et, b.k + 1)
                if not b.first:
                    pool.wait_ge(s_ddp, b.k)
                    pool.wait_ge(s_ebp, b.k)
                pool.tensor_tensor(ddiag[:, :, :], view(ident, 0, 32, 0, [[0, 2], [1, NH]]), view(eT, 0, 32, 2 * Q - 1, [[Q, 2], [0, NH]]),
                                   ALU.mult).then_inc(s_dg, 1)
                pool.tensor_copy(e_hl[:, :], eT[:, :]).then_inc(s_eh, 1)
                pool.wait_ge(s_dc, b.k + 1)
                pool.wait_ge(s_eh, b.k + 1)
                pool.wait_ge(s_dg, b.k + 1)
                pool.tensor_tensor(dd[32:64, :], dd[32:64, :], adif[32:64, :], ALU.mult).then_inc(s_dd, 1)
                pool.tensor_tensor(e_hl[32:64, :], eT[32:64, :], e_hl[32:64, :].bitcast(F32), ALU.subtract).then_inc(s_el, 1)
                pool.wait_ge(s_el, b.k + 1)
                pool.wait_ge(s_dd, b.k + 1)

            def double_x(b):
                if b.first:
                    pool.wait_ge(s_w2, 16 * 9)
                pool.wait_ge(s_xin[b.par], 32 * (b.half + 1))
                if not b.early:
                    pool.wait_ge(s_ln, 11 * (b.k - 1))
                pool.tensor_tensor(xx[:, b.par, :, :], xtok[:, b.par, :, :], xtok[:, b.par, :, :], ALU.add).then_inc(s_x2x, 1)
                pool.wait_ge(s_x2x, b.k + 1)
                pool.tensor_tensor(xx[:, b.par, :, :], xx[:, b.par, :, :], view(lnb, 0, P, 0, [[0, NT], [1, D]]), ALU.add).then_inc(s_xx, 1)

            def power_a(b):
                pool.wait_ge(s_ln, 11 * b.k + 6)
                pool.tensor_tensor(s1[:, :], w1[:, :], mhalf[:, 0:NT], ALU.pow).then_inc(s_pw, 1)

            def power_b(b):
                pool.wait_ge(s_f2, 5 * (b.k + 1))
                pool.tensor_tensor(s2[:, :], w2[:, :], mhalf[:, 0:NT], ALU.pow).then_inc(s_pw, 1)

            def keep_x1(b):
                pool.wait_ge(s_x1, 2 * (b.k + 1))
                pool.tensor_copy(x1[:, bass.ds(b.k * NT, NT), :], x1c[:, b.par, :, :]).then_inc(s_kp, 1)

            def x1_low(b):
                pool.wait_ge(s_x1f, 2 * (b.k + 1))
                pool.tensor_tensor(x1l[:, bass.ds(b.k * L, L)], x1Tf[:, :], x1h[:, bass.ds(b.k * L, L)].bitcast(F32), ALU.subtract).then_inc(s_x1l, 1)

            def pieces(b, nxt, prv):
                if nxt:
                    x_low(nxt)
                if prv:
                    power_a(prv)
                if nxt:
                    sums(nxt)
                if prv:
                    power_b(prv)
                if nxt:
                    exp_parts(nxt)
                    double_x(nxt)
                if prv:
                    keep_x1(prv)
                    x1_low(prv)

            b = [Batch(k, k % 2, k // 2) for k in range(NB)]
            pieces(None, b[0], None)
            pool.wait_ge(s_w2, 16 * 9)
            for m in range(2):
                pool.tensor_scalar(wo[:, m, :], wo_f[:, m, :], nw[:, m:m + 1], None, ALU.mult)
            pool.wait_ge(s_sua, 4)
            pool.tensor_tensor(g_lo[:, :], gu_f[:, :], g_hi[:, :].bitcast(F32), ALU.subtract).then_inc(s_sup, 1)
            pieces(b[0], b[1], None)
            pool.wait_ge(s_sua, 5)
            pool.tensor_tensor(u_lo[:, :], gu_f[:, :], u_hi[:, :].bitcast(F32), ALU.subtract).then_inc(s_sup, 1)
            with pool.Fori(0, NB // 2 - 1) as i:
                k0, k1, k2, k3 = (Batch(2 * i + n, n % 2, i + n // 2) for n in range(4))
                pieces(k1, k2, k0)
                pieces(k2, k3, k1)
            pieces(b[7], None, b[6])
            pieces(None, None, b[7])
            with pool.Fori(0, NBLK) as n:
                pool.wait_ge(s_f2, 5 * NB + 9 * n + 9)
                pool.tensor_tensor(fs[:, :], fw[:, :], mhalf[:, :], ALU.pow).then_inc(s_fp, 1)


def constants():
    h = np.arange(NH)
    pr = np.arange(NP * Q) // Q
    sel = (h[:, None] // 2 == pr[None, :]).astype(np.float32)
    selE = (h[:, None] == np.arange(DI)[None, :] // HD).astype(np.float32)
    par = -(h[:, None] % 2 == np.arange(2)[None, :]).astype(np.float32)
    s, q = np.arange(P) % Q, np.arange(Q)
    row, col = np.arange(4 * NC)[:, None, None], np.arange(P)[None, None, :]
    rows = ((row // NC % 2 == col // Q) & (row % NC == np.arange(NC)[None, :, None])).astype(np.float32)
    return {
        "c_ident": np.eye(P, dtype=np.float32),
        "c_tril": (q[None, :] >= s[:, None]).astype(np.float32),
        "c_negpar": np.concatenate([par, par]),
        "c_reset": np.tile((np.arange(L) % Q != 0).astype(np.float32), (64, 1)),
        "c_selE": np.concatenate([selE, selE]),
        "c_sel": np.concatenate([sel, sel]),
        "c_hilo": np.array([[1, 0], [-1, 1]], np.float32),
        "c_ones4": rows,
    }


def kernel(**inputs):
    import concourse.bacc as _bacc
    from concourse import mybir as _mybir
    from concourse.bass_utils import run_bass_kernel_spmd as _run

    v = {n.replace("L0_attn_", "").replace("L0_ffn_", ""): np.asarray(x) for n, x in inputs.items()}
    arrays = {
        "x": v["x"], "xT": v["x"].transpose(0, 2, 1), "in_wT": v["in_proj_w"].T, "cwT": v["conv_w"].T, "cb": v["conv_b"][None],
        "dtb": v["dt_bias"][:, None], "alog": v["A_log"][:, None],
        "dskip": np.repeat(v["D_skip"], HD).reshape(2, P).T, "nw": v["norm_w"].reshape(2, P).T,
        "woT": v["out_proj_w"].T, "lnw": v["ln_w"][None], "lnb": v["ln_b"][None], "gwT": v["gate_w"].T,
        "egT": v["eg"].transpose(2, 0, 1).reshape(D, E * I), "euT": v["eu"].transpose(2, 0, 1).reshape(D, E * I),
        "edT": v["ed"].transpose(0, 2, 1), "sgT": v["sg"].T, "suT": v["su"].T, "sdT": v["sd"].T,
        **constants(),
    }
    nc = _bacc.Bacc("TRN2", target_bir_lowering=False, num_devices=1)
    data, aps = {}, {}
    for name, x in arrays.items():
        data[f"in_{name}"] = np.ascontiguousarray(x)
        aps[name] = nc.dram_tensor(f"in_{name}", x.shape, _mybir.dt.from_np(x.dtype), kind="ExternalInput").ap()
    out = nc.dram_tensor("out_0", (NB * L, D), _mybir.dt.float32, kind="ExternalOutput").ap()
    mamba_moe(nc, aps, out)
    r = _run(nc, [data], core_ids=[0])
    return r.results[0]["out_0"].reshape(NB, L, D)
```

```python
from contextlib import ExitStack

import numpy as np

import concourse.bass as bass
from concourse import mybir

F32 = mybir.dt.float32
F32R = mybir.dt.float32r
ALU = mybir.AluOpType
ACT = mybir.ActivationFunctionType

P = 128
NB, L, D = 8, 256, 128
NT = L // P
Q = 64
NC = L // Q
NH, HD = 32, 8
DI = NH * HD
NP = NH // 2
K = 4
DT_MIN, DT_MAX = 0.001, 0.1
EPS = 1e-5
E, I = 4, 344
NE = E + 1
HC = [(0, 128), (128, 128), (256, 88)]
BT = 512
NBLK = NB * L // BT
NR = 64 + 4 * NC
PADW = 96 * NH // 4


class Batch:

    def __init__(self, k, par, half):
        self.k, self.par, self.half = k, par, half
        self.first = isinstance(k, int) and k == 0
        self.early = isinstance(k, int) and k < 2


def mamba_moe(nc, a, out):
    with ExitStack() as ctx:
        def sb(name, shape, dt=F32):
            return ctx.enter_context(nc.sbuf_tensor(name, shape, dt))

        def sem(name):
            return ctx.enter_context(nc.semaphore(name))

        def view(t, part, nparts, off, dims):
            row = 1
            for n in t.shape[1:]:
                row *= n
            return bass.AP(t, part * row + off, [[row, nparts], *dims])

        sums_d = [nc.dram_tensor(f"sums_d{p}", [64, NC, Q], F32, kind="Internal").ap() for p in range(2)]

        bank = [ctx.enter_context(nc.psum_tensor(f"bank{i}", [P, 512], F32)) for i in range(8)]
        ps_seg = bank[0:2]
        ps_y = bank[2]
        ps_yo = bank[3]
        ps_gl = bank[4]
        ps_so = bank[5]
        ps_a, ps_b = bank[6], bank[7]

        ident = sb("ident", [P, P])
        tril = sb("tril", [P, Q])
        negpar = sb("negpar", [64, 2])
        reset = sb("reset", [64, L])
        selE = sb("selE", [64, DI], F32R)
        ones4_f = sb("ones4_f", [NR, NC, P])
        hilo = sb("hilo", [2, 2])
        ones = sb("ones", [P, 2])
        ones32 = sb("ones32", [32, P])
        cw_b = sb("cw_b", [P, K, 512])
        w_cv = sb("w_cv", [P, 320])
        w_hi = sb("w_hi", [P, 320], F32R)
        w_lo = sb("w_lo", [P, 320], F32R)
        cv_hi = sb("cv_hi", [P, K, 512], F32R)
        cv_lo = sb("cv_lo", [P, K, 512], F32R)
        cb_s = sb("cb_s", [2, 512], F32R)
        cb_r = sb("cb_r", [2, 512], F32R)
        ones_r = sb("ones_r", [2, L], F32R)
        dtb = sb("dtb", [64, 1])
        dtb_h = sb("dtb_h", [64, 1])
        alog = sb("alog", [64, 1])
        aexp = sb("aexp", [64, 1])
        aneg = sb("aneg", [64, 1])
        dskip = sb("dskip", [P, 2])
        nw = sb("nw", [P, 2])
        wo = sb("wo", [P, 2, D])
        lnw = sb("lnw", [P, D])
        lnb = sb("lnb", [P, D])
        gw = sb("gw", [D, E])
        g_hi = sb("g_hi", [D, NE * I], F32R)
        g_lo = sb("g_lo", [D, NE * I], F32R)
        u_hi = sb("u_hi", [D, NE * I], F32R)
        u_lo = sb("u_lo", [D, NE * I], F32R)
        wd = sb("wd", [P, NE, len(HC), D])

        xTf = sb("xTf", [D, 2, L])
        xtok = sb("xtok", [P, 2, NT, D])
        xTh = [sb(f"xTh{p}", [D, K - 1 + L], F32R) for p in range(2)]
        xTl = [sb(f"xTl{p}", [D, K - 1 + L], F32R) for p in range(2)]
        th = sb("th", [P, 3, 512])
        tdt = sb("tdt", [64, L])
        dd = sb("dd", [64, L])
        dA = sb("dA", [64, L])
        acum = sb("acum", [64, L])
        a_hl = sb("a_hl", [64, L], F32R)
        adif = sb("adif", [64, L])
        eT = sb("eT", [64, L])
        e_hl = sb("e_hl", [64, L], F32R)
        ddiag = sb("ddiag", [32, 2, NH])
        neg = [sb(f"neg{p}", [NR, NC, 2, Q], F32R) for p in range(2)]
        mov = [sb(f"mov{p}", [NR, NP * Q], F32R) for p in range(2)]
        xs = [sb(f"xs{p}", [P, 2, L]) for p in range(2)]
        bc = [sb(f"bc{p}", [P, 2, L]) for p in range(2)]
        sz = [sb(f"sz{p}", [P, 2, L]) for p in range(2)]
        dd2 = sb("dd2", [64, NC, 2, Q])
        b2 = sb("b2", [P, NC, 2, Q])
        xs2 = sb("xs2", [P, 2, NC, 2, Q])
        ddt = sb("ddt", [P, NC * 64 + 64])
        btok = sb("btok", [Q, 3, P])
        eb = [sb(f"eb{p}", [P, 2, L]) for p in range(2)]
        xpad = sb("xpad", [P, NC, PADW])
        xdd = sb("xdd", [Q, 3, DI])
        gm = sb("gm", [P, NC, Q])
        ee = sb("ee", [P, 2, 512])
        mm = sb("mm", [P, 2, 512])
        sel_f, selE_f = ee[0:64, :, :].rearrange("p a n -> p (a n)"), mm[0:64, 0, 0:DI]
        st = sb("st", [P, 3, DI])
        stm = sb("stm", [P, DI])
        yo = sb("yo", [P, 2, L])
        yv = sb("yv", [P, 2, L])
        yf = sb("yf", [P, 2, L])
        ysq = sb("ysq", [P, 2, L])
        cb_f, cb_h = (t[0:2, :, :].rearrange("r m l -> r (m l)") for t in (yo, yv))
        xx = sb("xx", [P, 2, NT, D])
        bn = sb("bn", [P, NT, 6])
        mv = sb("mv", [P, NT, 2])
        m1 = sb("m1", [P, NT])
        w1 = sb("w1", [P, NT])
        s1 = sb("s1", [P, NT])
        an = sb("an", [P, NT, D])
        rr = sb("rr", [P, NT, D])
        bn2 = sb("bn2", [P, NT, 6])
        mv2 = sb("mv2", [P, NT, 2])
        s2 = sb("s2", [P, NT])
        pause = sb("pause", [P, 1])
        w2 = sb("w2", [P, NT])
        mhalf = sb("mhalf", [P, 4])
        x1c = sb("x1c", [P, 2, NT, D])
        x1Tf = sb("x1Tf", [D, L])
        x1 = sb("x1", [P, NB * NT, D])
        x1_flat = x1[:, :, :].rearrange("p t d -> p (t d)")
        w_raw, gu_f = x1_flat[:, 0:832], x1_flat[:, 0:NE * I]
        wo_f = x1_flat[:, NE * I:NE * I + 2 * D].rearrange("p (g d) -> p g d", g=2)
        x1h = sb("x1h", [D, NB * L], F32R)
        x1l = sb("x1l", [D, NB * L], F32R)
        lg = sb("lg", [P, NB * NT, E])

        s_wi = sem("projections_weights_loaded")
        s_wc = sem("taps_loaded")
        s_ws = sem("small_weights_loaded")
        s_w = sem("constants_loaded")
        s_w2 = sem("ffn_weights_loaded")
        s_lnb = sem("norm_bias_loaded")
        s_gu = sem("gate_loaded")
        s_up = sem("up_loaded")
        s_xin = [sem(f"x_loaded{p}") for p in range(2)]
        s_su = sem("setup_vector")
        s_sua = sem("setup_scalar")
        s_sup = sem("setup_pool")
        s_ps = sem("pool_setup_step")
        s_sr = sem("constant_rows")
        s_pz = sem("x_padding_zero")
        s_xh = sem("x_high")
        s_xl = sem("x_low")
        s_dtp = sem("dt_in_psum")
        s_xp = sem("xbc_z_in_psum")
        s_td = sem("dt_tanh")
        s_th = sem("silu_tanh")
        s_dt = sem("dt_chain")
        s_sl = sem("silu_done")
        s_ah = sem("sums_high")
        s_al = sem("sums_low")
        s_ng = sem("neg_sums")
        s_df = sem("decay_exponent")
        s_et = sem("exp_sums")
        s_dc = sem("exp_decay")
        s_eh = sem("exp_high")
        s_el = sem("exp_low")
        s_dd = sem("dt_decayed")
        s_dg = sem("decay_diagonal")
        s_fl = [sem(f"sums_flat{p}") for p in range(2)]
        s_d2 = sem("dt_doubled")
        s_b2 = sem("b_doubled")
        s_x2 = sem("x_doubled")
        s_fw = sem("sums_in_dram")
        s_ddp = sem("dt_tokens_psum")
        s_btp = sem("b_tokens_psum")
        s_ebp = sem("exp_rows_psum")
        s_xtp = sem("x_tokens_psum")
        s_ddt = sem("dt_tokens")
        s_bt = sem("b_tokens")
        s_eb = sem("exp_rows")
        s_pad = sem("x_padded")
        s_xd = sem("x_decayed")
        s_g = sem("g_in_psum")
        s_gm = sem("g_masked")
        s_sg = sem("seg_in_psum")
        s_e = sem("decays")
        s_m = sem("m_ready")
        s_yd = sem("yd_done")
        s_st = sem("state_in_psum")
        s_s = sem("state_ready")
        s_sm = sem("state_decayed")
        s_yo = sem("yo_in_psum")
        s_y = sem("y_steps")
        s_sq = sem("y_squared")
        s_op = sem("proj_in_psum")
        s_x2x = sem("x_doubled_sum")
        s_xx = sem("residual_ready")
        s_ln = sem("norm_steps")
        s_pw = sem("rsqrt_done")
        s_x1 = sem("x1_ready")
        s_kp = sem("x1_kept")
        s_x1p = sem("x1t_in_psum")
        s_x1f = sem("x1t_copied")
        s_x1l = sem("x1t_low")
        s_lp = sem("logits_in_psum")
        s_lg = sem("logits_kept")
        s_gp = sem("gate_in_psum")
        s_uo = sem("up_in_psum")
        s_si = sem("gate_silu")
        s_h = sem("hidden_ready")
        s_dn = sem("hidden_used")
        s_ye = sem("expert_in_psum")
        s_cb = sem("comb_steps")
        s_ac = sem("acc_steps")
        s_f2 = sem("final_stats")
        s_fp = sem("final_rsqrt")
        s_fo = sem("final_ready")
        s_out = sem("stored")
        sg, hh = cw_b, th
        fbn = sb("fbn", [P, 4, 6])
        fmv = sb("fmv", [P, 4, 2])
        fs = sb("fs", [P, 4])
        fw = sb("fw", [P, 4])
        acc, fo = yv[:, :, :].rearrange("p a (t d) -> p (a t) d", d=D), yf[:, :, :].rearrange("p a (t d) -> p (a t) d", d=D)
        NTT = NB * NT
        cmx = sb("cmx", [P, NTT])
        cex = sb("cex", [P, NTT, E])
        csm = sb("csm", [P, NTT])
        crc = sb("crc", [P, NTT])
        cpr = sb("cpr", [P, NTT, E])
        cge = sb("cge", [P, NTT, E, E])
        crk = sb("crk", [P, NTT, E])
        csl = sb("csl", [P, NTT, E])
        cts = sb("cts", [P, NTT])
        comb = sb("comb", [P, NTT, E])

        block = ctx.enter_context(nc.Block())

        N_W = 9
        N_PS = 3

        @block.sync
        def _(sp):
            def load_x(b):
                at, once = (x if isinstance(x, int) else sp.snap(x) for x in (b.k * (D * L), b.k - 1))
                if not b.early:
                    sp.wait_ge(s_xh, once)
                    sp.wait_ge(s_xl, once)
                    sp.wait_ge(s_x2x, once)
                sp.dma_start(xTf[:, b.par, :], bass.AP(a["xT"].tensor, at, [[L, D], [1, L]])).then_inc(s_xin[b.par], 16)
                sp.dma_start(xtok[:, b.par, :, :], bass.AP(a["x"].tensor, at, [[D, P], [P * D, NT], [1, D]])).then_inc(s_xin[b.par], 16)

            def flatten(b):
                made, sent = (x if isinstance(x, int) else sp.snap(x) for x in (b.k + 1, 16 * (b.k + 1)))
                sp.wait_ge(s_ah, made)
                sp.wait_ge(s_al, made)
                if not b.early:
                    sp.wait_ge(s_g, b.k)
                sp.dma_start(sums_d[b.par].rearrange("h c q -> h (c q)"), a_hl[:, :].bitcast(F32)).then_inc(s_fw, 16)
                sp.wait_ge(s_fw, sent)
                for part in range(2):
                    for h2 in range(2):
                        row = 64 + NC * (2 * part + h2)
                        dst = mov[b.par][row:row + NC, :].bitcast(F32).rearrange("c (h q) -> c h q", q=Q)
                        src = sums_d[b.par][32 * part:32 * part + 32].rearrange("(h g) c q -> g c h q", g=2)[h2]
                        sp.dma_start(dst, src).then_inc(s_fl[b.par], 16)

            sp.dma_start(w_raw[:, 0:256], a["in_wT"][:, 0:256]).then_inc(s_wi, 16)
            for r in range(2):
                sp.dma_start(w_raw[:, 768 + 32 * r:800 + 32 * r], a["in_wT"][:, 768:800]).then_inc(s_wi, 16)
            load_x(Batch(0, 0, 0))
            sp.dma_start(w_raw[:, 256:768], a["in_wT"][:, 256:768]).then_inc(s_wc, 16)
            for dst, name in ((negpar, "c_negpar"), (reset, "c_reset"), (ident, "c_ident"), (tril, "c_tril"),
                              (sel_f, "c_sel"), (selE_f, "c_selE"), (nw, "nw"), (dskip, "dskip")):
                sp.dma_start(dst[:, :], a[name]).then_inc(s_w, 16)
            sp.dma_start(ones4_f[64:NR, :, :], a["c_ones4"]).then_inc(s_w, 16)
            load_x(Batch(1, 1, 0))
            sp.dma_start(wo_f[:, :, :], a["woT"].rearrange("(g p) d -> p g d", p=P)).then_inc(s_w2, 16)
            sp.dma_start(lnw[:, :], a["lnw"].broadcast_to([P, D])).then_inc(s_w2, 16)
            sp.dma_start(lnb[:, :], a["lnb"].broadcast_to([P, D])).then_inc(s_lnb, 16)
            sp.dma_start(gw[:, :], a["gwT"]).then_inc(s_w2, 16)
            flatten(Batch(0, 0, 0))
            sp.wait_ge(s_su, 5)
            sp.dma_start(gu_f[:, 0:E * I], a["egT"]).then_inc(s_gu, 16)
            sp.dma_start(gu_f[:, E * I:], a["sgT"]).then_inc(s_gu, 16)
            for c, (h0, hn) in enumerate(HC):
                sp.dma_start(wd[0:hn, 0:E, c, :], a["edT"][:, h0:h0 + hn, :].rearrange("e i d -> i e d")).then_inc(s_w2, 16)
                sp.dma_start(wd[0:hn, E, c, :], a["sdT"][h0:h0 + hn, :]).then_inc(s_out if c == len(HC) - 1 else s_w2, 16)
            flatten(Batch(1, 1, 0))
            sp.wait_ge(s_sua, 6)
            sp.wait_ge(s_sup, 1)
            sp.dma_start(gu_f[:, 0:E * I], a["euT"]).then_inc(s_up, 16)
            sp.dma_start(gu_f[:, E * I:], a["suT"]).then_inc(s_up, 16)

            def body(b, nxt, nxt2, prv):
                if nxt2:
                    load_x(nxt2)
                if nxt and not nxt.early:
                    flatten(nxt)

            body(Batch(0, 0, 0), Batch(1, 1, 0), Batch(2, 0, 1), None)
            with sp.Fori(0, 2) as i:
                body(Batch(2 * i + 1, 1, i), Batch(2 * i + 2, 0, i + 1), Batch(2 * i + 3, 1, i + 1), Batch(2 * i, 0, i))
                body(Batch(2 * i + 2, 0, i + 1), Batch(2 * i + 3, 1, i + 1), Batch(2 * i + 4, 0, i + 2), Batch(2 * i + 1, 1, i))
            body(Batch(5, 1, 2), Batch(6, 0, 3), Batch(7, 1, 3), Batch(4, 0, 2))
            body(Batch(6, 0, 3), Batch(7, 1, 3), None, Batch(5, 1, 2))
            with sp.Fori(0, NBLK) as n:
                sp.wait_ge(s_fo, 4 * n + 5)
                sp.dma_start(out[bass.ds(n * BT, BT), :].rearrange("(t p) d -> p t d", p=P), fo[:, :, :]).then_inc(s_out, 16)
            sp.wait_ge(s_out, 16 * (NBLK + 1))

        def schedule(pieces, eng):
            def body(b, nxt, prv):
                pieces(b, nxt, prv)

            b = [Batch(k, k % 2, k // 2) for k in range(NB)]
            body(None, b[0], None)
            body(b[0], b[1], None)
            with eng.Fori(0, NB // 2 - 1) as i:
                k0, k1, k2, k3 = (Batch(2 * i + n, n % 2, i + n // 2) for n in range(4))
                body(k1, k2, k0)
                body(k2, k3, k1)
            body(b[7], None, b[6])

        b7 = Batch(NB - 1, (NB - 1) % 2, (NB - 1) // 2)
        NS = NE * len(HC)
        ps_g, ps_u, ps_e = bank[0:3], (bank[3], bank[6], bank[7]), (bank[5], bank[4])

        @block.tensor
        def _(pe):
            def mm3(dst, hi, lo, rhi, rlo, first, last):
                pe.matmul(dst, hi, rhi, start=first, stop=False)
                pe.matmul(dst, hi, rlo, start=False, stop=False)
                return pe.matmul(dst, lo, rhi, start=False, stop=last)

            def dt_proj(b):
                pe.wait_ge(s_xh, b.k + 1)
                pe.wait_ge(s_xl, b.k + 1)
                if b.first:
                    pe.wait_ge(s_su, 2)
                    pe.wait_ge(s_sua, 2)
                else:
                    pe.wait_ge(s_pad, 4 * b.k)
                    pe.wait_ge(s_xd, 2 * b.k)
                h, l = xTh[b.par][:, K - 1:], xTl[b.par][:, K - 1:]
                mm3(ps_a[0:64, 0:L], w_hi[:, 256:320], w_lo[:, 256:320], h, l, True, True).then_inc(s_dtp, 1)

            def conv(b, dst, chunks):
                for m, ch in enumerate(chunks):
                    o = dst[:, m * L:(m + 1) * L]
                    for t in range(K):
                        c = slice(ch * P, ch * P + P)
                        mm3(o, cv_hi[:, t, c], cv_lo[:, t, c], xTh[b.par][:, t:t + L], xTl[b.par][:, t:t + L], t == 0, False)
                    ins = pe.matmul(o, cb_r[:, ch * P:ch * P + P], ones_r[:, :], start=False, stop=True)
                ins.then_inc(s_xp, 1)

            def x_proj(b):
                if b.first:
                    pe.wait_ge(s_su, 8)
                    pe.wait_ge(s_sua, 4)
                    pe.wait_ge(s_ps, N_PS)
                else:
                    pe.wait_ge(s_pad, 4 * b.k - 2)
                    pe.wait_ge(s_xd, 2 * b.k - 1)
                conv(b, ps_b, (0, 1))

            def bc_proj(b):
                if b.first:
                    pe.wait_ge(s_su, 9)
                    pe.wait_ge(s_sua, 5)
                pe.wait_ge(s_td, b.k + 1)
                conv(b, ps_a, (2, 3))

            def z_proj(b):
                pe.wait_ge(s_sl, 3 * b.k + 1)
                h, l = xTh[b.par][:, K - 1:], xTl[b.par][:, K - 1:]
                for m in range(2):
                    c = slice(m * P, m * P + P)
                    ins = mm3(ps_b[:, m * L:(m + 1) * L], w_hi[:, c], w_lo[:, c], h, l, True, True)
                ins.then_inc(s_xp, 1)

            def turn_dt(b):
                pe.wait_ge(s_sl, 3 * b.k + 2)
                pe.wait_ge(s_d2, b.k + 1)
                pe.wait_ge(s_dg, b.k + 1)
                if b.first:
                    pe.wait_ge(s_w, 16 * N_W)
                pe.matmul(ps_a[:, 0:64], dd2[:, 0, :, :].rearrange("h a q -> h (a q)"), ident[0:64, 0:64], start=True, stop=True)
                for c in range(1, NC):
                    pe.transpose(ps_a[:, c * 64:c * 64 + 64], dd2[:, c, :, :].rearrange("h a q -> h (a q)"), ident[0:64, 0:64])
                pe.matmul(ps_a[:, 256:320], ones32[:, :], ddiag[:, :, :], start=True, stop=True).then_inc(s_ddp, 1)

            def turn_b(b):
                pe.wait_ge(s_sl, 3 * b.k + 3)
                pe.matmul(ps_b[0:Q, 0:P], bc[b.par][:, 0, 0:Q], ident[:, :], start=True, stop=True)
                for c in range(1, 3):
                    ins = pe.transpose(ps_b[0:Q, c * P:c * P + P], bc[b.par][:, 0, c * Q:c * Q + Q], ident[:, :])
                ins.then_inc(s_btp, 1)

            def spread_exp(b):
                pe.wait_ge(s_ddt, b.k + 1)
                pe.wait_ge(s_eh, b.k + 1)
                pe.wait_ge(s_el, b.k + 1)
                if b.first:
                    pe.wait_ge(s_sr, 5)
                for m in range(2):
                    ins = pe.matmul(ps_a[:, m * L:(m + 1) * L], selE[:, m * P:(m + 1) * P], e_hl[:, :], start=True, stop=True)
                ins.then_inc(s_ebp, 1)

            def turn_x(b):
                pe.wait_ge(s_bt, b.k + 1)
                pe.wait_ge(s_x2, 2 * (b.k + 1))
                for c in range(NC):
                    dst = ps_b if c < 2 else ps_a
                    if c == 2:
                        pe.wait_ge(s_eb, b.k + 1)
                    for m in range(2):
                        ins = pe.transpose(dst[:, (c % 2) * DI + m * P:(c % 2) * DI + (m + 1) * P],
                                           xs2[:, m, c, :, :].rearrange("h a q -> h (a q)"), ident[:, :])
                    if c % 2:
                        ins.then_inc(s_xtp, 1)

            def g_of(b):
                pe.wait_ge(s_b2, b.k + 1)
                for c in range(NC):
                    ins = pe.matmul(ps_gl[:, c * Q:c * Q + Q], b2[:, c, :, :].rearrange("h a q -> h (a q)"),
                                    bc[b.par][:, 1, c * Q:c * Q + Q], start=True, stop=True)
                ins.then_inc(s_g, 1)

            def seg(b, n):
                if n == 0:
                    pe.wait_ge(s_fl[b.par], 64 * (b.half + 1))
                    pe.wait_ge(s_ng, b.k + 1)
                if not (b.first and n < 2):
                    pe.wait_ge(s_e, 8 * b.k + n - 1)
                c, hf = n // 2, n % 2
                pe.matmul(ps_seg[hf][:, :], neg[b.par][:, c, :, :], mov[b.par][:, hf * 512:hf * 512 + 512],
                          start=True, stop=True).then_inc(s_sg, 1)

            def y_in(b, n):
                if n == 0:
                    pe.wait_ge(s_pad, 4 * (b.k + 1))
                    if not b.first:
                        pe.wait_ge(s_y, 5 * b.k)
                pe.wait_ge(s_m, 8 * b.k + n + 1)
                c, hf = n // 2, n % 2
                for i in range(2):
                    for j in range(4):
                        ins = pe.matmul(ps_y[32 * j:32 * j + 32, hf * L + c * Q:hf * L + c * Q + Q],
                                        xpad[:, c, (hf * 4 + j) * 96 + i * 32:(hf * 4 + j) * 96 + i * 32 + 32],
                                        mm[:, n % 2, (2 * j + i) * Q:(2 * j + i) * Q + Q], start=(i == 0), stop=(i == 1))
                ins.then_inc(s_yd, 1)

            def state(b, c):
                if c == 0:
                    pe.wait_ge(s_xd, 2 * (b.k + 1))
                    pe.wait_ge(s_bt, b.k + 1)
                    if not b.first:
                        pe.wait_ge(s_ln, 11 * b.k - 3)
                else:
                    pe.wait_ge(s_s, 3 * b.k + c)
                pe.matmul(ps_so[:, 0:DI], btok[:, c, :], xdd[:, c, :], start=True, stop=True).then_inc(s_st, 1)

            def y_out(b):
                for c in range(1, NC):
                    pe.wait_ge(s_s, 3 * b.k + c)
                    for m in range(2):
                        ins = pe.matmul(ps_yo[:, m * L + c * Q:m * L + c * Q + Q], st[:, c - 1, m * P:(m + 1) * P],
                                        bc[b.par][:, 1, c * Q:c * Q + Q], start=True, stop=True)
                ins.then_inc(s_yo, 1)

            def project(b):
                pe.wait_ge(s_sq, b.k + 1)
                pe.wait_ge(s_y, 5 * (b.k + 1))
                pe.wait_ge(s_s, 3 * (b.k + 1))
                for t in range(NT):
                    for m in range(2):
                        pe.matmul(ps_so[:, t * D:(t + 1) * D], yf[:, m, t * P:(t + 1) * P], wo[:, m, :], start=(m == 0), stop=(m == 1))
                for t in range(NT):
                    for m in range(2):
                        ins = pe.matmul(ps_so[:, 256 + t:257 + t], ysq[:, m, t * P:(t + 1) * P], ones[:, 0:1], start=(m == 0), stop=(m == 1))
                ins.then_inc(s_op, 1)

            def turn_x1(b):
                pe.wait_ge(s_x1, 2 * (b.k + 1))
                if b.k is not None and not (isinstance(b.k, int) and b.k == 7):
                    pe.wait_ge(s_gm, b.k + 2)
                for t in range(NT):
                    ins = pe.transpose(ps_gl[:, t * P:(t + 1) * P], x1c[:, b.par, t, :], ident[:, :])
                ins.then_inc(s_x1p, 1)

            def logits(b):
                pe.wait_ge(s_x1f, 2 * (b.k + 1))
                for t in range(NT):
                    ins = pe.matmul(ps_gl[:, 256 + t * E:256 + (t + 1) * E], x1Tf[:, t * P:(t + 1) * P], gw[:, :], start=True, stop=True)
                ins.then_inc(s_lp, 1)

            def pieces(b, nxt, prv):
                if b:
                    g_of(b)
                    seg(b, 0)
                    seg(b, 1)
                if prv:
                    project(prv)
                if nxt:
                    dt_proj(nxt)
                    x_proj(nxt)
                if b:
                    y_in(b, 0)
                    seg(b, 2)
                    y_in(b, 1)
                    seg(b, 3)
                if nxt:
                    bc_proj(nxt)
                if b:
                    y_in(b, 2)
                    seg(b, 4)
                    state(b, 0)
                    y_in(b, 3)
                    seg(b, 5)
                if nxt:
                    z_proj(nxt)
                if prv:
                    turn_x1(prv)
                if b:
                    state(b, 1)
                    y_in(b, 4)
                    seg(b, 6)
                    y_in(b, 5)
                    seg(b, 7)
                    state(b, 2)
                if prv:
                    logits(prv)
                if nxt:
                    turn_dt(nxt)
                    turn_b(nxt)
                if b:
                    y_in(b, 6)
                    y_in(b, 7)
                    y_out(b)
                if nxt:
                    spread_exp(nxt)
                    turn_x(nxt)

            pe.wait_ge(s_su, 1)
            schedule(pieces, pe)

            steps = [(e, c) for e in ([E] + list(range(E))) for c in range(len(HC))]

            def up(n, s):
                e, c = steps[s]
                h0, hn = HC[c]
                w = slice(e * I + h0, e * I + h0 + hn)
                xh, xl = x1h[:, bass.ds(n * BT, BT)], x1l[:, bass.ds(n * BT, BT)]
                g, u = ps_g[s % 3], ps_u[s % 3]
                if s >= 3 or not isinstance(n, int):
                    pe.wait_ge(s_h, n * NS + s - 2)
                mm3(g[0:hn, :], g_hi[:, w], g_lo[:, w], xh, xl, True, True).then_inc(s_gp, 1)
                mm3(u[0:hn, :], u_hi[:, w], u_lo[:, w], xh, xl, True, True).then_inc(s_uo, 1)

            def down(n, s):
                e, c = steps[s]
                hn = HC[c][1]
                o = s // len(HC)
                pe.wait_ge(s_h, n * NS + s + 1)
                if c == 0:
                    pe.wait_ge(s_ac, n * 17 + 1 + (1 + 4 * (o - 2) if o >= 2 else 0))
                    if o == 1:
                        pe.wait_ge(s_lg, NB)
                for t in range(4):
                    ins = pe.matmul(ps_e[o % 2][:, t * D:(t + 1) * D], hh[0:hn, s % 3, t * P:(t + 1) * P], wd[0:hn, e, c, :],
                                    start=(c == 0 and t == 0), stop=(c == len(HC) - 1), skip_group_check=True)
                ins.then_inc(s_dn, 1)

            def ffn(n, more):
                for s in range(NS):
                    down(n, s)
                    if s + 3 < NS:
                        up(n, s + 3)
                    elif more:
                        if s + 3 == NS:
                            pe.wait_ge(s_x1l, NB)
                        up(n + 1, s + 3 - NS)

            project(b7)
            pe.wait_ge(s_sua, 7)
            pe.wait_ge(s_sup, 2)
            pe.wait_ge(s_x1l, 2)
            for s in range(3):
                up(0, s)
            turn_x1(b7)
            logits(b7)
            with pe.Fori(0, NBLK - 1) as n:
                ffn(n, True)
            ffn(NBLK - 1, False)

        @block.scalar
        def _(act):
            for r in range(2):
                act.dma_start(alog[32 * r:32 * r + 32, :], a["alog"]).then_inc(s_ws, 16)
                act.dma_start(dtb[32 * r:32 * r + 32, :], a["dtb"]).then_inc(s_ws, 16)
                act.dma_start(cw_b[:, :, 256 * r:256 * r + 256], a["cwT"][:, 256 * r:256 * r + 256].rearrange("(o k) c -> o k c", o=1).broadcast_to([P, K, 256])).then_inc(s_wc, 16)
            for r in range(2):
                act.dma_start(yo[r:r + 1, :, :].rearrange("r m l -> r (m l)"), a["cb"]).then_inc(s_ws, 16)
            act.dma_start(hilo[:, :], a["c_hilo"]).then_inc(s_ws, 16)
            act.wait_ge(s_ws, 16 * 7)
            act.activation(aexp[:, :], alog[:, :], ACT.Exp).then_inc(s_sua, 1)
            act.wait_ge(s_su, 1)
            act.activation(w_hi[:, :], w_cv[:, :], ACT.Copy).then_inc(s_sua, 1)
            act.activation(cb_s[:, :], cb_f, ACT.Copy, scale=0.5).then_inc(s_sua, 1)

            def setup_conv():
                for m in range(2):
                    act.wait_ge(s_su, 4 + m)
                    act.activation(cv_hi[:, :, m * 256:m * 256 + 256], cw_b[:, :, m * 256:m * 256 + 256], ACT.Copy).then_inc(s_sua, 1)

            def setup_rows():
                act.wait_ge(s_w, 16 * N_W)
                for p in range(2):
                    act.activation(neg[p][64:NR, :, :, :].rearrange("r c h q -> r (c h q)"), ones4_f[64:NR, :, :].rearrange("r c n -> r (c n)"),
                                   ACT.Copy).then_inc(s_sr, 1)
                    act.activation(mov[p][0:64, :], sel_f, ACT.Copy).then_inc(s_sr, 1)
                act.activation(selE[:, :], selE_f, ACT.Copy).then_inc(s_sr, 1)

            def x_high(b):
                act.wait_ge(s_xin[b.par], 32 * (b.half + 1))
                if not b.early:
                    act.wait_ge(s_xp, 3 * (b.k - 1))
                act.activation(xTh[b.par][:, K - 1:], xTf[:, b.par, :], ACT.Copy).then_inc(s_xh, 1)

            def dt_tanh(b):
                act.wait_ge(s_dtp, b.k + 1)
                if b.first:
                    act.wait_ge(s_su, 3)
                else:
                    act.wait_ge(s_dt, 3 * b.k - 2)
                act.activation(tdt[:, :], ps_a[0:64, 0:L], ACT.Tanh, bias=dtb_h[:, 0:1], scale=0.5).then_inc(s_td, 1)

            def silu_tanh(b, n, src):
                act.wait_ge(s_xp, 3 * b.k + n + 1)
                if not b.first:
                    act.wait_ge(s_sl, 3 * (b.k - 1) + n + 1)
                act.activation(th[:, n, :], src[:, :], ACT.Tanh).then_inc(s_th, 1)

            def exps(b):
                act.wait_ge(s_dt, 3 * (b.k + 1))
                if not b.first:
                    act.wait_ge(s_el, b.k)
                    act.wait_ge(s_dg, b.k)
                act.activation(eT[:, :], acum[:, :], ACT.Exp).then_inc(s_et, 1)
                act.wait_ge(s_df, b.k + 1)
                if not b.first:
                    act.wait_ge(s_dd, b.k)
                act.activation(adif[:, :], adif[:, :], ACT.Exp).then_inc(s_dc, 1)

            def double(b, part):
                if part == "x":
                    act.wait_ge(s_sl, 3 * b.k + 1)
                    if not b.first:
                        act.wait_ge(s_xtp, 2 * b.k)
                    for m in range(2):
                        act.activation(xs2[:, m, :, :, :], view(xs[b.par], 0, P, m * L, [[Q, NC], [0, 2], [1, Q]]), ACT.Copy).then_inc(s_x2, 1)
                elif part == "b":
                    act.wait_ge(s_sl, 3 * b.k + 2)
                    if not b.first:
                        act.wait_ge(s_g, b.k)
                    act.activation(b2[:, :, :, :], view(bc[b.par], 0, P, 0, [[Q, NC], [0, 2], [1, Q]]), ACT.Copy).then_inc(s_b2, 1)
                else:
                    act.wait_ge(s_dd, b.k + 1)
                    if not b.first:
                        act.wait_ge(s_ddp, b.k)
                    act.activation(dd2[:, :, :, :], view(dd, 0, 64, 0, [[Q, NC], [0, 2], [1, Q]]), ACT.Copy).then_inc(s_d2, 1)

            def copies(b):
                act.wait_ge(s_ddp, b.k + 1)
                if not b.first:
                    act.wait_ge(s_s, 3 * b.k)
                act.activation(ddt[:, :], ps_a[:, 0:320], ACT.Copy).then_inc(s_ddt, 1)
                act.wait_ge(s_btp, b.k + 1)
                if not b.first:
                    act.wait_ge(s_st, 3 * b.k)
                act.activation(btok[:, :, :], ps_b[0:Q, 0:384], ACT.Copy).then_inc(s_bt, 1)
                act.wait_ge(s_ebp, b.k + 1)
                if not b.early:
                    act.wait_ge(s_y, 5 * (b.k - 1))
                act.activation(eb[b.par][:, :, :], ps_a[:, :], ACT.Copy).then_inc(s_eb, 1)

            def decays(b, n):
                act.wait_ge(s_sg, 8 * b.k + n + 1)
                if not (b.first and n < 2):
                    act.wait_ge(s_m, 8 * b.k + n - 1)
                act.activation(ee[:, n % 2, :], ps_seg[n % 2][:, :], ACT.Exp).then_inc(s_e, 1)

            def y_square(b):
                act.wait_ge(s_y, 5 * (b.k + 1))
                if not b.first:
                    act.wait_ge(s_op, b.k)
                act.activation(ysq[:, :, :], yf[:, :, :], ACT.Square).then_inc(s_sq, 1)

            def x1_turned(b):
                act.wait_ge(s_x1p, b.k + 1)
                act.activation(x1Tf[:, :], ps_gl[:, 0:L], ACT.Copy).then_inc(s_x1f, 1)
                act.activation(x1h[:, bass.ds(b.k * L, L)], ps_gl[:, 0:L], ACT.Copy).then_inc(s_x1f, 1)

            def keep_logits(b):
                act.wait_ge(s_lp, b.k + 1)
                act.activation(lg[:, bass.ds(b.k * NT, NT), :], ps_gl[:, 256:256 + NT * E], ACT.Copy).then_inc(s_lg, 1)

            def pieces(b, nxt, prv):
                if nxt:
                    x_high(nxt)
                    if nxt.first:
                        setup_conv()
                if b:
                    decays(b, 0)
                    decays(b, 1)
                if nxt:
                    dt_tanh(nxt)
                    if nxt.first:
                        setup_rows()
                if b:
                    decays(b, 2)
                if nxt:
                    silu_tanh(nxt, 0, ps_b)
                if b:
                    decays(b, 3)
                if nxt:
                    exps(nxt)
                    silu_tanh(nxt, 1, ps_a)
                    double(nxt, "x")
                if b:
                    decays(b, 4)
                    decays(b, 5)
                if nxt:
                    silu_tanh(nxt, 2, ps_b)
                    double(nxt, "b")
                    double(nxt, "dt")
                if prv:
                    x1_turned(prv)
                if b:
                    decays(b, 6)
                    decays(b, 7)
                if prv:
                    keep_logits(prv)
                if nxt:
                    copies(nxt)
                if b:
                    y_square(b)

            def once():
                act.wait_ge(s_gu, 32)
                act.activation(g_hi[:, :], gu_f[:, :], ACT.Copy).then_inc(s_sua, 1)

            b = [Batch(k, k % 2, k // 2) for k in range(NB)]
            pieces(None, b[0], None)
            once()
            pieces(b[0], b[1], None)
            act.wait_ge(s_up, 32)
            act.activation(u_hi[:, :], gu_f[:, :], ACT.Copy).then_inc(s_sua, 1)
            with act.Fori(0, NB // 2 - 1) as i:
                k0, k1, k2, k3 = (Batch(2 * i + n, n % 2, i + n // 2) for n in range(4))
                pieces(k1, k2, k0)
                pieces(k2, k3, k1)
            pieces(b[7], None, b[6])

            def silu_gate(n, s):
                hn = HC[s % 3][1]
                act.wait_ge(s_gp, n * NS + s + 1)
                if s >= 3 or not isinstance(n, int):
                    act.wait_ge(s_h, n * NS + s - 2)
                act.activation(sg[0:hn, s % 3, :], ps_g[s % 3][0:hn, :], ACT.Silu).then_inc(s_si, 1)

            def ffn(n, more):
                for s in range(3, NS + 3 if more else NS):
                    silu_gate(n + s // NS, s % NS)

            silu_gate(0, 0)
            silu_gate(0, 1)
            x1_turned(b7)
            silu_gate(0, 2)
            keep_logits(b7)
            act.wait_ge(s_cb, 2)
            act.activation(cex[:, :, :], cpr[:, :, :], ACT.Exp).then_inc(s_sua, 1)

            with act.Fori(0, NBLK - 1) as n:
                ffn(n, True)
            ffn(NBLK - 1, False)

        @block.vector
        def _(dve):
            dve.wait_ge(s_wi, 16 * 3)
            dve.tensor_scalar(w_cv[:, 256:320], w_raw[:, 768:832], 1.0, None, ALU.mult)
            dve.tensor_scalar(w_cv[:, 0:256], w_raw[:, 0:256], 0.5, None, ALU.mult).then_inc(s_su, 1)
            dve.wait_ge(s_sua, 2)
            dve.tensor_tensor(w_lo[:, :], w_cv[:, :], w_hi[:, :].bitcast(F32), ALU.subtract).then_inc(s_su, 1)
            dve.wait_ge(s_ws, 16 * 7)
            dve.tensor_scalar(dtb_h[:, :], dtb[:, :], 0.5, None, ALU.mult)
            dve.tensor_scalar(aneg[:, :], aexp[:, :], -1.0, None, ALU.mult).then_inc(s_su, 1)
            dve.wait_ge(s_wc, 16 * 3)
            for m in range(2):
                dve.scalar_tensor_tensor(out=cw_b[:, :, m * 256:m * 256 + 256], in0=cw_b[:, :, m * 256:m * 256 + 256], scalar=0.5,
                                         in1=view(x1, 0, P, 256 + m * 256, [[0, K], [1, 256]]), op0=ALU.mult, op1=ALU.mult).then_inc(s_su, 1)
            dve.tensor_scalar(cb_h, cb_f, hilo[:, 1:2], 0.5, ALU.mult, ALU.mult).then_inc(s_su, 1)
            dve.wait_ge(s_sua, 4)
            dve.tensor_tensor(cv_lo[:, :, 0:256], cw_b[:, :, 0:256], cv_hi[:, :, 0:256].bitcast(F32), ALU.subtract).then_inc(s_su, 1)
            dve.wait_ge(s_su, 6)
            dve.scalar_tensor_tensor(out=cb_r[:, :], in0=cb_s[:, :].bitcast(F32), scalar=hilo[:, 0:1], in1=cb_h, op0=ALU.mult, op1=ALU.add).then_inc(s_su, 1)
            dve.wait_ge(s_sua, 5)
            dve.tensor_tensor(cv_lo[:, :, 256:512], cw_b[:, :, 256:512], cv_hi[:, :, 256:512].bitcast(F32), ALU.subtract).then_inc(s_su, 1)

            def dt_chain(b):
                dve.wait_ge(s_td, b.k + 1)
                if not b.first:
                    dve.wait_ge(s_ddp, b.k)
                dve.tensor_scalar(dd[:, :], tdt[:, :], (DT_MAX - DT_MIN) / 2, (DT_MAX + DT_MIN) / 2, ALU.mult, ALU.add).then_inc(s_dt, 1)
                dve.wait_ge(s_dt, 3 * b.k + 1)
                dve.tensor_scalar(dA[:, :], dd[:, :], aneg[:, 0:1], None, ALU.mult).then_inc(s_dt, 1)
                dve.wait_ge(s_dt, 3 * b.k + 2)
                if not b.first:
                    dve.wait_ge(s_al, b.k)
                    dve.wait_ge(s_df, b.k)
                    dve.wait_ge(s_et, b.k)
                if b.first:
                    dve.wait_ge(s_w, 16 * N_W)
                dve.tensor_tensor_scan(acum[:, :], reset[:, :], dA[:, :], 0.0, ALU.mult, ALU.add).then_inc(s_dt, 1)

            def silu(b, n, src, dst):
                dve.wait_ge(s_th, 3 * b.k + n + 1)
                if not b.early:
                    if n == 0:
                        dve.wait_ge(s_xtp, 2 * (b.k - 1))
                    if n == 1:
                        dve.wait_ge(s_yo, b.k - 1)
                        dve.wait_ge(s_btp, b.k - 1)
                    dve.wait_ge(s_y, 5 * (b.k - 1))
                dve.scalar_tensor_tensor(out=dst[b.par][:, :, :].rearrange("p a l -> p (a l)"), in0=th[:, n, :], scalar=1.0,
                                         in1=src[:, :], op0=ALU.add, op1=ALU.mult).then_inc(s_sl, 1)

            def pad_x(b, g):
                src = ps_b if g == 0 else ps_a
                dve.wait_ge(s_xtp, 2 * b.k + g + 1)
                if g == 0:
                    dve.wait_ge(s_ddt, b.k + 1)
                    if b.first:
                        dve.wait_ge(s_pz, 1)
                    else:
                        dve.wait_ge(s_yd, 8 * b.k)
                        dve.wait_ge(s_st, 3 * b.k)
                for h2 in range(2):
                    dve.tensor_tensor(view(xpad, 64 * h2, 64, 2 * g * PADW + 8 * h2, [[PADW, 2], [48, NP], [1, HD]]),
                                      view(src, 64 * h2, 64, 8 * h2, [[DI, 2], [16, NP], [1, HD]]),
                                      view(ddt, 64 * h2, 64, 2 * g * 64 + h2, [[64, 2], [2, NP], [0, HD]]),
                                      ALU.mult).then_inc(s_pad, 1)
                n = 2 if g == 0 else 1
                dve.tensor_tensor(view(xdd, 0, 64, 2 * g * DI, [[DI, n], [HD, NH], [1, HD]]),
                                  view(src, 0, 64, 0, [[DI, n], [HD, NH], [1, HD]]),
                                  view(ddt, 0, 64, 2 * g * 64 + 32, [[64, n], [1, NH], [0, HD]]),
                                  ALU.mult).then_inc(s_xd, 1)

            def g_mask(b):
                dve.wait_ge(s_g, b.k + 1)
                if not b.first:
                    dve.wait_ge(s_m, 8 * b.k)
                dve.tensor_tensor(gm[:, :, :], view(ps_gl, 0, P, 0, [[Q, NC], [1, Q]]), view(tril, 0, P, 0, [[0, NC], [1, Q]]),
                                  ALU.mult).then_inc(s_gm, 1)

            def m_of(b, n):
                if n == 0:
                    dve.wait_ge(s_gm, b.k + 1)
                dve.wait_ge(s_e, 8 * b.k + n + 1)
                if not (b.first and n < 2):
                    dve.wait_ge(s_yd, 8 * b.k + n - 1)
                c = n // 2
                dve.scalar_tensor_tensor(out=view(mm, 0, P, (n % 2) * 512, [[Q, 8], [1, Q]]), in0=view(ee, 0, P, (n % 2) * 512, [[Q, 8], [1, Q]]),
                                         scalar=1.0, in1=view(gm, 0, P, c * Q, [[0, 8], [1, Q]]), op0=ALU.min, op1=ALU.mult).then_inc(s_m, 1)

            def state(b, c):
                dve.wait_ge(s_st, 3 * b.k + c + 1)
                if c == 0:
                    if not b.first:
                        dve.wait_ge(s_yo, b.k)
                    dve.tensor_copy(st[:, 0, :], ps_so[:, 0:DI]).then_inc(s_s, 1)
                    return
                dve.wait_ge(s_s, 3 * b.k + c)
                dve.tensor_tensor(view(stm, 0, P, 0, [[HD, NH], [1, HD]]), view(st, 0, P, (c - 1) * DI, [[HD, NH], [1, HD]]),
                                  view(ddt, 0, P, 256 + (c - 1) * 32, [[1, NH], [0, HD]]), ALU.mult).then_inc(s_sm, 1)
                dve.wait_ge(s_sm, 2 * b.k + c)
                dve.tensor_tensor(st[:, c, :], stm[:, :], ps_so[:, 0:DI], ALU.add).then_inc(s_s, 1)

            def y_of(b):
                dve.wait_ge(s_yd, 8 * (b.k + 1))
                for m in range(2):
                    dve.scalar_tensor_tensor(out=yv[:, m, :], in0=xs[b.par][:, m, :], scalar=dskip[:, m:m + 1], in1=ps_y[:, m * L:(m + 1) * L],
                                             op0=ALU.mult, op1=ALU.add).then_inc(s_y, 1)
                dve.wait_ge(s_yo, b.k + 1)
                dve.wait_ge(s_eb, b.k + 1)
                dve.tensor_tensor(yo[:, :, Q:], view(ps_yo, 0, P, Q, [[L, 2], [1, L - Q]]), eb[b.par][:, :, Q:], ALU.mult).then_inc(s_y, 1)
                dve.wait_ge(s_y, 5 * b.k + 3)
                dve.tensor_tensor(yv[:, :, Q:], yv[:, :, Q:], yo[:, :, Q:], ALU.add).then_inc(s_y, 1)
                dve.wait_ge(s_y, 5 * b.k + 4)
                if not b.first:
                    dve.wait_ge(s_op, b.k)
                    dve.wait_ge(s_sq, b.k)
                dve.tensor_tensor(yf[:, :, :], yv[:, :, :], sz[b.par][:, :, :], ALU.mult).then_inc(s_y, 1)

            def norm_a(b):
                dve.wait_ge(s_op, b.k + 1)
                for t in range(NT):
                    dve.bn_stats(bn[:, t, :], ps_so[:, t * D:(t + 1) * D]).then_inc(s_ln, 1)
                dve.wait_ge(s_ln, 11 * b.k + 2)
                dve.tensor_scalar(m1[:, :], ps_so[:, 256:256 + NT], EPS / DI, EPS * EPS, ALU.mult, ALU.add).then_inc(s_ln, 1)
                for t in range(NT):
                    dve.bn_aggr(mv[:, t, :], bn[:, t, :]).then_inc(s_ln, 1)
                dve.wait_ge(s_ln, 11 * b.k + 5)
                dve.tensor_tensor(w1[:, :], mv[:, :, 1], m1[:, :], ALU.add).then_inc(s_ln, 1)

            def norm_b(b):
                dve.wait_ge(s_pw, 2 * b.k + 1)
                for t in range(NT):
                    dve.tensor_scalar(an[:, t, :], ps_so[:, t * D:(t + 1) * D], mv[:, t, 0:1], s1[:, t:t + 1], ALU.subtract, ALU.mult).then_inc(s_ln, 1)
                dve.wait_ge(s_ln, 11 * b.k + 8)
                dve.tensor_tensor(an[:, :, :], an[:, :, :], view(lnw, 0, P, 0, [[0, NT], [1, D]]), ALU.mult).then_inc(s_ln, 1)
                dve.wait_ge(s_ln, 11 * b.k + 9)
                dve.wait_ge(s_xx, b.k + 1)
                dve.tensor_tensor(rr[:, :, :], an[:, :, :], xx[:, b.par, :, :], ALU.add).then_inc(s_ln, 1)

            def norm_c(b):
                dve.wait_ge(s_ln, 11 * b.k + 10)
                for t in range(NT):
                    dve.bn_stats(bn2[:, t, :], rr[:, t, :]).then_inc(s_f2, 1)
                dve.wait_ge(s_f2, 5 * b.k + 2)
                dve.memset(pause[:, :], 0.0)
                for t in range(NT):
                    dve.bn_aggr(mv2[:, t, :], bn2[:, t, :]).then_inc(s_f2, 1)
                dve.wait_ge(s_f2, 5 * b.k + 4)
                dve.tensor_scalar(w2[:, :], mv2[:, :, 1], EPS, None, ALU.add).then_inc(s_f2, 1)

            def norm_d(b):
                dve.wait_ge(s_pw, 2 * b.k + 2)
                for t in range(NT):
                    dve.tensor_scalar(x1c[:, b.par, t, :], rr[:, t, :], mv2[:, t, 0:1], s2[:, t:t + 1], ALU.subtract, ALU.mult).then_inc(s_x1, 1)
                dve.memset(m1[:, 0:1], 0.0).then_inc(s_ln, 1)

            def pieces(b, nxt, prv):
                if b:
                    g_mask(b)
                    m_of(b, 0)
                if prv:
                    norm_a(prv)
                if b:
                    m_of(b, 1)
                if nxt:
                    dt_chain(nxt)
                if prv:
                    norm_b(prv)
                if b:
                    m_of(b, 2)
                if nxt:
                    silu(nxt, 0, ps_b, xs)
                if prv:
                    norm_c(prv)
                if b:
                    m_of(b, 3)
                    state(b, 0)
                if prv:
                    norm_d(prv)
                if nxt:
                    silu(nxt, 1, ps_a, bc)
                if b:
                    m_of(b, 4)
                    state(b, 1)
                    m_of(b, 5)
                if nxt:
                    silu(nxt, 2, ps_b, sz)
                if b:
                    m_of(b, 6)
                    state(b, 2)
                    m_of(b, 7)
                    y_of(b)
                if nxt:
                    pad_x(nxt, 0)
                    pad_x(nxt, 1)

            schedule(pieces, dve)

            def hidden(n, s):
                hn = HC[s % 3][1]
                dve.wait_ge(s_si, n * NS + s + 1)
                dve.wait_ge(s_uo, n * NS + s + 1)
                if s >= 3 or not isinstance(n, int):
                    dve.wait_ge(s_dn, n * NS + s - 2)
                dve.tensor_tensor(hh[0:hn, s % 3, :], sg[0:hn, s % 3, :], ps_u[s % 3][0:hn, :], ALU.mult).then_inc(s_h, 1)

            def gate():
                steps = 0

                def did(ins):
                    nonlocal steps
                    steps += 1
                    ins.then_inc(s_cb, 1)
                    dve.wait_ge(s_cb, steps)

                def over_e(t):
                    return view(t, 0, P, 0, [[1, NTT], [0, E]])

                dve.wait_ge(s_lg, NB)
                did(dve.tensor_reduce(cmx[:, :], lg[:, :, :], mybir.AxisListType.X, ALU.max))
                did(dve.tensor_tensor(cpr[:, :, :], lg[:, :, :], over_e(cmx), ALU.subtract))
                dve.wait_ge(s_sua, 8)
                did(dve.tensor_reduce(csm[:, :], cex[:, :, :], mybir.AxisListType.X, ALU.add))
                did(dve.reciprocal(crc[:, :], csm[:, :]))
                did(dve.tensor_tensor(cpr[:, :, :], cex[:, :, :], over_e(crc), ALU.mult))
                for e in range(E):
                    for f0, f1, op in ((0, e, ALU.is_ge), (e, E, ALU.is_gt)):
                        if f1 > f0:
                            ins = dve.tensor_tensor(cge[:, :, e, f0:f1], cpr[:, :, f0:f1], view(cpr, 0, P, e, [[E, NTT], [0, f1 - f0]]), op)
                did(ins)
                did(dve.tensor_reduce(crk[:, :, :], cge[:, :, :, :], mybir.AxisListType.X, ALU.add))
                did(dve.scalar_tensor_tensor(out=csl[:, :, :], in0=crk[:, :, :], scalar=1.5, in1=cpr[:, :, :], op0=ALU.is_lt, op1=ALU.mult))
                did(dve.tensor_reduce(cts[:, :], csl[:, :, :], mybir.AxisListType.X, ALU.add))
                did(dve.tensor_scalar(csm[:, :], cts[:, :], 1e-20, None, ALU.add))
                did(dve.reciprocal(crc[:, :], csm[:, :]))
                did(dve.tensor_tensor(comb[:, :, :], csl[:, :, :], over_e(crc), ALU.mult))

            def add_expert(n, o):
                dve.wait_ge(s_dn, n * NS + 3 * o + 3)
                ps = ps_e[o % 2]
                if o == 0:
                    dve.wait_ge(s_fo, 4 * n + 1)
                    dve.tensor_tensor(yv[:, :, :].rearrange("p a l -> p (a l)"), ps[:, :],
                                      x1[:, bass.ds(n * 4, 4), :].rearrange("p t d -> p (t d)"), ALU.add).then_inc(s_ac, 1)
                    return
                dve.wait_ge(s_ac, 17 * n + 2 + 4 * (o - 1))
                for t in range(4):
                    dve.scalar_tensor_tensor(out=acc[:, t, :], in0=ps[:, t * D:(t + 1) * D], scalar=comb[:, bass.ds(n * 4 + t, 1), o - 1],
                                             in1=acc[:, t, :], op0=ALU.mult, op1=ALU.add).then_inc(s_ac, 1)

            def final_norm(n):
                dve.wait_ge(s_ac, 17 * n + 18)
                for t in range(4):
                    dve.bn_stats(fbn[:, t, :], acc[:, t, :]).then_inc(s_f2, 1)
                dve.wait_ge(s_f2, 5 * NB + 9 * n + 4)
                dve.memset(pause[:, :], 0.0)
                for t in range(4):
                    dve.bn_aggr(fmv[:, t, :], fbn[:, t, :]).then_inc(s_f2, 1)
                dve.wait_ge(s_f2, 5 * NB + 9 * n + 8)
                dve.tensor_scalar(fw[:, :], fmv[:, :, 1], EPS, None, ALU.add).then_inc(s_f2, 1)
                dve.wait_ge(s_fp, n + 1)
                dve.wait_ge(s_out, 16 * (n + 1))
                for t in range(4):
                    dve.tensor_scalar(fo[:, t, :], acc[:, t, :], fmv[:, t, 0:1], fs[:, t:t + 1], ALU.subtract, ALU.mult).then_inc(s_fo, 1)

            def ffn(n, more):
                for s in range(NS):
                    if s % 3 == 2:
                        add_expert(n, s // 3)
                    if s + 3 < NS:
                        hidden(n, s + 3)
                    elif more:
                        hidden(n + 1, s + 3 - NS)
                final_norm(n)

            norm_a(b7)
            norm_b(b7)
            norm_c(b7)
            hidden(0, 0)
            norm_d(b7)
            dve.memset(cts[:, 0:1], 0.0).then_inc(s_ac, 1)
            dve.memset(cts[:, 1:2], 0.0).then_inc(s_fo, 1)
            hidden(0, 1)
            hidden(0, 2)
            gate()
            dve.wait_ge(s_kp, NB)
            with dve.Fori(0, NBLK - 1) as n:
                ffn(n, True)
            ffn(NBLK - 1, False)

        @block.gpsimd
        def _(pool):
            steps = 0

            def step(ins):
                nonlocal steps
                steps += 1
                ins.then_inc(s_ps, 1)
                pool.wait_ge(s_ps, steps)

            for p in range(2):
                pool.memset(xTh[p][:, 0:K - 1].bitcast(F32), 0.0)
                pool.memset(xTl[p][:, 0:K - 1].bitcast(F32), 0.0)
            pool.memset(ones[:, :], 1.0)
            pool.memset(mhalf[:, :], -0.5)
            step(pool.memset(pause[:, :], 0.0))
            step(pool.memset(ones_r[:, :].bitcast(F32), 1.0))
            step(pool.memset(ones32[:, :], 1.0))
            pool.memset(xpad[:, :, :], 0.0).then_inc(s_pz, 1)

            def x_low(b):
                pool.wait_ge(s_xh, b.k + 1)
                if not b.early:
                    pool.wait_ge(s_xp, 3 * (b.k - 1))
                pool.tensor_tensor(xTl[b.par][:, K - 1:], xTf[:, b.par, :], xTh[b.par][:, K - 1:].bitcast(F32), ALU.subtract).then_inc(s_xl, 1)

            def sums(b):
                pool.wait_ge(s_dt, 3 * (b.k + 1))
                if not b.first:
                    pool.wait_ge(s_fw, 16 * b.k)
                pool.tensor_tensor(view(adif, 0, 64, 0, [[Q, NC], [1, Q]]), view(acum, 0, 64, Q - 1, [[Q, NC], [0, Q]]),
                                   view(acum, 0, 64, 0, [[Q, NC], [1, Q]]), ALU.subtract).then_inc(s_df, 1)
                pool.tensor_copy(a_hl[:, :], acum[:, :]).then_inc(s_ah, 1)
                pool.wait_ge(s_ah, b.k + 1)
                pool.wait_ge(s_df, b.k + 1)
                pool.tensor_tensor(a_hl[32:64, :], acum[32:64, :], a_hl[32:64, :].bitcast(F32), ALU.subtract).then_inc(s_al, 1)
                pool.wait_ge(s_al, b.k + 1)
                if b.first:
                    pool.wait_ge(s_w, 16 * N_W)
                if not b.early:
                    pool.wait_ge(s_sg, 8 * (b.k - 1))
                pool.tensor_tensor(neg[b.par][0:64, :, :, :], view(a_hl, 0, 64, 0, [[Q, NC], [0, 2], [1, Q]]).bitcast(F32),
                                   view(negpar, 0, 64, 0, [[0, NC], [1, 2], [0, Q]]), ALU.mult).then_inc(s_ng, 1)

            def exp_parts(b):
                pool.wait_ge(s_et, b.k + 1)
                if not b.first:
                    pool.wait_ge(s_ddp, b.k)
                    pool.wait_ge(s_ebp, b.k)
                pool.tensor_tensor(ddiag[:, :, :], view(ident, 0, 32, 0, [[0, 2], [1, NH]]), view(eT, 0, 32, 2 * Q - 1, [[Q, 2], [0, NH]]),
                                   ALU.mult).then_inc(s_dg, 1)
                pool.tensor_copy(e_hl[:, :], eT[:, :]).then_inc(s_eh, 1)
                pool.wait_ge(s_dc, b.k + 1)
                pool.wait_ge(s_eh, b.k + 1)
                pool.wait_ge(s_dg, b.k + 1)
                pool.tensor_tensor(dd[32:64, :], dd[32:64, :], adif[32:64, :], ALU.mult).then_inc(s_dd, 1)
                pool.tensor_tensor(e_hl[32:64, :], eT[32:64, :], e_hl[32:64, :].bitcast(F32), ALU.subtract).then_inc(s_el, 1)
                pool.wait_ge(s_el, b.k + 1)
                pool.wait_ge(s_dd, b.k + 1)

            def double_x(b):
                if b.first:
                    pool.wait_ge(s_lnb, 16)
                pool.wait_ge(s_xin[b.par], 32 * (b.half + 1))
                if not b.early:
                    pool.wait_ge(s_ln, 11 * (b.k - 1))
                pool.tensor_tensor(xx[:, b.par, :, :], xtok[:, b.par, :, :], xtok[:, b.par, :, :], ALU.add).then_inc(s_x2x, 1)
                pool.wait_ge(s_x2x, b.k + 1)
                pool.tensor_tensor(xx[:, b.par, :, :], xx[:, b.par, :, :], view(lnb, 0, P, 0, [[0, NT], [1, D]]), ALU.add).then_inc(s_xx, 1)

            def power_a(b):
                pool.wait_ge(s_ln, 11 * b.k + 6)
                pool.tensor_tensor(s1[:, :], w1[:, :], mhalf[:, 0:NT], ALU.pow).then_inc(s_pw, 1)

            def power_b(b):
                pool.wait_ge(s_f2, 5 * (b.k + 1))
                pool.tensor_tensor(s2[:, :], w2[:, :], mhalf[:, 0:NT], ALU.pow).then_inc(s_pw, 1)

            def keep_x1(b):
                pool.wait_ge(s_x1, 2 * (b.k + 1))
                pool.tensor_copy(x1[:, bass.ds(b.k * NT, NT), :], x1c[:, b.par, :, :]).then_inc(s_kp, 1)

            def x1_low(b):
                pool.wait_ge(s_x1f, 2 * (b.k + 1))
                pool.tensor_tensor(x1l[:, bass.ds(b.k * L, L)], x1Tf[:, :], x1h[:, bass.ds(b.k * L, L)].bitcast(F32), ALU.subtract).then_inc(s_x1l, 1)

            def once():
                pool.wait_ge(s_w2, 16 * 8)
                for m in range(2):
                    pool.tensor_scalar(wo[:, m, :], wo_f[:, m, :], nw[:, m:m + 1], None, ALU.mult)
                pool.wait_ge(s_sua, 6)
                pool.tensor_tensor(g_lo[:, :], gu_f[:, :], g_hi[:, :].bitcast(F32), ALU.subtract).then_inc(s_sup, 1)

            def pieces(b, nxt, prv):
                if nxt:
                    x_low(nxt)
                if prv:
                    power_a(prv)
                if nxt:
                    sums(nxt)
                    if b and b.first:
                        once()
                if prv:
                    power_b(prv)
                if nxt:
                    exp_parts(nxt)
                    double_x(nxt)
                if prv:
                    keep_x1(prv)
                    x1_low(prv)

            b = [Batch(k, k % 2, k // 2) for k in range(NB)]
            pieces(None, b[0], None)
            pieces(b[0], b[1], None)
            pool.wait_ge(s_sua, 7)
            pool.tensor_tensor(u_lo[:, :], gu_f[:, :], u_hi[:, :].bitcast(F32), ALU.subtract).then_inc(s_sup, 1)
            with pool.Fori(0, NB // 2 - 1) as i:
                k0, k1, k2, k3 = (Batch(2 * i + n, n % 2, i + n // 2) for n in range(4))
                pieces(k1, k2, k0)
                pieces(k2, k3, k1)
            pieces(b[7], None, b[6])
            pieces(None, None, b[7])
            with pool.Fori(0, NBLK) as n:
                pool.wait_ge(s_f2, 5 * NB + 9 * n + 9)
                pool.tensor_tensor(fs[:, :], fw[:, :], mhalf[:, :], ALU.pow).then_inc(s_fp, 1)


def constants():
    h = np.arange(NH)
    pr = np.arange(NP * Q) // Q
    sel = (h[:, None] // 2 == pr[None, :]).astype(np.float32)
    selE = (h[:, None] == np.arange(DI)[None, :] // HD).astype(np.float32)
    par = -(h[:, None] % 2 == np.arange(2)[None, :]).astype(np.float32)
    s, q = np.arange(P) % Q, np.arange(Q)
    row, col = np.arange(4 * NC)[:, None, None], np.arange(P)[None, None, :]
    rows = ((row // NC % 2 == col // Q) & (row % NC == np.arange(NC)[None, :, None])).astype(np.float32)
    return {
        "c_ident": np.eye(P, dtype=np.float32),
        "c_tril": (q[None, :] >= s[:, None]).astype(np.float32),
        "c_negpar": np.concatenate([par, par]),
        "c_reset": np.tile((np.arange(L) % Q != 0).astype(np.float32), (64, 1)),
        "c_selE": np.concatenate([selE, selE]),
        "c_sel": np.concatenate([sel, sel]),
        "c_hilo": np.array([[1, 0], [-1, 1]], np.float32),
        "c_ones4": rows,
    }


def kernel(**inputs):
    import concourse.bacc as _bacc
    from concourse import mybir as _mybir
    from concourse.bass_utils import run_bass_kernel_spmd as _run

    v = {n.replace("L0_attn_", "").replace("L0_ffn_", ""): np.asarray(x) for n, x in inputs.items()}
    arrays = {
        "x": v["x"], "xT": v["x"].transpose(0, 2, 1), "in_wT": v["in_proj_w"].T, "cwT": v["conv_w"].T, "cb": v["conv_b"][None],
        "dtb": v["dt_bias"][:, None], "alog": v["A_log"][:, None],
        "dskip": np.repeat(v["D_skip"], HD).reshape(2, P).T, "nw": v["norm_w"].reshape(2, P).T,
        "woT": v["out_proj_w"].T, "lnw": v["ln_w"][None], "lnb": v["ln_b"][None], "gwT": v["gate_w"].T,
        "egT": v["eg"].transpose(2, 0, 1).reshape(D, E * I), "euT": v["eu"].transpose(2, 0, 1).reshape(D, E * I),
        "edT": v["ed"].transpose(0, 2, 1), "sgT": v["sg"].T, "suT": v["su"].T, "sdT": v["sd"].T,
        **constants(),
    }
    nc = _bacc.Bacc("TRN2", target_bir_lowering=False, num_devices=1)
    data, aps = {}, {}
    for name, x in arrays.items():
        data[f"in_{name}"] = np.ascontiguousarray(x)
        aps[name] = nc.dram_tensor(f"in_{name}", x.shape, _mybir.dt.from_np(x.dtype), kind="ExternalInput").ap()
    out = nc.dram_tensor("out_0", (NB * L, D), _mybir.dt.float32, kind="ExternalOutput").ap()
    mamba_moe(nc, aps, out)
    r = _run(nc, [data], core_ids=[0])
    return r.results[0]["out_0"].reshape(NB, L, D)
```

```python
from contextlib import ExitStack

import numpy as np

import concourse.bass as bass
from concourse import mybir

F32 = mybir.dt.float32
F32R = mybir.dt.float32r
ALU = mybir.AluOpType
ACT = mybir.ActivationFunctionType

P = 128
NB, L, D = 8, 256, 128
NT = L // P
Q = 64
NC = L // Q
NH, HD = 32, 8
DI = NH * HD
NP = NH // 2
K = 4
DT_MIN, DT_MAX = 0.001, 0.1
EPS = 1e-5
E, I = 4, 344
NE = E + 1
HC = [(0, 128), (128, 128), (256, 88)]
BT = 512
NBLK = NB * L // BT
NR = 64 + 4 * NC
PADW = 96 * NH // 4


class Batch:

    def __init__(self, k, par, half):
        self.k, self.par, self.half = k, par, half
        self.first = isinstance(k, int) and k == 0
        self.early = isinstance(k, int) and k < 2


def mamba_moe(nc, a, out):
    with ExitStack() as ctx:
        def sb(name, shape, dt=F32):
            return ctx.enter_context(nc.sbuf_tensor(name, shape, dt))

        def sem(name):
            return ctx.enter_context(nc.semaphore(name))

        def view(t, part, nparts, off, dims):
            row = 1
            for n in t.shape[1:]:
                row *= n
            return bass.AP(t, part * row + off, [[row, nparts], *dims])

        sums_d = [nc.dram_tensor(f"sums_d{p}", [64, NC, Q], F32, kind="Internal").ap() for p in range(2)]

        bank = [ctx.enter_context(nc.psum_tensor(f"bank{i}", [P, 512], F32)) for i in range(8)]
        ps_seg = bank[0:2]
        ps_y = bank[2]
        ps_yo = bank[3]
        ps_gl = bank[4]
        ps_so = bank[5]
        ps_a, ps_b = bank[6], bank[7]

        ident = sb("ident", [P, P])
        tril = sb("tril", [P, Q])
        negpar = sb("negpar", [64, 2])
        reset = sb("reset", [64, L])
        selE = sb("selE", [64, DI], F32R)
        ones4_f = sb("ones4_f", [NR, NC, P])
        hilo = sb("hilo", [2, 2])
        ones = sb("ones", [P, 2])
        ones32 = sb("ones32", [32, P])
        cw_b = sb("cw_b", [P, K, 512])
        w_cv = sb("w_cv", [P, 320])
        w_hi = sb("w_hi", [P, 320], F32R)
        w_lo = sb("w_lo", [P, 320], F32R)
        cv_hi = sb("cv_hi", [P, K, 512], F32R)
        cv_lo = sb("cv_lo", [P, K, 512], F32R)
        cb_s = sb("cb_s", [2, 512], F32R)
        cb_r = sb("cb_r", [2, 512], F32R)
        ones_r = sb("ones_r", [2, L], F32R)
        dtal = sb("dtal", [64, 2])
        dtb_h = sb("dtb_h", [64, 1])
        aexp = sb("aexp", [64, 1])
        aneg = sb("aneg", [64, 1])
        dskip = sb("dskip", [P, 2])
        nw = sb("nw", [P, 2])
        wo = sb("wo", [P, 2, D])
        lnw = sb("lnw", [P, D])
        lnb = sb("lnb", [P, D])
        gw = sb("gw", [D, E])
        g_hi = sb("g_hi", [D, NE * I], F32R)
        g_lo = sb("g_lo", [D, NE * I], F32R)
        u_hi = sb("u_hi", [D, NE * I], F32R)
        u_lo = sb("u_lo", [D, NE * I], F32R)
        wd = sb("wd", [P, NE, len(HC), D])

        xTf = sb("xTf", [D, 2, L])
        xtok = sb("xtok", [P, 2, NT, D])
        xTh = [sb(f"xTh{p}", [D, K - 1 + L], F32R) for p in range(2)]
        xTl = [sb(f"xTl{p}", [D, K - 1 + L], F32R) for p in range(2)]
        th = sb("th", [P, 3, 512])
        tdt = sb("tdt", [64, L])
        dd = sb("dd", [64, L])
        dA = sb("dA", [64, L])
        acum = sb("acum", [64, L])
        a_hl = sb("a_hl", [64, L], F32R)
        adif = sb("adif", [64, L])
        eT = sb("eT", [64, L])
        e_hl = sb("e_hl", [64, L], F32R)
        ddiag = sb("ddiag", [32, 2, NH])
        neg = [sb(f"neg{p}", [NR, NC, 2, Q], F32R) for p in range(2)]
        mov = [sb(f"mov{p}", [NR, NP * Q], F32R) for p in range(2)]
        xs = [sb(f"xs{p}", [P, 2, L]) for p in range(2)]
        bc = [sb(f"bc{p}", [P, 2, L]) for p in range(2)]
        sz = [sb(f"sz{p}", [P, 2, L]) for p in range(2)]
        dd2 = sb("dd2", [64, NC, 2, Q])
        b2 = sb("b2", [P, NC, 2, Q])
        xs2 = sb("xs2", [P, 2, NC, 2, Q])
        ddts = [sb(f"ddt{p}", [P, NC * 64 + 64]) for p in range(2)]
        btok = sb("btok", [Q, 3, P])
        eb = [sb(f"eb{p}", [P, 2, L]) for p in range(2)]
        xpad = sb("xpad", [P, NC, PADW])
        xdd = sb("xdd", [Q, 3, DI])
        gm = sb("gm", [P, NC, Q])
        ee = sb("ee", [P, 2, 512])
        mm = sb("mm", [P, 2, 512])
        sel_f, selE_f = ee[0:64, :, :].rearrange("p a n -> p (a n)"), mm[0:64, 0, 0:DI]
        st = sb("st", [P, 3, DI])
        stm = sb("stm", [P, DI])
        yo = sb("yo", [P, 2, L])
        yv = sb("yv", [P, 2, L])
        yf = sb("yf", [P, 2, L])
        ysq = sb("ysq", [P, 2, L])
        cb_f, cb_h = (t[0:2, :, :].rearrange("r m l -> r (m l)") for t in (yo, yv))
        xx = sb("xx", [P, 2, NT, D])
        bn = sb("bn", [P, NT, 6])
        mv = sb("mv", [P, NT, 2])
        m1 = sb("m1", [P, NT])
        w1 = sb("w1", [P, NT])
        s1 = sb("s1", [P, NT])
        an = sb("an", [P, NT, D])
        rr = sb("rr", [P, NT, D])
        bn2 = sb("bn2", [P, NT, 6])
        mv2 = sb("mv2", [P, NT, 2])
        s2 = sb("s2", [P, NT])
        pause = sb("pause", [P, 1])
        w2 = sb("w2", [P, NT])
        mhalf = sb("mhalf", [P, 4])
        x1c = sb("x1c", [P, 2, NT, D])
        x1Tf = sb("x1Tf", [D, L])
        x1 = sb("x1", [P, NB * NT, D])
        x1_flat = x1[:, :, :].rearrange("p t d -> p (t d)")
        w_raw, gu_f = x1_flat[:, 0:832], x1_flat[:, 0:NE * I]
        wo_f = x1_flat[:, NE * I:NE * I + 2 * D].rearrange("p (g d) -> p g d", g=2)
        x1h = sb("x1h", [D, NB * L], F32R)
        x1l = sb("x1l", [D, NB * L], F32R)
        lg = sb("lg", [P, NB * NT, E])

        s_wi = sem("z_dt_weights_loaded")
        s_wc = sem("xbc_weights_taps_loaded")
        s_ws = sem("small_weights_loaded")
        s_w = sem("constants_loaded")
        s_w2 = sem("ffn_weights_loaded")
        s_lnb = sem("norm_bias_loaded")
        s_wo = sem("output_projection_loaded")
        s_gu = sem("gate_loaded")
        s_up = sem("up_loaded")
        s_xin = [sem(f"x_loaded{p}") for p in range(2)]
        s_su = sem("setup_vector")
        s_sua = sem("setup_scalar")
        s_sup = sem("ffn_low_parts")
        s_ps = sem("pool_setup_step")
        s_sr = sem("constant_rows")
        s_pz = sem("x_padding_zero")
        s_xh = sem("x_high")
        s_xl = sem("x_low")
        s_dtp = sem("dt_in_psum")
        s_xp = sem("xbc_z_in_psum")
        s_td = sem("dt_tanh")
        s_th = sem("silu_tanh")
        s_dt = sem("dt_chain")
        s_sl = sem("silu_done")
        s_ah = sem("sums_high")
        s_al = sem("sums_low")
        s_ng = sem("neg_sums")
        s_df = sem("decay_exponent")
        s_et = sem("exp_sums")
        s_dc = sem("exp_decay")
        s_eh = sem("exp_high")
        s_el = sem("exp_low")
        s_dd = sem("dt_decayed")
        s_dg = sem("decay_diagonal")
        s_fl = [sem(f"sums_flat{p}") for p in range(2)]
        s_d2 = sem("dt_doubled")
        s_b2 = sem("b_doubled")
        s_x2 = sem("x_doubled")
        s_fw = sem("sums_in_dram")
        s_ddp = sem("dt_tokens_psum")
        s_btp = sem("b_tokens_psum")
        s_ebp = sem("exp_rows_psum")
        s_xtp = sem("x_tokens_psum")
        s_ddt = sem("dt_tokens")
        s_bt = sem("b_tokens")
        s_eb = sem("exp_rows")
        s_pad = sem("x_padded")
        s_xd = sem("x_decayed")
        s_g = sem("g_in_psum")
        s_gm = sem("g_masked")
        s_sg = sem("seg_in_psum")
        s_e = sem("decays")
        s_m = sem("m_ready")
        s_yd = sem("yd_done")
        s_st = sem("state_in_psum")
        s_s = sem("state_ready")
        s_sm = sem("state_decayed")
        s_yo = sem("yo_in_psum")
        s_y = sem("y_steps")
        s_sq = sem("y_squared")
        s_op = sem("proj_in_psum")
        s_x2x = sem("x_doubled_sum")
        s_xx = sem("residual_ready")
        s_ln = sem("norm_steps")
        s_pw = sem("rsqrt_done")
        s_x1 = sem("x1_ready")
        s_kp = sem("x1_kept")
        s_x1p = sem("x1t_in_psum")
        s_x1f = sem("x1t_copied")
        s_x1l = sem("x1t_low")
        s_lp = sem("logits_in_psum")
        s_lg = sem("logits_kept")
        s_gp = sem("gate_in_psum")
        s_uo = sem("up_in_psum")
        s_si = sem("gate_silu")
        s_h = sem("hidden_ready")
        s_dn = sem("hidden_used")
        s_cb = sem("comb_steps")
        s_ac = sem("acc_steps")
        s_f2 = sem("final_stats")
        s_fp = sem("final_rsqrt")
        s_fo = sem("final_ready")
        s_out = sem("stored")
        sg, hh = cw_b, th
        fbn = sb("fbn", [P, 4, 6])
        fmv = sb("fmv", [P, 4, 2])
        fs = sb("fs", [P, 4])
        fw = sb("fw", [P, 4])
        acc, fo = yv[:, :, :].rearrange("p a (t d) -> p (a t) d", d=D), yf[:, :, :].rearrange("p a (t d) -> p (a t) d", d=D)
        NTT = NB * NT
        cmx = sb("cmx", [P, NTT])
        cex = sb("cex", [P, NTT, E])
        csm = sb("csm", [P, NTT])
        crc = sb("crc", [P, NTT])
        cpr = sb("cpr", [P, NTT, E])
        cge = sb("cge", [P, NTT, E, E])
        crk = sb("crk", [P, NTT, E])
        csl = sb("csl", [P, NTT, E])
        cts = sb("cts", [P, NTT])
        comb = sb("comb", [P, NTT, E])

        block = ctx.enter_context(nc.Block())

        N_W = 9
        N_PS = 3

        @block.sync
        def _(sp):
            def load_x(b):
                at, once = (x if isinstance(x, int) else sp.snap(x) for x in (b.k * (D * L), b.k - 1))
                if not b.early:
                    sp.wait_ge(s_xh, once)
                    sp.wait_ge(s_xl, once)
                    sp.wait_ge(s_x2x, once)
                sp.dma_start(xTf[:, b.par, :], bass.AP(a["xT"].tensor, at, [[L, D], [1, L]])).then_inc(s_xin[b.par], 16)
                sp.dma_start(xtok[:, b.par, :, :], bass.AP(a["x"].tensor, at, [[D, P], [P * D, NT], [1, D]])).then_inc(s_xin[b.par], 16)

            def flatten(b):
                made, sent = (x if isinstance(x, int) else sp.snap(x) for x in (b.k + 1, 16 * (b.k + 1)))
                sp.wait_ge(s_ah, made)
                sp.wait_ge(s_al, made)
                if not b.early:
                    sp.wait_ge(s_g, b.k)
                sp.dma_start(sums_d[b.par].rearrange("h c q -> h (c q)"), a_hl[:, :].bitcast(F32)).then_inc(s_fw, 16)
                sp.wait_ge(s_fw, sent)
                for part in range(2):
                    for h2 in range(2):
                        row = 64 + NC * (2 * part + h2)
                        dst = mov[b.par][row:row + NC, :].bitcast(F32).rearrange("c (h q) -> c h q", q=Q)
                        src = sums_d[b.par][32 * part:32 * part + 32].rearrange("(h g) c q -> g c h q", g=2)[h2]
                        sp.dma_start(dst, src).then_inc(s_fl[b.par], 16)

            sp.dma_start(w_raw[:, 0:320], a["in_wT"][:, 0:320]).then_inc(s_wi, 16)
            load_x(Batch(0, 0, 0))
            sp.dma_start(dtal[:, :], a["dtal"]).then_inc(s_ws, 16)
            sp.dma_start(cb_f, a["cb"].broadcast_to([2, 512])).then_inc(s_ws, 16)
            sp.dma_start(hilo[:, :], a["c_hilo"]).then_inc(s_ws, 16)
            for dst, name in ((negpar, "c_negpar"), (reset, "c_reset"), (ident, "c_ident"), (tril, "c_tril"),
                              (sel_f, "c_sel"), (selE_f, "c_selE"), (nw, "nw"), (dskip, "dskip")):
                sp.dma_start(dst[:, :], a[name]).then_inc(s_w, 16)
            sp.dma_start(ones4_f[64:NR, :, :], a["c_ones4"]).then_inc(s_w, 16)
            load_x(Batch(1, 1, 0))
            sp.dma_start(wo_f[:, :, :], a["woT"].rearrange("(g p) d -> p g d", p=P)).then_inc(s_wo, 16)
            sp.dma_start(lnw[:, :], a["lnw"].broadcast_to([P, D])).then_inc(s_w2, 16)
            sp.dma_start(lnb[:, :], a["lnb"].broadcast_to([P, D])).then_inc(s_lnb, 16)
            sp.dma_start(gw[:, :], a["gwT"]).then_inc(s_w2, 16)
            flatten(Batch(0, 0, 0))
            sp.wait_ge(s_su, 8)
            sp.dma_start(gu_f[:, 0:E * I], a["egT"]).then_inc(s_gu, 16)
            sp.dma_start(gu_f[:, E * I:], a["sgT"]).then_inc(s_gu, 16)
            for c, (h0, hn) in enumerate(HC):
                sp.dma_start(wd[0:hn, 0:E, c, :], a["edT"][:, h0:h0 + hn, :].rearrange("e i d -> i e d")).then_inc(s_w2, 16)
                sp.dma_start(wd[0:hn, E, c, :], a["sdT"][h0:h0 + hn, :]).then_inc(s_out if c == len(HC) - 1 else s_w2, 16)
            flatten(Batch(1, 1, 0))
            sp.wait_ge(s_sua, 6)
            sp.wait_ge(s_sup, 1)
            sp.dma_start(gu_f[:, 0:E * I], a["euT"]).then_inc(s_up, 16)
            sp.dma_start(gu_f[:, E * I:], a["suT"]).then_inc(s_up, 16)

            def body(b, nxt, nxt2, prv):
                if nxt2:
                    load_x(nxt2)
                if nxt and not nxt.early:
                    flatten(nxt)

            body(Batch(0, 0, 0), Batch(1, 1, 0), Batch(2, 0, 1), None)
            with sp.Fori(0, 2) as i:
                body(Batch(2 * i + 1, 1, i), Batch(2 * i + 2, 0, i + 1), Batch(2 * i + 3, 1, i + 1), Batch(2 * i, 0, i))
                body(Batch(2 * i + 2, 0, i + 1), Batch(2 * i + 3, 1, i + 1), Batch(2 * i + 4, 0, i + 2), Batch(2 * i + 1, 1, i))
            body(Batch(5, 1, 2), Batch(6, 0, 3), Batch(7, 1, 3), Batch(4, 0, 2))
            body(Batch(6, 0, 3), Batch(7, 1, 3), None, Batch(5, 1, 2))
            with sp.Fori(0, NBLK) as n:
                sp.wait_ge(s_fo, 4 * n + 5)
                sp.dma_start(out[bass.ds(n * BT, BT), :].rearrange("(t p) d -> p t d", p=P), fo[:, :, :]).then_inc(s_out, 16)
            sp.wait_ge(s_out, 16 * (NBLK + 1))

        b7 = Batch(NB - 1, (NB - 1) % 2, (NB - 1) // 2)

        def y_last(eng, b):
            eng.wait_ge(s_y, 5 * b.k + 3)
            eng.tensor_tensor(yv[:, :, Q:], yv[:, :, Q:], yo[:, :, Q:], ALU.add).then_inc(s_y, 1)
            eng.wait_ge(s_y, 5 * b.k + 4)
            if not b.first:
                eng.wait_ge(s_op, b.k)
                eng.wait_ge(s_sq, b.k)
            eng.tensor_tensor(yf[:, :, :], yv[:, :, :], sz[b.par][:, :, :], ALU.mult).then_inc(s_y, 1)

        def schedule(pieces, eng):
            b = [Batch(k, k % 2, k // 2) for k in range(NB)]
            pieces(None, b[0], None, b[1])
            pieces(b[0], b[1], None, b[2])
            with eng.Fori(0, NB // 2 - 2) as i:
                k0, k1, k2, k3, k4 = (Batch(2 * i + n, n % 2, i + n // 2) for n in range(5))
                pieces(k1, k2, k0, k3)
                pieces(k2, k3, k1, k4)
            pieces(b[5], b[6], b[4], b[7])
            pieces(b[6], b[7], b[5], None)
            pieces(b7, None, b[6], None)

        NS = NE * len(HC)
        ps_g, ps_u, ps_e = (bank[6], bank[0], bank[2]), (bank[7], bank[1], bank[3]), (bank[4], bank[5])

        @block.tensor
        def _(pe):
            def mm3(dst, hi, lo, rhi, rlo, first, last):
                pe.matmul(dst, hi, rhi, start=first, stop=False)
                pe.matmul(dst, hi, rlo, start=False, stop=False)
                return pe.matmul(dst, lo, rhi, start=False, stop=last)

            def dt_proj(b):
                pe.wait_ge(s_xh, b.k + 1)
                pe.wait_ge(s_xl, b.k + 1)
                if b.first:
                    pe.wait_ge(s_su, 2)
                    pe.wait_ge(s_sua, 2)
                else:
                    pe.wait_ge(s_pad, 4 * b.k)
                    pe.wait_ge(s_xd, 2 * b.k)
                h, l = xTh[b.par][:, K - 1:], xTl[b.par][:, K - 1:]
                mm3(ps_a[0:64, 0:L], w_hi[:, 256:320], w_lo[:, 256:320], h, l, True, True).then_inc(s_dtp, 1)

            def conv(b, dst, ch):
                m = ch % 2
                o = dst[:, m * L:(m + 1) * L]
                for t in range(K):
                    c = slice(ch * P, ch * P + P)
                    mm3(o, cv_hi[:, t, c], cv_lo[:, t, c], xTh[b.par][:, t:t + L], xTl[b.par][:, t:t + L], t == 0, False)
                return pe.matmul(o, cb_r[:, ch * P:ch * P + P], ones_r[:, :], start=False, stop=True)

            def x_proj(b, m):
                if m == 0:
                    pe.wait_ge(s_xh, b.k + 1)
                    pe.wait_ge(s_xl, b.k + 1)
                    if b.first:
                        pe.wait_ge(s_su, 7)
                        pe.wait_ge(s_sua, 4)
                        pe.wait_ge(s_ps, N_PS)
                    else:
                        pe.wait_ge(s_pad, 4 * b.k - 2)
                        pe.wait_ge(s_xd, 2 * b.k - 1)
                ins = conv(b, ps_b, m)
                if m == 1:
                    ins.then_inc(s_xp, 1)

            def bc_proj(b, m):
                if m == 0:
                    if b.first:
                        pe.wait_ge(s_su, 9)
                        pe.wait_ge(s_sua, 5)
                    pe.wait_ge(s_td, b.k + 1)
                ins = conv(b, ps_a, 2 + m)
                if m == 1:
                    ins.then_inc(s_xp, 1)

            def z_proj(b):
                pe.wait_ge(s_sl, 3 * b.k + 1)
                h, l = xTh[b.par][:, K - 1:], xTl[b.par][:, K - 1:]
                for m in range(2):
                    c = slice(m * P, m * P + P)
                    ins = mm3(ps_b[:, m * L:(m + 1) * L], w_hi[:, c], w_lo[:, c], h, l, True, True)
                ins.then_inc(s_xp, 1)

            def turn_dt(b):
                pe.wait_ge(s_sl, 3 * b.k + 2)
                pe.wait_ge(s_d2, b.k + 1)
                pe.wait_ge(s_dg, b.k + 1)
                if b.first:
                    pe.wait_ge(s_w, 16 * N_W)
                pe.matmul(ps_a[:, 0:64], dd2[:, 0, :, :].rearrange("h a q -> h (a q)"), ident[0:64, 0:64], start=True, stop=True)
                for c in range(1, NC):
                    pe.transpose(ps_a[:, c * 64:c * 64 + 64], dd2[:, c, :, :].rearrange("h a q -> h (a q)"), ident[0:64, 0:64])
                pe.matmul(ps_a[:, 256:320], ones32[:, :], ddiag[:, :, :], start=True, stop=True).then_inc(s_ddp, 1)

            def turn_b(b):
                pe.wait_ge(s_sl, 3 * b.k + 3)
                pe.matmul(ps_b[0:Q, 0:P], bc[b.par][:, 0, 0:Q], ident[:, :], start=True, stop=True)
                for c in range(1, 3):
                    ins = pe.transpose(ps_b[0:Q, c * P:c * P + P], bc[b.par][:, 0, c * Q:c * Q + Q], ident[:, :])
                ins.then_inc(s_btp, 1)

            def spread_exp(b):
                pe.wait_ge(s_ddt, b.k + 1)
                pe.wait_ge(s_eh, b.k + 1)
                pe.wait_ge(s_el, b.k + 1)
                if b.first:
                    pe.wait_ge(s_sr, 5)
                for m in range(2):
                    ins = pe.matmul(ps_a[:, m * L:(m + 1) * L], selE[:, m * P:(m + 1) * P], e_hl[:, :], start=True, stop=True)
                ins.then_inc(s_ebp, 1)

            def turn_x(b, g):
                dst = ps_a if g else ps_b
                if g == 0:
                    pe.wait_ge(s_bt, b.k + 1)
                    pe.wait_ge(s_x2, 2 * (b.k + 1))
                else:
                    pe.wait_ge(s_eb, b.k + 1)
                for c in range(2 * g, 2 * g + 2):
                    for m in range(2):
                        ins = pe.transpose(dst[:, (c % 2) * DI + m * P:(c % 2) * DI + (m + 1) * P],
                                           xs2[:, m, c, :, :].rearrange("h a q -> h (a q)"), ident[:, :])
                ins.then_inc(s_xtp, 1)

            def g_of(b):
                pe.wait_ge(s_b2, b.k + 1)
                if not b.first:
                    pe.wait_ge(s_gm, b.k)
                for c in range(NC):
                    ins = pe.matmul(ps_gl[:, c * Q:c * Q + Q], b2[:, c, :, :].rearrange("h a q -> h (a q)"),
                                    bc[b.par][:, 1, c * Q:c * Q + Q], start=True, stop=True)
                ins.then_inc(s_g, 1)

            def seg(b, n):
                if n == 0:
                    pe.wait_ge(s_fl[b.par], 64 * (b.half + 1))
                    pe.wait_ge(s_ng, b.k + 1)
                if not (b.first and n < 2):
                    pe.wait_ge(s_e, 8 * b.k + n - 1)
                c, hf = n // 2, n % 2
                pe.matmul(ps_seg[hf][:, :], neg[b.par][:, c, :, :], mov[b.par][:, hf * 512:hf * 512 + 512],
                          start=True, stop=True).then_inc(s_sg, 1)

            def y_in(b, n):
                if n == 0:
                    pe.wait_ge(s_pad, 4 * (b.k + 1))
                    if not b.first:
                        pe.wait_ge(s_y, 5 * b.k - 3)
                pe.wait_ge(s_m, 8 * b.k + n + 1)
                c, hf = n // 2, n % 2
                for i in range(2):
                    for j in range(4):
                        ins = pe.matmul(ps_y[32 * j:32 * j + 32, hf * L + c * Q:hf * L + c * Q + Q],
                                        xpad[:, c, (hf * 4 + j) * 96 + i * 32:(hf * 4 + j) * 96 + i * 32 + 32],
                                        mm[:, n % 2, (2 * j + i) * Q:(2 * j + i) * Q + Q], start=(i == 0), stop=(i == 1))
                ins.then_inc(s_yd, 1)

            def state(b, c):
                if c == 0:
                    pe.wait_ge(s_xd, 2 * (b.k + 1))
                    pe.wait_ge(s_bt, b.k + 1)
                    if not b.first:
                        pe.wait_ge(s_ln, 11 * b.k - 3)
                else:
                    pe.wait_ge(s_s, 3 * b.k + c)
                pe.matmul(ps_so[:, 0:DI], btok[:, c, :], xdd[:, c, :], start=True, stop=True).then_inc(s_st, 1)

            def y_out(b):
                for c in range(1, NC):
                    pe.wait_ge(s_s, 3 * b.k + c)
                    for m in range(2):
                        ins = pe.matmul(ps_yo[:, m * L + c * Q:m * L + c * Q + Q], st[:, c - 1, m * P:(m + 1) * P],
                                        bc[b.par][:, 1, c * Q:c * Q + Q], start=True, stop=True)
                ins.then_inc(s_yo, 1)

            def project(b):
                pe.wait_ge(s_sq, b.k + 1)
                pe.wait_ge(s_y, 5 * (b.k + 1))
                pe.wait_ge(s_s, 3 * (b.k + 1))
                pe.wait_ge(s_lg, b.k + 1)
                for t in range(NT):
                    for m in range(2):
                        pe.matmul(ps_so[:, t * D:(t + 1) * D], yf[:, m, t * P:(t + 1) * P], wo[:, m, :], start=(m == 0), stop=(m == 1))
                for t in range(NT):
                    for m in range(2):
                        ins = pe.matmul(ps_so[:, 256 + t:257 + t], ysq[:, m, t * P:(t + 1) * P], ones[:, 0:1], start=(m == 0), stop=(m == 1))
                ins.then_inc(s_op, 1)

            def turn_x1(b):
                pe.wait_ge(s_x1, 2 * (b.k + 1))
                if b is not b7:
                    pe.wait_ge(s_s, 3 * (b.k + 2))
                for t in range(NT):
                    ins = pe.transpose(ps_so[:, t * P:(t + 1) * P], x1c[:, b.par, t, :], ident[:, :])
                ins.then_inc(s_x1p, 1)

            def logits(b):
                pe.wait_ge(s_x1f, 2 * (b.k + 1))
                for t in range(NT):
                    ins = pe.matmul(ps_so[:, 256 + t * E:256 + (t + 1) * E], x1Tf[:, t * P:(t + 1) * P], gw[:, :], start=True, stop=True)
                ins.then_inc(s_lp, 1)

            steps = [(e, c) for e in ([E] + list(range(E))) for c in range(len(HC))]

            def up(n, s):
                e, c = steps[s]
                h0, hn = HC[c]
                w = slice(e * I + h0, e * I + h0 + hn)
                xh, xl = x1h[:, bass.ds(n * BT, BT)], x1l[:, bass.ds(n * BT, BT)]
                g, u = ps_g[s % 3], ps_u[s % 3]
                if s >= 3 or not isinstance(n, int):
                    pe.wait_ge(s_h, n * NS + s - 2)
                mm3(g[0:hn, :], g_hi[:, w], g_lo[:, w], xh, xl, True, True).then_inc(s_gp, 1)
                mm3(u[0:hn, :], u_hi[:, w], u_lo[:, w], xh, xl, True, True).then_inc(s_uo, 1)

            def down(n, s):
                e, c = steps[s]
                hn = HC[c][1]
                o = s // len(HC)
                pe.wait_ge(s_h, n * NS + s + 1)
                if c == 0:
                    pe.wait_ge(s_ac, n * 17 + 1 + (1 + 4 * (o - 2) if o >= 2 else 0))
                    if o == 1:
                        pe.wait_ge(s_lg, NB + 1)
                for t in range(4):
                    ins = pe.matmul(ps_e[o % 2][:, t * D:(t + 1) * D], hh[0:hn, s % 3, t * P:(t + 1) * P], wd[0:hn, e, c, :],
                                    start=(c == 0 and t == 0), stop=(c == len(HC) - 1), skip_group_check=True)
                ins.then_inc(s_dn, 1)

            def pieces(b, nxt, prv, nxt2):
                if b is b7:
                    pe.wait_ge(s_sua, 7)
                    pe.wait_ge(s_sup, 3)
                    pe.wait_ge(s_x1l, 2)
                    pe.wait_ge(s_pad, 4 * NB)
                    pe.wait_ge(s_xd, 2 * NB)
                    up(0, 0)
                if nxt:
                    dt_proj(nxt)
                    x_proj(nxt, 0)
                if b:
                    y_in(b, 0)
                    seg(b, 2)
                if nxt:
                    x_proj(nxt, 1)
                if b:
                    y_in(b, 1)
                    seg(b, 3)
                if prv:
                    project(prv)
                if b:
                    y_in(b, 2)
                    seg(b, 4)
                if nxt:
                    bc_proj(nxt, 0)
                if b:
                    y_in(b, 3)
                    seg(b, 5)
                if nxt:
                    bc_proj(nxt, 1)
                if b:
                    y_in(b, 4)
                    seg(b, 6)
                    state(b, 0)
                if nxt:
                    z_proj(nxt)
                if b:
                    y_in(b, 5)
                    seg(b, 7)
                    state(b, 1)
                if nxt:
                    turn_dt(nxt)
                if b:
                    y_in(b, 6)
                    state(b, 2)
                if nxt:
                    turn_b(nxt)
                    spread_exp(nxt)
                if b:
                    y_in(b, 7)
                    if b.first:
                        pe.wait_ge(s_w2, 16 * 7)
                if nxt:
                    turn_x(nxt, 0)
                if b:
                    y_out(b)
                if nxt:
                    turn_x(nxt, 1)
                if prv:
                    turn_x1(prv)
                if b is b7:
                    up(0, 1)
                if nxt:
                    g_of(nxt)
                    seg(nxt, 0)
                    seg(nxt, 1)
                if prv:
                    logits(prv)
                if b is b7:
                    down(0, 0)

            pe.wait_ge(s_su, 1)
            schedule(pieces, pe)

            def ffn(n, more):
                first = isinstance(n, int) and n == 0
                for s in range(NS):
                    if not (first and s == 0):
                        down(n, s)
                    if s + 3 < NS:
                        up(n, s + 3)
                    elif more:
                        if s + 3 == NS:
                            pe.wait_ge(s_x1l, NB)
                        up(n + 1, s + 3 - NS)
                    if first and s == 1:
                        turn_x1(b7)
                    if first and s == 2:
                        logits(b7)

            project(b7)
            up(0, 2)
            ffn(0, True)
            with pe.Fori(1, NBLK - 1) as n:
                ffn(n, True)
            ffn(NBLK - 1, False)

        @block.scalar
        def _(act):
            act.dma_start(w_raw[:, 320:832], a["in_wT"][:, 320:832]).then_inc(s_wc, 16)
            for m in range(2):
                act.dma_start(cw_b[:, :, 256 * m:256 * m + 256],
                              a["cwT"][:, 256 * m:256 * m + 256].rearrange("(o k) c -> o k c", o=1).broadcast_to([P, K, 256])).then_inc(s_wc, 16)
            act.wait_ge(s_su, 1)
            act.activation(w_hi[:, :], w_cv[:, :], ACT.Copy).then_inc(s_sua, 1)

            def setup_small():
                act.wait_ge(s_ws, 16 * 3)
                act.activation(aexp[:, :], dtal[:, 1:2], ACT.Exp).then_inc(s_sua, 1)
                act.activation(cb_s[:, :], cb_f, ACT.Copy, scale=0.5).then_inc(s_sua, 1)

            def setup_conv(m):
                act.wait_ge(s_su, (3, 8)[m])
                act.activation(cv_hi[:, :, m * 256:m * 256 + 256], cw_b[:, :, m * 256:m * 256 + 256], ACT.Copy).then_inc(s_sua, 1)

            def setup_rows(p):
                act.wait_ge(s_w, 16 * N_W)
                act.activation(neg[p][64:NR, :, :, :].rearrange("r c h q -> r (c h q)"), ones4_f[64:NR, :, :].rearrange("r c n -> r (c n)"),
                               ACT.Copy).then_inc(s_sr, 1)
                act.activation(mov[p][0:64, :], sel_f, ACT.Copy).then_inc(s_sr, 1)
                if p == 0:
                    act.activation(selE[:, :], selE_f, ACT.Copy).then_inc(s_sr, 1)

            def x_high(b):
                act.wait_ge(s_xin[b.par], 32 * (b.half + 1))
                if not b.early:
                    act.wait_ge(s_xp, 3 * (b.k - 1))
                act.activation(xTh[b.par][:, K - 1:], xTf[:, b.par, :], ACT.Copy).then_inc(s_xh, 1)

            def dt_tanh(b):
                act.wait_ge(s_dtp, b.k + 1)
                if b.first:
                    act.wait_ge(s_su, 4)
                else:
                    act.wait_ge(s_dt, 3 * b.k - 2)
                act.activation(tdt[:, :], ps_a[0:64, 0:L], ACT.Tanh, bias=dtb_h[:, 0:1], scale=0.5).then_inc(s_td, 1)

            def silu_tanh(b, n, src):
                act.wait_ge(s_xp, 3 * b.k + n + 1)
                if not b.first:
                    act.wait_ge(s_sl, 3 * (b.k - 1) + n + 1)
                act.activation(th[:, n, :], src[:, :], ACT.Tanh).then_inc(s_th, 1)

            def sums_high(b):
                act.wait_ge(s_dt, 3 * (b.k + 1))
                if not b.first:
                    act.wait_ge(s_fw, 16 * b.k)
                    act.wait_ge(s_ng, b.k)
                act.activation(a_hl[:, :], acum[:, :], ACT.Copy).then_inc(s_ah, 1)

            def exps(b):
                act.wait_ge(s_dt, 3 * (b.k + 1))
                if not b.first:
                    act.wait_ge(s_el, b.k)
                    act.wait_ge(s_dg, b.k)
                act.activation(eT[:, :], acum[:, :], ACT.Exp).then_inc(s_et, 1)
                act.wait_ge(s_df, b.k + 1)
                if not b.first:
                    act.wait_ge(s_dd, b.k)
                act.activation(adif[:, :], adif[:, :], ACT.Exp).then_inc(s_dc, 1)
                act.wait_ge(s_et, b.k + 1)
                if not b.first:
                    act.wait_ge(s_ebp, b.k)
                act.activation(e_hl[:, :], eT[:, :], ACT.Copy).then_inc(s_eh, 1)

            def double(b, part):
                if part == "x":
                    act.wait_ge(s_sl, 3 * b.k + 1)
                    if not b.first:
                        act.wait_ge(s_xtp, 2 * b.k)
                    for m in range(2):
                        act.activation(xs2[:, m, :, :, :], view(xs[b.par], 0, P, m * L, [[Q, NC], [0, 2], [1, Q]]), ACT.Copy).then_inc(s_x2, 1)
                elif part == "b":
                    act.wait_ge(s_sl, 3 * b.k + 2)
                    if not b.first:
                        act.wait_ge(s_g, b.k)
                    act.activation(b2[:, :, :, :], view(bc[b.par], 0, P, 0, [[Q, NC], [0, 2], [1, Q]]), ACT.Copy).then_inc(s_b2, 1)
                else:
                    act.wait_ge(s_dd, b.k + 1)
                    if not b.first:
                        act.wait_ge(s_ddp, b.k)
                    act.activation(dd2[:, :, :, :], view(dd, 0, 64, 0, [[Q, NC], [0, 2], [1, Q]]), ACT.Copy).then_inc(s_d2, 1)

            def copy_dt(b):
                act.wait_ge(s_ddp, b.k + 1)
                act.activation(ddts[b.par][:, :], ps_a[:, 0:320], ACT.Copy).then_inc(s_ddt, 1)

            def copy_b(b):
                act.wait_ge(s_btp, b.k + 1)
                if not b.first:
                    act.wait_ge(s_st, 3 * b.k)
                act.activation(btok[:, :, :], ps_b[0:Q, 0:384], ACT.Copy).then_inc(s_bt, 1)

            def copy_exp(b):
                act.wait_ge(s_ebp, b.k + 1)
                if not b.early:
                    act.wait_ge(s_y, 5 * (b.k - 1))
                act.activation(eb[b.par][:, :, :], ps_a[:, :], ACT.Copy).then_inc(s_eb, 1)

            def decays(b, n):
                act.wait_ge(s_sg, 8 * b.k + n + 1)
                if not (b.first and n < 2):
                    act.wait_ge(s_m, 8 * b.k + n - 1)
                act.activation(ee[:, n % 2, :], ps_seg[n % 2][:, :], ACT.Exp).then_inc(s_e, 1)

            def y_square(b):
                act.wait_ge(s_y, 5 * (b.k + 1))
                act.activation(ysq[:, :, :], yf[:, :, :], ACT.Square).then_inc(s_sq, 1)

            def x1_turned(b):
                act.wait_ge(s_x1p, b.k + 1)
                act.activation(x1[:, bass.ds(b.k * NT, NT), :], x1c[:, b.par, :, :], ACT.Copy).then_inc(s_kp, 1)
                act.activation(x1Tf[:, :], ps_so[:, 0:L], ACT.Copy).then_inc(s_x1f, 1)
                act.activation(x1h[:, bass.ds(b.k * L, L)], ps_so[:, 0:L], ACT.Copy).then_inc(s_x1f, 1)

            def keep_logits(b):
                act.wait_ge(s_lp, b.k + 1)
                act.activation(lg[:, bass.ds(b.k * NT, NT), :], ps_so[:, 256:256 + NT * E], ACT.Copy).then_inc(s_lg, 1)

            def once(high, loaded):
                act.wait_ge(loaded, 32)
                act.activation(high[:, :], gu_f[:, :], ACT.Copy).then_inc(s_sua, 1)

            def silu_gate(n, s):
                hn = HC[s % 3][1]
                act.wait_ge(s_gp, n * NS + s + 1)
                if s >= 3 or not isinstance(n, int):
                    act.wait_ge(s_h, n * NS + s - 2)
                act.activation(sg[0:hn, s % 3, :], ps_g[s % 3][0:hn, :], ACT.Silu).then_inc(s_si, 1)

            def first_pieces(nxt, nxt2):
                x_high(nxt)
                setup_small()
                setup_conv(0)
                dt_tanh(nxt)
                sums_high(nxt)
                exps(nxt)
                setup_conv(1)
                setup_rows(0)
                double(nxt, "dt")
                silu_tanh(nxt, 0, ps_b)
                setup_rows(1)
                silu_tanh(nxt, 1, ps_a)
                silu_tanh(nxt, 2, ps_b)
                double(nxt, "x")
                copy_dt(nxt)
                copy_b(nxt)
                copy_exp(nxt)
                x_high(nxt2)
                double(nxt, "b")
                decays(nxt, 0)
                decays(nxt, 1)

            def pieces(b, nxt, prv, nxt2):
                if not b:
                    first_pieces(nxt, nxt2)
                    return
                if b:
                    if b.first:
                        once(g_hi, s_gu)
                if nxt:
                    dt_tanh(nxt)
                if b:
                    decays(b, 2)
                if nxt:
                    sums_high(nxt)
                if prv:
                    y_square(prv)
                if nxt:
                    silu_tanh(nxt, 0, ps_b)
                if b:
                    decays(b, 3)
                if nxt:
                    exps(nxt)
                if b:
                    decays(b, 4)
                if nxt:
                    double(nxt, "x")
                if b:
                    decays(b, 5)
                if nxt:
                    double(nxt, "dt")
                    silu_tanh(nxt, 1, ps_a)
                if b:
                    decays(b, 6)
                if nxt:
                    silu_tanh(nxt, 2, ps_b)
                if b:
                    decays(b, 7)
                if b is b7:
                    silu_gate(0, 0)
                if nxt:
                    copy_dt(nxt)
                    copy_b(nxt)
                    copy_exp(nxt)
                if nxt2:
                    x_high(nxt2)
                if nxt:
                    double(nxt, "b")
                if b and b.first:
                    once(u_hi, s_up)
                if prv:
                    x1_turned(prv)
                if nxt:
                    decays(nxt, 0)
                    decays(nxt, 1)
                if b is b7:
                    y_square(b)
                if prv:
                    keep_logits(prv)

            schedule(pieces, act)

            def ffn(n, more):
                for s in range(3, NS + 3 if more else NS):
                    silu_gate(n + s // NS, s % NS)
                    if isinstance(n, int) and n == 0:
                        if s == 4:
                            x1_turned(b7)
                        if s == 5:
                            keep_logits(b7)
                        if s == 6:
                            gate_exp()

            silu_gate(0, 1)
            silu_gate(0, 2)

            def gate_exp():
                act.wait_ge(s_cb, 2)
                act.activation(cex[:, :, :], cpr[:, :, :], ACT.Exp).then_inc(s_sua, 1)

            ffn(0, True)
            with act.Fori(1, NBLK - 1) as n:
                ffn(n, True)
            ffn(NBLK - 1, False)

        @block.vector
        def _(dve):
            dve.wait_ge(s_wi, 16)
            dve.tensor_scalar(w_cv[:, 256:320], w_raw[:, 256:320], 1.0, None, ALU.mult)
            dve.tensor_scalar(w_cv[:, 0:256], w_raw[:, 0:256], 0.5, None, ALU.mult).then_inc(s_su, 1)
            dve.wait_ge(s_sua, 1)
            dve.tensor_tensor(w_lo[:, :], w_cv[:, :], w_hi[:, :].bitcast(F32), ALU.subtract).then_inc(s_su, 1)
            dve.wait_ge(s_wc, 16 * 3)

            def taps(m):
                dve.scalar_tensor_tensor(out=cw_b[:, :, m * 256:m * 256 + 256], in0=cw_b[:, :, m * 256:m * 256 + 256], scalar=0.5,
                                         in1=view(x1, 0, P, 320 + m * 256, [[0, K], [1, 256]]), op0=ALU.mult, op1=ALU.mult).then_inc(s_su, 1)

            def taps_low(m):
                dve.wait_ge(s_sua, 4 + m)
                dve.tensor_tensor(cv_lo[:, :, m * 256:m * 256 + 256], cw_b[:, :, m * 256:m * 256 + 256],
                                  cv_hi[:, :, m * 256:m * 256 + 256].bitcast(F32), ALU.subtract).then_inc(s_su, 1)

            taps(0)
            dve.wait_ge(s_ws, 16 * 3)
            dve.wait_ge(s_sua, 3)
            dve.tensor_scalar(dtb_h[:, :], dtal[:, 0:1], 0.5, None, ALU.mult)
            dve.tensor_scalar(aneg[:, :], aexp[:, :], -1.0, None, ALU.mult).then_inc(s_su, 1)
            dve.tensor_scalar(cb_h, cb_f, hilo[:, 1:2], 0.5, ALU.mult, ALU.mult).then_inc(s_su, 1)
            dve.wait_ge(s_su, 5)
            dve.scalar_tensor_tensor(out=cb_r[:, :], in0=cb_s[:, :].bitcast(F32), scalar=hilo[:, 0:1], in1=cb_h, op0=ALU.mult, op1=ALU.add).then_inc(s_su, 1)
            taps_low(0)

            def dt_chain(b):
                dve.wait_ge(s_td, b.k + 1)
                if not b.first:
                    dve.wait_ge(s_ddp, b.k)
                dve.tensor_scalar(dd[:, :], tdt[:, :], (DT_MAX - DT_MIN) / 2, (DT_MAX + DT_MIN) / 2, ALU.mult, ALU.add).then_inc(s_dt, 1)
                dve.wait_ge(s_dt, 3 * b.k + 1)
                dve.tensor_scalar(dA[:, :], dd[:, :], aneg[:, 0:1], None, ALU.mult).then_inc(s_dt, 1)
                dve.wait_ge(s_dt, 3 * b.k + 2)
                if not b.first:
                    dve.wait_ge(s_al, b.k)
                    dve.wait_ge(s_df, b.k)
                    dve.wait_ge(s_et, b.k)
                if b.first:
                    dve.wait_ge(s_w, 16 * N_W)
                dve.tensor_tensor_scan(acum[:, :], reset[:, :], dA[:, :], 0.0, ALU.mult, ALU.add).then_inc(s_dt, 1)

            def silu(b, n, src, dst):
                dve.wait_ge(s_th, 3 * b.k + n + 1)
                if not b.early:
                    if n == 0:
                        dve.wait_ge(s_xtp, 2 * (b.k - 1))
                    if n == 1:
                        dve.wait_ge(s_yo, b.k - 1)
                        dve.wait_ge(s_btp, b.k - 1)
                    dve.wait_ge(s_y, 5 * (b.k - 1))
                dve.scalar_tensor_tensor(out=dst[b.par][:, :, :].rearrange("p a l -> p (a l)"), in0=th[:, n, :], scalar=1.0,
                                         in1=src[:, :], op0=ALU.add, op1=ALU.mult).then_inc(s_sl, 1)

            def pad_x(b, g):
                src = ps_b if g == 0 else ps_a
                dve.wait_ge(s_xtp, 2 * b.k + g + 1)
                if g == 0:
                    dve.wait_ge(s_ddt, b.k + 1)
                    if b.first:
                        dve.wait_ge(s_pz, 1)
                    else:
                        dve.wait_ge(s_yd, 8 * b.k)
                        dve.wait_ge(s_st, 3 * b.k)
                for h2 in range(2):
                    dve.tensor_tensor(view(xpad, 64 * h2, 64, 2 * g * PADW + 8 * h2, [[PADW, 2], [48, NP], [1, HD]]),
                                      view(src, 64 * h2, 64, 8 * h2, [[DI, 2], [16, NP], [1, HD]]),
                                      view(ddts[b.par], 64 * h2, 64, 2 * g * 64 + h2, [[64, 2], [2, NP], [0, HD]]),
                                      ALU.mult).then_inc(s_pad, 1)
                n = 2 if g == 0 else 1
                dve.tensor_tensor(view(xdd, 0, 64, 2 * g * DI, [[DI, n], [HD, NH], [1, HD]]),
                                  view(src, 0, 64, 0, [[DI, n], [HD, NH], [1, HD]]),
                                  view(ddts[b.par], 0, 64, 2 * g * 64 + 32, [[64, n], [1, NH], [0, HD]]),
                                  ALU.mult).then_inc(s_xd, 1)

            def g_mask(b):
                dve.wait_ge(s_g, b.k + 1)
                if not b.first:
                    dve.wait_ge(s_m, 8 * b.k)
                dve.tensor_tensor(gm[:, :, :], view(ps_gl, 0, P, 0, [[Q, NC], [1, Q]]), view(tril, 0, P, 0, [[0, NC], [1, Q]]),
                                  ALU.mult).then_inc(s_gm, 1)

            def m_of(b, n):
                if n == 0:
                    dve.wait_ge(s_gm, b.k + 1)
                dve.wait_ge(s_e, 8 * b.k + n + 1)
                if not (b.first and n < 2):
                    dve.wait_ge(s_yd, 8 * b.k + n - 1)
                c = n // 2
                dve.scalar_tensor_tensor(out=view(mm, 0, P, (n % 2) * 512, [[Q, 8], [1, Q]]), in0=view(ee, 0, P, (n % 2) * 512, [[Q, 8], [1, Q]]),
                                         scalar=1.0, in1=view(gm, 0, P, c * Q, [[0, 8], [1, Q]]), op0=ALU.min, op1=ALU.mult).then_inc(s_m, 1)

            def state(b, c):
                if c == 0:
                    dve.wait_ge(s_st, 3 * b.k + 1)
                    if not b.first:
                        dve.wait_ge(s_yo, b.k)
                    dve.tensor_copy(st[:, 0, :], ps_so[:, 0:DI]).then_inc(s_s, 1)
                    return
                dve.wait_ge(s_s, 3 * b.k + c)
                dve.tensor_tensor(view(stm, 0, P, 0, [[HD, NH], [1, HD]]), view(st, 0, P, (c - 1) * DI, [[HD, NH], [1, HD]]),
                                  view(ddts[b.par], 0, P, 256 + (c - 1) * 32, [[1, NH], [0, HD]]), ALU.mult).then_inc(s_sm, 1)
                dve.wait_ge(s_sm, 2 * b.k + c)
                dve.wait_ge(s_st, 3 * b.k + c + 1)
                dve.tensor_tensor(st[:, c, :], stm[:, :], ps_so[:, 0:DI], ALU.add).then_inc(s_s, 1)

            def y_a(b):
                dve.wait_ge(s_yd, 8 * (b.k + 1))
                if not b.first:
                    dve.wait_ge(s_y, 5 * b.k)
                for m in range(2):
                    dve.scalar_tensor_tensor(out=yv[:, m, :], in0=xs[b.par][:, m, :], scalar=dskip[:, m:m + 1], in1=ps_y[:, m * L:(m + 1) * L],
                                             op0=ALU.mult, op1=ALU.add).then_inc(s_y, 1)

            def y_b(b):
                dve.wait_ge(s_yo, b.k + 1)
                dve.wait_ge(s_eb, b.k + 1)
                dve.tensor_tensor(yo[:, :, Q:], view(ps_yo, 0, P, Q, [[L, 2], [1, L - Q]]), eb[b.par][:, :, Q:], ALU.mult).then_inc(s_y, 1)

            def norm_a(b):
                dve.wait_ge(s_op, b.k + 1)
                for t in range(NT):
                    dve.bn_stats(bn[:, t, :], ps_so[:, t * D:(t + 1) * D]).then_inc(s_ln, 1)
                dve.wait_ge(s_ln, 11 * b.k + 2)
                dve.tensor_scalar(m1[:, :], ps_so[:, 256:256 + NT], EPS / DI, EPS * EPS, ALU.mult, ALU.add).then_inc(s_ln, 1)
                for t in range(NT):
                    dve.bn_aggr(mv[:, t, :], bn[:, t, :]).then_inc(s_ln, 1)
                dve.wait_ge(s_ln, 11 * b.k + 5)
                dve.tensor_tensor(w1[:, :], mv[:, :, 1], m1[:, :], ALU.add).then_inc(s_ln, 1)

            def norm_b(b):
                for t in range(NT):
                    dve.scalar_tensor_tensor(out=an[:, t, :], in0=ps_so[:, t * D:(t + 1) * D], scalar=mv[:, t, 0:1], in1=lnw[:, :],
                                             op0=ALU.subtract, op1=ALU.mult).then_inc(s_ln, 1)
                dve.wait_ge(s_ln, 11 * b.k + 8)
                dve.wait_ge(s_pw, 2 * b.k + 1)
                dve.wait_ge(s_xx, b.k + 1)
                for t in range(NT):
                    dve.scalar_tensor_tensor(out=rr[:, t, :], in0=an[:, t, :], scalar=s1[:, t:t + 1], in1=xx[:, b.par, t, :],
                                             op0=ALU.mult, op1=ALU.add).then_inc(s_ln, 1)

            def norm_c(b):
                dve.wait_ge(s_ln, 11 * b.k + 10)
                for t in range(NT):
                    dve.bn_stats(bn2[:, t, :], rr[:, t, :]).then_inc(s_f2, 1)
                dve.wait_ge(s_f2, 5 * b.k + 2)
                dve.memset(pause[:, :], 0.0)
                for t in range(NT):
                    dve.bn_aggr(mv2[:, t, :], bn2[:, t, :]).then_inc(s_f2, 1)
                dve.wait_ge(s_f2, 5 * b.k + 4)
                dve.tensor_scalar(w2[:, :], mv2[:, :, 1], EPS, None, ALU.add).then_inc(s_f2, 1)

            def norm_d(b):
                dve.wait_ge(s_pw, 2 * b.k + 2)
                for t in range(NT):
                    dve.tensor_scalar(x1c[:, b.par, t, :], rr[:, t, :], mv2[:, t, 0:1], s2[:, t:t + 1], ALU.subtract, ALU.mult).then_inc(s_x1, 1)
                dve.memset(m1[:, 0:1], 0.0).then_inc(s_ln, 1)

            def hidden(n, s):
                hn = HC[s % 3][1]
                dve.wait_ge(s_si, n * NS + s + 1)
                dve.wait_ge(s_uo, n * NS + s + 1)
                if s >= 3 or not isinstance(n, int):
                    dve.wait_ge(s_dn, n * NS + s - 2)
                dve.tensor_tensor(hh[0:hn, s % 3, :], sg[0:hn, s % 3, :], ps_u[s % 3][0:hn, :], ALU.mult).then_inc(s_h, 1)

            def gate_low():
                dve.wait_ge(s_w2, 16 * 7)
                dve.wait_ge(s_sua, 6)
                dve.tensor_tensor(g_lo[:, :], gu_f[:, :], g_hi[:, :].bitcast(F32), ALU.subtract).then_inc(s_sup, 1)

            def pieces(b, nxt, prv, nxt2):
                if nxt:
                    dt_chain(nxt)
                    if nxt.first:
                        taps(1)
                        taps_low(1)
                if b:
                    m_of(b, 2)
                if nxt:
                    silu(nxt, 0, ps_b, xs)
                if b:
                    m_of(b, 3)
                if prv:
                    norm_a(prv)
                if b:
                    m_of(b, 4)
                if prv:
                    norm_b(prv)
                if b and b.first:
                    gate_low()
                if b:
                    m_of(b, 5)
                if prv:
                    norm_c(prv)
                if nxt:
                    silu(nxt, 1, ps_a, bc)
                if b:
                    state(b, 0)
                    m_of(b, 6)
                    state(b, 1)
                if nxt:
                    silu(nxt, 2, ps_b, sz)
                if b:
                    m_of(b, 7)
                    state(b, 2)
                    y_a(b)
                if prv:
                    norm_d(prv)
                if b is b7:
                    hidden(0, 0)
                if nxt:
                    pad_x(nxt, 0)
                    pad_x(nxt, 1)
                if b:
                    y_b(b)
                if nxt:
                    g_mask(nxt)
                    m_of(nxt, 0)
                    m_of(nxt, 1)

            schedule(pieces, dve)

            steps = 0

            def did(ins):
                nonlocal steps
                steps += 1
                ins.then_inc(s_cb, 1)
                dve.wait_ge(s_cb, steps)

            def over_e(t):
                return view(t, 0, P, 0, [[1, NTT], [0, E]])

            def gate_max():
                dve.wait_ge(s_lg, NB + 1)
                did(dve.tensor_reduce(cmx[:, :], lg[:, :, :], mybir.AxisListType.X, ALU.max))
                did(dve.tensor_tensor(cpr[:, :, :], lg[:, :, :], over_e(cmx), ALU.subtract))

            def gate_weights():
                dve.wait_ge(s_sua, 8)
                did(dve.tensor_reduce(csm[:, :], cex[:, :, :], mybir.AxisListType.X, ALU.add))
                did(dve.reciprocal(crc[:, :], csm[:, :]))
                did(dve.tensor_tensor(cpr[:, :, :], cex[:, :, :], over_e(crc), ALU.mult))
                for e in range(E):
                    for f0, f1, op in ((0, e, ALU.is_ge), (e, E, ALU.is_gt)):
                        if f1 > f0:
                            ins = dve.tensor_tensor(cge[:, :, e, f0:f1], cpr[:, :, f0:f1], view(cpr, 0, P, e, [[E, NTT], [0, f1 - f0]]), op)
                did(ins)
                did(dve.tensor_reduce(crk[:, :, :], cge[:, :, :, :], mybir.AxisListType.X, ALU.add))
                did(dve.scalar_tensor_tensor(out=csl[:, :, :], in0=crk[:, :, :], scalar=1.5, in1=cpr[:, :, :], op0=ALU.is_lt, op1=ALU.mult))
                did(dve.tensor_reduce(cts[:, :], csl[:, :, :], mybir.AxisListType.X, ALU.add))
                did(dve.tensor_scalar(csm[:, :], cts[:, :], 1e-20, None, ALU.add))
                did(dve.reciprocal(crc[:, :], csm[:, :]))
                did(dve.tensor_tensor(comb[:, :, :], csl[:, :, :], over_e(crc), ALU.mult))

            def add_expert(n, o):
                dve.wait_ge(s_dn, n * NS + 3 * o + 3)
                ps = ps_e[o % 2]
                if o == 0:
                    dve.wait_ge(s_fo, 4 * n + 1)
                    dve.wait_ge(s_kp, 2 * n + 2)
                    dve.tensor_tensor(yv[:, :, :].rearrange("p a l -> p (a l)"), ps[:, :],
                                      x1[:, bass.ds(n * 4, 4), :].rearrange("p t d -> p (t d)"), ALU.add).then_inc(s_ac, 1)
                    return
                dve.wait_ge(s_ac, 17 * n + 2 + 4 * (o - 1))
                for t in range(4):
                    dve.scalar_tensor_tensor(out=acc[:, t, :], in0=ps[:, t * D:(t + 1) * D], scalar=comb[:, bass.ds(n * 4 + t, 1), o - 1],
                                             in1=acc[:, t, :], op0=ALU.mult, op1=ALU.add).then_inc(s_ac, 1)

            def final_norm(n):
                dve.wait_ge(s_ac, 17 * n + 18)
                for t in range(4):
                    dve.bn_stats(fbn[:, t, :], acc[:, t, :]).then_inc(s_f2, 1)
                dve.wait_ge(s_f2, 5 * NB + 9 * n + 4)
                dve.memset(pause[:, :], 0.0)
                for t in range(4):
                    dve.bn_aggr(fmv[:, t, :], fbn[:, t, :]).then_inc(s_f2, 1)
                dve.wait_ge(s_f2, 5 * NB + 9 * n + 8)
                dve.tensor_scalar(fw[:, :], fmv[:, :, 1], EPS, None, ALU.add).then_inc(s_f2, 1)
                dve.wait_ge(s_fp, n + 1)
                dve.wait_ge(s_out, 16 * (n + 1))
                for t in range(4):
                    dve.tensor_scalar(fo[:, t, :], acc[:, t, :], fmv[:, t, 0:1], fs[:, t:t + 1], ALU.subtract, ALU.mult).then_inc(s_fo, 1)

            def ffn(n, more):
                for s in range(NS):
                    if s % 3 == 2:
                        add_expert(n, s // 3)
                    if s + 3 < NS:
                        hidden(n, s + 3)
                    elif more:
                        hidden(n + 1, s + 3 - NS)
                    if isinstance(n, int) and n == 0:
                        if s == 2:
                            gate_max()
                        if s == 3:
                            gate_weights()
                final_norm(n)

            y_last(dve, b7)
            dve.memset(cts[:, 0:1], 0.0).then_inc(s_ac, 1)
            dve.memset(cts[:, 1:2], 0.0).then_inc(s_fo, 1)
            hidden(0, 1)
            norm_a(b7)
            norm_b(b7)
            hidden(0, 2)
            norm_c(b7)
            norm_d(b7)
            ffn(0, True)
            with dve.Fori(1, NBLK - 1) as n:
                ffn(n, True)
            ffn(NBLK - 1, False)

        @block.gpsimd
        def _(pool):
            steps = 0

            def step(ins):
                nonlocal steps
                steps += 1
                ins.then_inc(s_ps, 1)
                pool.wait_ge(s_ps, steps)

            for p in range(2):
                pool.memset(xTh[p][:, 0:K - 1].bitcast(F32), 0.0)
                pool.memset(xTl[p][:, 0:K - 1].bitcast(F32), 0.0)
            pool.memset(ones[:, :], 1.0)
            pool.memset(mhalf[:, :], -0.5).then_inc(s_lg, 1)
            step(pool.memset(pause[:, :], 0.0))
            step(pool.memset(ones_r[:, :].bitcast(F32), 1.0))
            step(pool.memset(ones32[:, :], 1.0))
            pool.memset(xpad[:, :, :], 0.0).then_inc(s_pz, 1)

            def x_low(b):
                pool.wait_ge(s_xh, b.k + 1)
                if not b.early:
                    pool.wait_ge(s_xp, 3 * (b.k - 1))
                pool.tensor_tensor(xTl[b.par][:, K - 1:], xTf[:, b.par, :], xTh[b.par][:, K - 1:].bitcast(F32), ALU.subtract).then_inc(s_xl, 1)

            def sums(b):
                pool.wait_ge(s_dt, 3 * (b.k + 1))
                pool.tensor_tensor(view(adif, 0, 64, 0, [[Q, NC], [1, Q]]), view(acum, 0, 64, Q - 1, [[Q, NC], [0, Q]]),
                                   view(acum, 0, 64, 0, [[Q, NC], [1, Q]]), ALU.subtract).then_inc(s_df, 1)
                pool.wait_ge(s_ah, b.k + 1)
                pool.wait_ge(s_df, b.k + 1)
                pool.tensor_tensor(a_hl[32:64, :], acum[32:64, :], a_hl[32:64, :].bitcast(F32), ALU.subtract).then_inc(s_al, 1)
                pool.wait_ge(s_al, b.k + 1)
                if b.first:
                    pool.wait_ge(s_w, 16 * N_W)
                if not b.early:
                    pool.wait_ge(s_sg, 8 * (b.k - 1))
                pool.tensor_tensor(neg[b.par][0:64, :, :, :], view(a_hl, 0, 64, 0, [[Q, NC], [0, 2], [1, Q]]).bitcast(F32),
                                   view(negpar, 0, 64, 0, [[0, NC], [1, 2], [0, Q]]), ALU.mult).then_inc(s_ng, 1)

            def exp_parts(b):
                pool.wait_ge(s_et, b.k + 1)
                if not b.first:
                    pool.wait_ge(s_ddp, b.k)
                    pool.wait_ge(s_ebp, b.k)
                pool.tensor_tensor(ddiag[:, :, :], view(ident, 0, 32, 0, [[0, 2], [1, NH]]), view(eT, 0, 32, 2 * Q - 1, [[Q, 2], [0, NH]]),
                                   ALU.mult).then_inc(s_dg, 1)
                pool.wait_ge(s_dc, b.k + 1)
                pool.wait_ge(s_eh, b.k + 1)
                pool.wait_ge(s_dg, b.k + 1)
                pool.tensor_tensor(dd[32:64, :], dd[32:64, :], adif[32:64, :], ALU.mult).then_inc(s_dd, 1)
                pool.tensor_tensor(e_hl[32:64, :], eT[32:64, :], e_hl[32:64, :].bitcast(F32), ALU.subtract).then_inc(s_el, 1)
                pool.wait_ge(s_el, b.k + 1)
                pool.wait_ge(s_dd, b.k + 1)

            def double_x(b):
                if b.first:
                    pool.wait_ge(s_lnb, 16)
                pool.wait_ge(s_xin[b.par], 32 * (b.half + 1))
                if not b.early:
                    pool.wait_ge(s_ln, 11 * (b.k - 1))
                pool.tensor_tensor(xx[:, b.par, :, :], xtok[:, b.par, :, :], xtok[:, b.par, :, :], ALU.add).then_inc(s_x2x, 1)
                pool.wait_ge(s_x2x, b.k + 1)
                pool.tensor_tensor(xx[:, b.par, :, :], xx[:, b.par, :, :], view(lnb, 0, P, 0, [[0, NT], [1, D]]), ALU.add).then_inc(s_xx, 1)

            def power_a(b):
                pool.wait_ge(s_ln, 11 * b.k + 6)
                pool.tensor_tensor(s1[:, :], w1[:, :], mhalf[:, 0:NT], ALU.pow).then_inc(s_pw, 1)

            def power_b(b):
                pool.wait_ge(s_f2, 5 * (b.k + 1))
                pool.tensor_tensor(s2[:, :], w2[:, :], mhalf[:, 0:NT], ALU.pow).then_inc(s_pw, 1)

            def x1_low(b):
                pool.wait_ge(s_x1f, 2 * (b.k + 1))
                pool.tensor_tensor(x1l[:, bass.ds(b.k * L, L)], x1Tf[:, :], x1h[:, bass.ds(b.k * L, L)].bitcast(F32), ALU.subtract).then_inc(s_x1l, 1)

            def up_low(part):
                pool.wait_ge(s_sua, 7)
                pool.tensor_tensor(u_lo[:, part], gu_f[:, part], u_hi[:, part].bitcast(F32), ALU.subtract).then_inc(s_sup, 1)

            def output_weights():
                pool.wait_ge(s_wo, 16)
                for m in range(2):
                    pool.tensor_scalar(wo[:, m, :], wo_f[:, m, :], nw[:, m:m + 1], None, ALU.mult)

            def pieces(b, nxt, prv, nxt2):
                if nxt:
                    if nxt.first:
                        x_low(nxt)
                    sums(nxt)
                if prv:
                    power_a(prv)
                if nxt:
                    exp_parts(nxt)
                if prv:
                    power_b(prv)
                if nxt:
                    double_x(nxt)
                    if nxt.first:
                        output_weights()
                if nxt2:
                    x_low(nxt2)
                if b and b.first:
                    up_low(slice(0, NE * I // 2))
                if b and b is not b7:
                    y_last(pool, b)
                if prv:
                    x1_low(prv)
                if b and b.first:
                    up_low(slice(NE * I // 2, NE * I))

            schedule(pieces, pool)
            pieces(None, None, b7, None)
            with pool.Fori(0, NBLK) as n:
                pool.wait_ge(s_f2, 5 * NB + 9 * n + 9)
                pool.tensor_tensor(fs[:, :], fw[:, :], mhalf[:, :], ALU.pow).then_inc(s_fp, 1)


def constants():
    h = np.arange(NH)
    pr = np.arange(NP * Q) // Q
    sel = (h[:, None] // 2 == pr[None, :]).astype(np.float32)
    selE = (h[:, None] == np.arange(DI)[None, :] // HD).astype(np.float32)
    par = -(h[:, None] % 2 == np.arange(2)[None, :]).astype(np.float32)
    s, q = np.arange(P) % Q, np.arange(Q)
    row, col = np.arange(4 * NC)[:, None, None], np.arange(P)[None, None, :]
    rows = ((row // NC % 2 == col // Q) & (row % NC == np.arange(NC)[None, :, None])).astype(np.float32)
    return {
        "c_ident": np.eye(P, dtype=np.float32),
        "c_tril": (q[None, :] >= s[:, None]).astype(np.float32),
        "c_negpar": np.concatenate([par, par]),
        "c_reset": np.tile((np.arange(L) % Q != 0).astype(np.float32), (64, 1)),
        "c_selE": np.concatenate([selE, selE]),
        "c_sel": np.concatenate([sel, sel]),
        "c_hilo": np.array([[1, 0], [-1, 1]], np.float32),
        "c_ones4": rows,
    }


def kernel(**inputs):
    import concourse.bacc as _bacc
    from concourse import mybir as _mybir
    from concourse.bass_utils import run_bass_kernel_spmd as _run

    v = {n.replace("L0_attn_", "").replace("L0_ffn_", ""): np.asarray(x) for n, x in inputs.items()}
    w = v["in_proj_w"]
    arrays = {
        "x": v["x"], "xT": v["x"].transpose(0, 2, 1), "in_wT": np.concatenate([w[:256], w[768:], w[768:], w[256:768]]).T, "cwT": v["conv_w"].T, "cb": v["conv_b"][None],
        "dtal": np.tile(np.stack([v["dt_bias"], v["A_log"]], 1), (2, 1)),
        "dskip": np.repeat(v["D_skip"], HD).reshape(2, P).T, "nw": v["norm_w"].reshape(2, P).T,
        "woT": v["out_proj_w"].T, "lnw": v["ln_w"][None], "lnb": v["ln_b"][None], "gwT": v["gate_w"].T,
        "egT": v["eg"].transpose(2, 0, 1).reshape(D, E * I), "euT": v["eu"].transpose(2, 0, 1).reshape(D, E * I),
        "edT": v["ed"].transpose(0, 2, 1), "sgT": v["sg"].T, "suT": v["su"].T, "sdT": v["sd"].T,
        **constants(),
    }
    nc = _bacc.Bacc("TRN2", target_bir_lowering=False, num_devices=1)
    data, aps = {}, {}
    for name, x in arrays.items():
        data[f"in_{name}"] = np.ascontiguousarray(x)
        aps[name] = nc.dram_tensor(f"in_{name}", x.shape, _mybir.dt.from_np(x.dtype), kind="ExternalInput").ap()
    out = nc.dram_tensor("out_0", (NB * L, D), _mybir.dt.float32, kind="ExternalOutput").ap()
    mamba_moe(nc, aps, out)
    r = _run(nc, [data], core_ids=[0])
    return r.results[0]["out_0"].reshape(NB, L, D)
```
